# Optimizing a Trainium2 kernel written in Bass

```python
import numpy as np
import jax
import jax.numpy as jnp

def _softmax(x, axis=-1):
    return jax.nn.softmax(x, axis=axis)

def _gelu(x):
    return jax.nn.gelu(x, approximate=True)

def _silu(x):
    return jax.nn.silu(x)

def _sigmoid(x):
    return jax.nn.sigmoid(x)

def _layernorm(x, axis=-1, eps=1e-05):
    m = jnp.mean(x, axis=axis, keepdims=True)
    v = jnp.var(x, axis=axis, keepdims=True)
    return (x - m) / jnp.sqrt(v + eps)

def _scatter_add(tgt, idx, src, axis=0):
    return tgt.at[idx].add(src)

def _segment_sum(src, seg, n):
    return jax.ops.segment_sum(src, seg, n)
kernel_name = 'mk_adaln_d1_jaxref_r8_ec1303'

def setup_inputs(seed: int=0):
    np.random.seed(seed)
    _w = jnp.asarray

    def _L0_attn_setup():
        import jax, jax.numpy as jnp
        import numpy as np
        import math
        N_HEAD = 8

        def _rope(x):
            D = x.shape[-1]
            S = x.shape[-2]
            inv_freq = 1.0 / 10000.0 ** (jnp.arange(0, D, 2, dtype=jnp.float32) / D)
            t = jnp.arange(S, dtype=jnp.float32)
            freqs = jnp.repeat(t[:, None] * inv_freq[None, :], 2, axis=-1)
            cos = jnp.cos(freqs).astype(x.dtype)
            sin = jnp.sin(freqs).astype(x.dtype)
            xp = x.reshape(*x.shape[:-1], D // 2, 2)
            rot = jnp.stack((-xp[..., 1], xp[..., 0]), axis=-1).reshape(x.shape)
            return x * cos + rot * sin

        def _row_linear(x, Wo):
            B, S, P = x.shape
            E = Wo.shape[0]
            x = jnp.swapaxes(x, 1, 2).reshape(B, S, P)
            x = jnp.einsum('bsp,ep->bse', x, Wo)
            x = x.reshape(B, E, -1)
            return jnp.swapaxes(x, 1, 2)
        key = jax.random.key(seed)
        k0, k1, k2, k3, k4 = jax.random.split(key, 5)
        B, S, E, P = (4, 256, 128, 128)
        std = 1.0 / math.sqrt(E)
        return {'emb': jax.random.normal(k0, (B, S, E), dtype=jnp.float32), 'W1': jax.random.normal(k1, (P, E), dtype=jnp.float32) * std, 'W2': jax.random.normal(k2, (P, E), dtype=jnp.float32) * std, 'W3': jax.random.normal(k3, (P, E), dtype=jnp.float32) * std, 'Wo': jax.random.normal(k4, (E, P), dtype=jnp.float32) * std}
    _L0_attn_in = _L0_attn_setup()

    def _L0_ffn_setup():
        import jax, jax.numpy as jnp
        import numpy as np
        DIM = 128
        DEPTH = 6
        HEADS = 16
        DIM_HEAD = 64
        WINDOW = 32
        INNER = HEADS * DIM_HEAD
        DIM_INNER = int(DIM * 4 * 2 / 3)
        QK_SCALE = 8.0

        def shift_tokens(t):
            a, s = jnp.split(t, 2, -1)
            s = jnp.pad(s, ((0, 0), (1, 0), (0, 0)))[:, :-1]
            return jnp.concatenate([a, s], -1)

        def l2norm(t):
            return t / jnp.maximum(jnp.linalg.norm(t, axis=-1, keepdims=True), 1e-12)

        def rotate_half(x):
            x1, x2 = jnp.split(x, 2, -1)
            return jnp.concatenate([-x2, x1], -1)

        def rotary_tables(n):
            half = jnp.arange(0, DIM_HEAD, 2, dtype=jnp.float32)
            inv_freq = 1.0 / 10000.0 ** (half / DIM_HEAD)
            t = jnp.arange(n, dtype=jnp.float32)
            freqs = t[:, None] * inv_freq[None, :]
            freqs = jnp.concatenate([freqs, freqs], -1)
            base_scale = (half + 0.4 * DIM_HEAD) / (1.4 * DIM_HEAD)
            power = (t - n // 2) / (WINDOW // 2)
            scale = base_scale[None, :] ** power[:, None]
            scale = jnp.concatenate([scale, scale], -1)
            return (freqs, scale)

        def local_attention(q, k, v):
            b, h, n, d = q.shape
            w = WINDOW
            nw = n // w
            bq = q.reshape(b, h, nw, w, d)
            bk = k.reshape(b, h, nw, w, d)
            bv = v.reshape(b, h, nw, w, d)

            def look(t):
                p = jnp.pad(t, ((0, 0), (0, 0), (1, 0), (0, 0), (0, 0)))
                return jnp.concatenate([p[:, :, :nw], p[:, :, 1:]], axis=3)
            bk2, bv2 = (look(bk), look(bv))
            seq = jnp.arange(n).reshape(nw, w)
            seq_p = jnp.pad(seq, ((1, 0), (0, 0)), constant_values=-1)
            jt = jnp.concatenate([seq_p[:nw], seq_p[1:]], axis=1)
            it = seq[:, :, None]
            jb = jt[:, None, :]
            mask = (it < jb) | (it > jb + w) | (jb == -1)
            sim = jnp.einsum('bhwie,bhwje->bhwij', bq, bk2) * QK_SCALE
            sim = jnp.where(mask, -jnp.finfo(sim.dtype).max, sim)
            attn = jax.nn.softmax(sim, -1)
            out = jnp.einsum('bhwij,bhwje->bhwie', attn, bv2)
            return out.reshape(b, h, n, d)

        def attn_layer(x, Wqkv, qs, ksc, Wo):
            b, n, _ = x.shape
            qkv = x @ Wqkv
            q, k, v = jnp.split(qkv, 3, -1)
            sh = lambda t: t.reshape(b, n, HEADS, DIM_HEAD).transpose(0, 2, 1, 3)
            q, k, v = (sh(q), sh(k), sh(v))
            q = l2norm(q) * qs
            k = l2norm(k) * ksc
            freqs, scale = rotary_tables(n)
            cos, sin = (jnp.cos(freqs), jnp.sin(freqs))
            q = q * cos * scale + rotate_half(q) * sin * scale
            inv = 1.0 / scale
            k = k * cos * inv + rotate_half(k) * sin * inv
            out = local_attention(q, k, v)
            out = out.transpose(0, 2, 1, 3).reshape(b, n, INNER)
            return out @ Wo

        def ffn_layer(x, g, bln, W1, b1, W2, b2):
            mu = x.mean(-1, keepdims=True)
            var = ((x - mu) ** 2).mean(-1, keepdims=True)
            xn = (x - mu) / jnp.sqrt(var + 1e-05) * g + bln
            hg = xn @ W1 + b1
            a, gate = jnp.split(hg, 2, -1)
            return a * jax.nn.gelu(gate, approximate=False) @ W2 + b2
        key = jax.random.key(seed)
        ks = jax.random.split(key, 8)
        B, N = (2, 256)
        init = lambda k, shape: jax.random.normal(k, shape, jnp.float32) * 0.02
        return {'x': jax.random.normal(ks[0], (B, N, DIM), jnp.float32), 'Wqkv': init(ks[1], (DEPTH, DIM, 3 * INNER)), 'q_scale': jnp.ones((DEPTH, DIM_HEAD), jnp.float32), 'k_scale': jnp.ones((DEPTH, DIM_HEAD), jnp.float32), 'Wo': init(ks[2], (DEPTH, INNER, DIM)), 'ln_g': jnp.ones((DEPTH, DIM), jnp.float32), 'ln_b': jnp.zeros((DEPTH, DIM), jnp.float32), 'W1': init(ks[3], (DEPTH, DIM, 2 * DIM_INNER)), 'b1': jnp.zeros((DEPTH, 2 * DIM_INNER), jnp.float32), 'W2': init(ks[4], (DEPTH, DIM_INNER, DIM)), 'b2': jnp.zeros((DEPTH, DIM), jnp.float32)}
    _L0_ffn_in = _L0_ffn_setup()
    _L0_c = _w((lambda *s: np.random.randn(*s).astype(np.float32) * 0.05)(8, 128))
    _L0_wmod = _w((lambda *s: np.random.randn(*s).astype(np.float32) * 0.05)(128, 6 * 128) * 128 ** (-0.5))
    _d = {'L0_attn_emb': _L0_attn_in['emb'], 'L0_attn_W1': _L0_attn_in['W1'], 'L0_attn_W2': _L0_attn_in['W2'], 'L0_attn_W3': _L0_attn_in['W3'], 'L0_attn_Wo': _L0_attn_in['Wo'], 'L0_ffn_Wqkv': _L0_ffn_in['Wqkv'], 'L0_ffn_q_scale': _L0_ffn_in['q_scale'], 'L0_ffn_k_scale': _L0_ffn_in['k_scale'], 'L0_ffn_Wo': _L0_ffn_in['Wo'], 'L0_ffn_ln_g': _L0_ffn_in['ln_g'], 'L0_ffn_ln_b': _L0_ffn_in['ln_b'], 'L0_ffn_W1': _L0_ffn_in['W1'], 'L0_ffn_b1': _L0_ffn_in['b1'], 'L0_ffn_W2': _L0_ffn_in['W2'], 'L0_ffn_b2': _L0_ffn_in['b2'], 'L0_c': _L0_c, 'L0_wmod': _L0_wmod}
    _x0 = _d['L0_attn_emb']
    _d['L0_attn_emb'] = jax.random.normal(jax.random.fold_in(jax.random.key(seed), 1), (8, 256, 128), dtype=_x0.dtype)
    del _x0
    return _d

def reference(L0_attn_emb, L0_attn_W1, L0_attn_W2, L0_attn_W3, L0_attn_Wo, L0_ffn_Wqkv, L0_ffn_q_scale, L0_ffn_k_scale, L0_ffn_Wo, L0_ffn_ln_g, L0_ffn_ln_b, L0_ffn_W1, L0_ffn_b1, L0_ffn_W2, L0_ffn_b2, L0_c, L0_wmod):

    def _L0_attn_ref(emb, W1, W2, W3, Wo):
        import jax, jax.numpy as jnp
        import numpy as np
        import math
        N_HEAD = 8

        def _rope(x):
            D = x.shape[-1]
            S = x.shape[-2]
            inv_freq = 1.0 / 10000.0 ** (jnp.arange(0, D, 2, dtype=jnp.float32) / D)
            t = jnp.arange(S, dtype=jnp.float32)
            freqs = jnp.repeat(t[:, None] * inv_freq[None, :], 2, axis=-1)
            cos = jnp.cos(freqs).astype(x.dtype)
            sin = jnp.sin(freqs).astype(x.dtype)
            xp = x.reshape(*x.shape[:-1], D // 2, 2)
            rot = jnp.stack((-xp[..., 1], xp[..., 0]), axis=-1).reshape(x.shape)
            return x * cos + rot * sin

        def _row_linear(x, Wo):
            B, S, P = x.shape
            E = Wo.shape[0]
            x = jnp.swapaxes(x, 1, 2).reshape(B, S, P)
            x = jnp.einsum('bsp,ep->bse', x, Wo)
            x = x.reshape(B, E, -1)
            return jnp.swapaxes(x, 1, 2)
        B, S, E = emb.shape
        P = W1.shape[0]
        H = N_HEAD
        D = P // H
        q = jnp.einsum('bse,pe->bsp', emb, W1).reshape(B, H, S, D)
        k = jnp.einsum('bse,pe->bsp', emb, W2).reshape(B, H, S, D)
        v = jnp.einsum('bse,pe->bsp', emb, W3).reshape(B, H, S, D)
        q = _rope(q)
        k = _rope(k)
        scores = jnp.einsum('bhqd,bhkd->bhqk', q, k).astype(jnp.float32) / math.sqrt(H)
        attn = jax.nn.softmax(scores, axis=-1).astype(v.dtype)
        out = jnp.einsum('bhqk,bhkd->bhqd', attn, v)
        out = jnp.swapaxes(out, 1, 2).reshape(B, S, P)
        return _row_linear(out, Wo)

    def _L0_ffn_ref(x, Wqkv, q_scale, k_scale, Wo, ln_g, ln_b, W1, b1, W2, b2):
        import jax, jax.numpy as jnp
        import numpy as np
        DIM = 128
        DEPTH = 6
        HEADS = 16
        DIM_HEAD = 64
        WINDOW = 32
        INNER = HEADS * DIM_HEAD
        DIM_INNER = int(DIM * 4 * 2 / 3)
        QK_SCALE = 8.0

        def shift_tokens(t):
            a, s = jnp.split(t, 2, -1)
            s = jnp.pad(s, ((0, 0), (1, 0), (0, 0)))[:, :-1]
            return jnp.concatenate([a, s], -1)

        def l2norm(t):
            return t / jnp.maximum(jnp.linalg.norm(t, axis=-1, keepdims=True), 1e-12)

        def rotate_half(x):
            x1, x2 = jnp.split(x, 2, -1)
            return jnp.concatenate([-x2, x1], -1)

        def rotary_tables(n):
            half = jnp.arange(0, DIM_HEAD, 2, dtype=jnp.float32)
            inv_freq = 1.0 / 10000.0 ** (half / DIM_HEAD)
            t = jnp.arange(n, dtype=jnp.float32)
            freqs = t[:, None] * inv_freq[None, :]
            freqs = jnp.concatenate([freqs, freqs], -1)
            base_scale = (half + 0.4 * DIM_HEAD) / (1.4 * DIM_HEAD)
            power = (t - n // 2) / (WINDOW // 2)
            scale = base_scale[None, :] ** power[:, None]
            scale = jnp.concatenate([scale, scale], -1)
            return (freqs, scale)

        def local_attention(q, k, v):
            b, h, n, d = q.shape
            w = WINDOW
            nw = n // w
            bq = q.reshape(b, h, nw, w, d)
            bk = k.reshape(b, h, nw, w, d)
            bv = v.reshape(b, h, nw, w, d)

            def look(t):
                p = jnp.pad(t, ((0, 0), (0, 0), (1, 0), (0, 0), (0, 0)))
                return jnp.concatenate([p[:, :, :nw], p[:, :, 1:]], axis=3)
            bk2, bv2 = (look(bk), look(bv))
            seq = jnp.arange(n).reshape(nw, w)
            seq_p = jnp.pad(seq, ((1, 0), (0, 0)), constant_values=-1)
            jt = jnp.concatenate([seq_p[:nw], seq_p[1:]], axis=1)
            it = seq[:, :, None]
            jb = jt[:, None, :]
            mask = (it < jb) | (it > jb + w) | (jb == -1)
            sim = jnp.einsum('bhwie,bhwje->bhwij', bq, bk2) * QK_SCALE
            sim = jnp.where(mask, -jnp.finfo(sim.dtype).max, sim)
            attn = jax.nn.softmax(sim, -1)
            out = jnp.einsum('bhwij,bhwje->bhwie', attn, bv2)
            return out.reshape(b, h, n, d)

        def attn_layer(x, Wqkv, qs, ksc, Wo):
            b, n, _ = x.shape
            qkv = x @ Wqkv
            q, k, v = jnp.split(qkv, 3, -1)
            sh = lambda t: t.reshape(b, n, HEADS, DIM_HEAD).transpose(0, 2, 1, 3)
            q, k, v = (sh(q), sh(k), sh(v))
            q = l2norm(q) * qs
            k = l2norm(k) * ksc
            freqs, scale = rotary_tables(n)
            cos, sin = (jnp.cos(freqs), jnp.sin(freqs))
            q = q * cos * scale + rotate_half(q) * sin * scale
            inv = 1.0 / scale
            k = k * cos * inv + rotate_half(k) * sin * inv
            out = local_attention(q, k, v)
            out = out.transpose(0, 2, 1, 3).reshape(b, n, INNER)
            return out @ Wo

        def ffn_layer(x, g, bln, W1, b1, W2, b2):
            mu = x.mean(-1, keepdims=True)
            var = ((x - mu) ** 2).mean(-1, keepdims=True)
            xn = (x - mu) / jnp.sqrt(var + 1e-05) * g + bln
            hg = xn @ W1 + b1
            a, gate = jnp.split(hg, 2, -1)
            return a * jax.nn.gelu(gate, approximate=False) @ W2 + b2
        for i in range(DEPTH):
            x = attn_layer(shift_tokens(x), Wqkv[i], q_scale[i], k_scale[i], Wo[i]) + x
            x = ffn_layer(shift_tokens(x), ln_g[i], ln_b[i], W1[i], b1[i], W2[i], b2[i]) + x
        return x
    x = L0_attn_emb
    mod = (_silu(L0_c) @ L0_wmod).reshape(L0_c.shape[0], 6, 1, -1)
    sa, ca, ga, sb, cb, gb = (mod[:, 0], mod[:, 1], mod[:, 2], mod[:, 3], mod[:, 4], mod[:, 5])
    ga = (2 * (ga >= 0) - 1) * jnp.maximum(jnp.abs(ga), 0.25)
    gb = (2 * (gb >= 0) - 1) * jnp.maximum(jnp.abs(gb), 0.25)
    h = _layernorm(x, axis=-1) * (1 + ca) + sa
    x = x + ga * _L0_attn_ref(h, L0_attn_W1, L0_attn_W2, L0_attn_W3, L0_attn_Wo)
    h = _layernorm(x, axis=-1) * (1 + cb) + sb
    x = x + gb * _L0_ffn_ref(h, L0_ffn_Wqkv, L0_ffn_q_scale, L0_ffn_k_scale, L0_ffn_Wo, L0_ffn_ln_g, L0_ffn_ln_b, L0_ffn_W1, L0_ffn_b1, L0_ffn_W2, L0_ffn_b2)
    return x

_drawn_inputs = setup_inputs


def setup_inputs(seed=0):
    import zlib

    import numpy as np

    out = dict(_drawn_inputs(seed))
    spreads = {'L0_ffn_q_scale': (1.0, 0.6),
     'L0_ffn_k_scale': (1.0, 0.6),
     'L0_ffn_ln_g': (1.0, 0.6),
     'L0_ffn_ln_b': (0.0, 0.8),
     'L0_ffn_b1': (0.0, 0.8),
     'L0_ffn_b2': (0.0, 0.655)}
    factors = {'L0_ffn_W1': 7.423, 'L0_ffn_W2': 7.286}
    for name, (base, spread) in spreads.items():
        noise = np.random.default_rng([zlib.crc32(name.encode()), seed]).standard_normal(out[name].shape)
        drawn = base * np.exp(spread * noise) if base else spread * noise
        out[name] = jnp.asarray(drawn.astype(out[name].dtype))
    for name, factor in factors.items():
        out[name] = (out[name] * factor).astype(out[name].dtype)
    return out
```

```python
from contextlib import ExitStack

import concourse.bass as bass
from concourse import mybir

ACT = mybir.ActivationFunctionType
ALU = mybir.AluOpType
AX = mybir.AxisListType
F32 = mybir.dt.float32
BF16 = mybir.dt.bfloat16

P = 128
B, N, E = 8, 256, 128
T = B * N
DEPTH = 6
AH, AD = 8, 16
AG = E // AD
AT = N // AH
H, D = 16, 64
INNER = H * D
W = 32
SPAN = 96
U = N // P
HC = H // 2
VD = D + 1
OW = 96
DENSE = W + P
HID = 341
HT = [(0, 128), (128, 128), (256, HID - 256)]
CH = 512
NC = T // CH
HP = N + 1
NEG = -1e30

C_ID, C_MEAN, C_SUM2, C_MASK, C_ROPE, C_ROPE1 = 0, 128, 256, 384, 384 + 2 * SPAN, 384 + 2 * SPAN + 2 * 4 * D
C_END = C_ROPE1 + AG * AT
L_G, L_B, L_B2, L_BA, L_BG, L_END = 0, 1, 2, 3, 6, 9


def build(nc, xT, w1s, w2s, w3T, woT, cT, wmod, wqkv, scales, wo, params, w1, w2, consts, out):
    with ExitStack() as ctx:
        def sb(name, shape, dt=F32):
            return ctx.enter_context(nc.sbuf_tensor(name, shape, dt))

        def sem(name):
            return ctx.enter_context(nc.semaphore(name))

        cst = sb("cst", [P, C_END])
        ident = cst[:, C_ID:C_ID + P]
        mean_w = cst[:, C_MEAN:C_MEAN + P]
        sum2_w = cst[:, C_SUM2:C_SUM2 + P]
        ident_bf = sb("ident_bf", [P, P], BF16)
        mask_bf = sb("mask_bf", [P, U, 4, SPAN], BF16)
        x1 = sb("x1", [P, T])
        h0 = sb("h0", [P, B * HP])
        h1 = sb("h1", [P, B * HP])
        mod = sb("mod", [P, 6, B])
        gate = sb("gate", [P, 2, B])
        wqkv_sb = sb("wqkv_sb", [P, 3 * INNER])
        wo_sb = sb("wo_sb", [P, INNER // P, E])
        w1_sb = sb("w1_sb", [P, 2 * HID])
        w2_sb = sb("w2_sb", [P, 3, E])
        par = sb("par", [P, L_END])
        scl = sb("scl", [P, 4, D])
        rope = sb("rope", [P, U, 4, D])
        k_t = sb("k_t", [P, U, H // 2, DENSE])
        v_sb = sb("v_sb", [P, U, H * VD + OW - VD])
        v_prev = sb("v_prev", [P, H * VD + OW - VD])
        pd = sb("pd", [P, 96 + H * DENSE])
        x_u = sb("x_u", [P, U, P])
        norm2 = sb("norm2", [P, 2 * H])
        norml = sb("norml", [P, 2 * H])
        rnorm = sb("rnorm", [P, 2 * H])
        rmax = sb("rmax", [P, H])
        rden = sb("rden", [P, H])
        arena = sb("arena", [P, 15 * 1024])

        def take(at, *shape):
            n = 1
            for s in shape:
                n *= s
            assert at + n <= 15 * 1024
            v = arena[:, at:at + n]
            if len(shape) == 2:
                v = v.rearrange("p (a b) -> p a b", a=shape[0])
            elif len(shape) == 3:
                v = v.rearrange("p (a b c) -> p a b c", a=shape[0], b=shape[1])
            return v

        t_cos = take(0, 2, INNER)
        t_sin = take(2048, 2, INNER)
        sq = take(4096, 2, INNER)
        q_t = take(6144, H // 2, P)
        s_sb = take(7168, 2, HC, SPAN)
        p_t = take(8704, H, P)
        pp_t = take(10752, H, W)
        o_n = take(11264, INNER)
        o_t = take(12288, H // 2, P)
        f_x = take(0, NC, CH)
        f_xc = take(2048, NC, CH)
        f_sq = take(4096, NC, CH)
        f_r = take(6144, NC, CH)
        f_xn = take(8192, NC, CH)
        f_g = take(10240, 3, CH)
        f_a = take(11776, 3, CH)
        a_h = take(0, T)
        a_q = take(2048, AG, T // 4)
        a_k = take(6144, AG, T // 4)
        a_raw = take(10240, 2, CH)
        a_w1 = take(11264, AG, 2 * AD)
        a_w2 = take(11520, AG, 2 * AD)
        a_w3 = take(11776, E)
        a_wo = take(11904, E)
        a_cT = take(12032, B)
        a_sil = take(12040, B)
        a_wm = take(12288, 6 * E)
        a_qs = sb("a_qs", [P, 2, P])
        a_ks = sb("a_ks", [P, N])
        a_hs = sb("a_hs", [P, 4, 4, AT])
        a_v = sb("a_v", [P, 4, 2, AD])
        a_p = wqkv_sb[:, 0:2048].rearrange("p (a b) -> p a b", a=8)
        a_pt = h1[:, 0:2048].rearrange("p (a b c) -> p a b c", a=8, b=2)
        a_o = sb("a_o", [P, 4, 2, 2, AH, AD])
        a_max = sb("a_max", [P, 8])
        a_nmax = sb("a_nmax", [P, 8])
        a_den = sb("a_den", [P, 8])
        a_rden = sb("a_rden", [P, 8])

        ps = ctx.enter_context(nc.psum_tensor("ps", [P, 8, 512], F32))

        def pair_of_banks(g):
            return ps[:, 2 * g:2 * g + 2, :]

        names = """
        const_loaded x_loaded a_loaded mod_loaded w_a_loaded w_f_loaded w_q_loaded zeroed bf_ready
        silu_e silu_1 silu_r silu_ready mod_mm mod_ready gate_abs gate_sign
        ln_mean ln_centred ln_squared ln_var ln_log ln_rstd ln_normed ln_scaled
        a_proj a_roped a_summed a_k_ready a_staged a_v_mm a_v_ready a_scored a_maxed a_negated a_exped
        a_turned a_pt_ready a_pv a_recip a_o_ready a_out_mm x1_ready h0_ready
        f_shifted f_up f_gated f_prod f_down f_done
        rope_ready x_staged q_proj k_proj v_proj squared roped normed guarded logged inverted
        rope_added rope_scaled q_turned k_turned q_copied k_copied v_copied v_prev_loaded
        scored maxed centred exped p_turned pp_turned p_copied pp_copied attended recip o_normed
        o_turned o_copied projected att_done final_done stored
        """.split()
        s = {n: sem(n) for n in names}

        def ln_tensor(pe, src, ready, k):
            for c in range(NC):
                ready(pe, c)
                pe.matmul(ps[:, c, :], mean_w, src[:, c, :], start=True, stop=True).then_inc(s["ln_mean"], 1)
            for c in range(NC):
                pe.wait_ge(s["ln_squared"], NC * k + c + 1)
                pe.matmul(ps[:, 4 + c, :], mean_w, f_sq[:, c, :], start=True, stop=True).then_inc(s["ln_var"], 1)

        def ln_vector(dve, src, k):
            for c in range(NC):
                dve.wait_ge(s["ln_mean"], NC * k + c + 1)
                dve.tensor_tensor(f_xc[:, c, :], src[:, c, :], ps[:, c, :], ALU.subtract)\
                   .then_inc(s["ln_centred"], 1)
            for c in range(NC):
                dve.wait_ge(s["ln_rstd"], NC * k + c + 1)
                dve.wait_ge(s["ln_centred"], NC * k + c + 1)
                dve.tensor_tensor(f_xc[:, c, :], f_xc[:, c, :], f_r[:, c, :], ALU.mult)\
                   .then_inc(s["ln_normed"], 1)

        def ln_scalar(act, k):
            for c in range(NC):
                act.wait_ge(s["ln_centred"], NC * k + c + 1)
                act.activation(f_sq[:, c, :], f_xc[:, c, :], ACT.Square).then_inc(s["ln_squared"], 1)
            for c in range(NC):
                act.wait_ge(s["ln_var"], NC * k + c + 1)
                act.activation(f_r[:, c, :], ps[:, 4 + c, :], ACT.Ln, bias=1e-5).then_inc(s["ln_log"], 1)
                act.wait_ge(s["ln_log"], NC * k + c + 1)
                act.activation(f_r[:, c, :], f_r[:, c, :], ACT.Exp, scale=-0.5).then_inc(s["ln_rstd"], 1)

        x1_c = x1[:, :].rearrange("p (c t) -> p c t", c=NC)

        h0_b = h0[:, :].rearrange("p (b t) -> p b t", b=B)
        h1_b = h1[:, :].rearrange("p (b t) -> p b t", b=B)

        block = ctx.enter_context(nc.Block())

        @block.sync
        def _(sp):
            sp.dma_start(cst[:, :], consts).then_inc(s["const_loaded"], 16)
            sp.dma_start(x1[:, :], xT).then_inc(s["x_loaded"], 16)
            sp.dma_start(a_cT, cT).then_inc(s["mod_loaded"], 16)
            sp.dma_start(a_wm, wmod).then_inc(s["mod_loaded"], 16)
            sp.dma_start(a_w1, w1s).then_inc(s["a_loaded"], 16)
            sp.dma_start(a_w2, w2s).then_inc(s["a_loaded"], 16)
            sp.dma_start(a_w3, w3T).then_inc(s["a_loaded"], 16)
            sp.dma_start(a_wo, woT).then_inc(s["a_loaded"], 16)
            sp.wait_ge(s["a_turned"], 32)
            with sp.Fori(0, DEPTH) as layer:
                sp.wait_ge(s["v_proj"], 16 * layer)
                sp.dma_start(wqkv_sb[:, :], wqkv[layer, :, :]).then_inc(s["w_q_loaded"], 16)
                sp.wait_ge(s["rope_ready"], layer)
                sp.dma_start(scl[:, :, :], scales[layer, :, :].unsqueeze(0).to_broadcast([P, 4, D]))\
                  .then_inc(s["w_q_loaded"], 16)
                sp.wait_ge(s["projected"], 16 * layer)
                sp.dma_start(wo_sb[:, :, :], wo[layer, :, :].rearrange("(c p) e -> p c e", p=P))\
                  .then_inc(s["w_a_loaded"], 16)
                sp.wait_ge(s["f_done"], NC * layer)
                sp.dma_start(w1_sb[:, :], w1[layer, :, :]).then_inc(s["w_f_loaded"], 16)
                sp.dma_start(w2_sb[:, 0:2, :], w2[layer, 0:256, :].rearrange("(c p) e -> p c e", p=P))\
                  .then_inc(s["w_f_loaded"], 16)
                sp.dma_start(w2_sb[0:HT[2][1], 2, :], w2[layer, 256:HID, :]).then_inc(s["w_f_loaded"], 16)
                sp.dma_start(par[:, :], params[layer, :, :]).then_inc(s["w_f_loaded"], 16)
                with sp.Fori(0, B) as b:
                    pair = sp.snap(layer * B + b)
                    sp.wait_ge(s["v_copied"], 2 * pair + 1)
                    sp.dma_start(v_prev[96:128, :], v_sb[96:128, 0, :]).then_inc(s["v_prev_loaded"], 16)
            sp.wait_ge(s["final_done"], B)
            sp.dma_start(out, x1[:, :]).then_inc(s["stored"], 16)
            sp.wait_ge(s["stored"], 16)

        @block.gpsimd
        def _(pool):
            pool.memset(h0[:, :], 0.0).then_inc(s["zeroed"], 1)
            pool.memset(v_sb[:, :, :], 1.0).then_inc(s["zeroed"], 1)
            pool.memset(k_t[:, :, :, :], 0.0).then_inc(s["zeroed"], 1)
            pool.memset(pd[:, :], 0.0).then_inc(s["zeroed"], 1)

            with pool.Fori(0, 2) as bb:
                with pool.Fori(0, AH) as head:
                    i = pool.snap(bb * AH + head)
                    col = pool.snap(bb * N + head * AT)
                    pool.wait_ge(s["a_scored"], 2 * i)
                    pool.wait_ge(s["a_k_ready"], AG)
                    for c in range(2):
                        pool.tensor_copy(a_qs[:, c, :].rearrange("p (g t) -> p g t", g=AG),
                                         a_q[:, :, bass.ds(col + 16 * c, 16)]).then_inc(s["a_staged"], 1)
                    pool.tensor_copy(a_ks[:, :].rearrange("p (g t) -> p g t", g=AG),
                                     a_k[:, :, bass.ds(col, AT)]).then_inc(s["a_staged"], 1)
                    for r in range(4):
                        pool.tensor_copy(a_hs[:, :, r, :],
                                         a_h.rearrange("p (j t) -> p j t", j=4)[:, :, bass.ds(col, AT)])\
                            .then_inc(s["a_staged"], 1)
            pool.wait_ge(s["h0_ready"], B)

            def rotate(pair, m):
                n = 2 * pair + m
                for j in range(2):
                    pool.wait_ge(s["roped"], 4 * n + 2 * j + 2)
                    pool.tensor_tensor(t_cos[:, j, :], t_cos[:, j, :], t_sin[:, j, :], ALU.add)\
                        .then_inc(s["rope_added"], 1)
                pool.wait_ge(s["inverted"], n + 1)
                for j in range(2):
                    pool.wait_ge(s["rope_added"], 2 * n + j + 1)
                    v = t_cos[:, j, :].rearrange("p (h d) -> p h d", h=H)
                    pool.tensor_tensor(v, v, rnorm[:, j * H:j * H + H].unsqueeze(2).to_broadcast([P, H, D]),
                                       ALU.mult).then_inc(s["rope_scaled"], 1)

            with pool.Fori(0, DEPTH) as layer:
                first = pool.snap(layer * B)
                pool.wait_ge(s["w_q_loaded"], 32 * layer + 32)
                pool.wait_ge(s["f_done"], NC * layer)
                for m in range(U):
                    pool.tensor_tensor(rope[:, m, :, :],
                                       cst[:, C_ROPE + 4 * D * m:C_ROPE + 4 * D * (m + 1)]
                                       .rearrange("p (k d) -> p k d", k=4), scl[:, :, :], ALU.mult)
                pool.drain().then_inc(s["rope_ready"], 1)
                rotate(first, 0)
                with pool.Fori(0, B - 1) as b:
                    pair = pool.snap(first + b)
                    rotate(pair, 1)
                    rotate(pair + 1, 0)
                rotate(first + (B - 1), 1)

        @block.tensor
        def _(pe):
            pe.wait_ge(s["mod_loaded"], 32)
            pe.wait_ge(s["silu_ready"], 1)
            for k in range(6):
                mm = pe.matmul(ps[:, 7, B * k:B * k + B], a_wm[:, E * k:E * k + E], a_sil, start=True, stop=True)
            mm.then_inc(s["mod_mm"], 1)
            pe.wait_ge(s["mod_ready"], 1)
            pe.wait_ge(s["const_loaded"], 16)

            def x_ready(pe, c):
                pe.wait_ge(s["x_loaded"], 16)

            ln_tensor(pe, x1_c, x_ready, 0)
            pe.wait_ge(s["ln_scaled"], B)
            pe.wait_ge(s["a_loaded"], 64)
            for n, w in enumerate((a_w1, a_w2)):
                for g in range(AG):
                    i = n * AG + g
                    if i >= 4:
                        pe.wait_ge(s["a_roped"], i - 3)
                    for j in range(4):
                        mm = pe.matmul(ps[32 * j:32 * j + 32, i % 4, :], w[:, g, :],
                                       a_h[:, CH * j:CH * j + CH], start=True, stop=True)
                    mm.then_inc(s["a_proj"], 1)
            for g in range(AG):
                pe.wait_ge(s["a_roped"], AG + g + 1)
                if g >= 2:
                    pe.wait_ge(s["a_k_ready"], g - 1)
                pe.matmul(ps[:, 4 + g % 2, :], sum2_w, a_k[:, g, :], start=True, stop=True)\
                    .then_inc(s["a_summed"], 1)
            pe.wait_ge(s["a_k_ready"], AG)
            pe.wait_ge(s["a_roped"], 2 * AG)

            with pe.Fori(0, 2 * AH) as i:
                pe.wait_ge(s["a_staged"], 7 * i + 7)
                pe.wait_ge(s["a_v_ready"], 4 * i)
                for j in range(4):
                    mm = pe.matmul(ps[:, 6, P * j:P * j + P], a_hs[:, j, :, :].rearrange("p r t -> p (r t)"),
                                   a_w3, start=True, stop=True)
                mm.then_inc(s["a_v_mm"], 1)
                for half in range(2):
                    pe.wait_ge(s["a_exped"], 8 * i)
                    for q in range(4):
                        j, c = 2 * half + q // 2, q % 2
                        mm = pe.matmul(ps[:, 2 * half + q // 2, N * c:N * c + N],
                                       a_qs[32 * j:32 * j + 32, c, :], a_ks[32 * j:32 * j + 32, :],
                                       start=True, stop=True, tile_position=(32 * j, 0))
                    mm.then_inc(s["a_scored"], 1)
                for half in range(2):
                    pe.wait_ge(s["a_exped"], 8 * i + 4 * half + 4)
                    pe.wait_ge(s["a_pt_ready"], 2 * i + half)
                    for q in range(4):
                        for kh in range(2):
                            mm = pe.transpose(ps[:, 4 + q // 2, P * (2 * (q % 2) + kh):][:, 0:P],
                                              a_p[:, 4 * half + q, P * kh:P * kh + P], ident)
                    mm.then_inc(s["a_turned"], 1)
                pe.wait_ge(s["a_v_ready"], 4 * i + 4)
                pe.wait_ge(s["a_o_ready"], i)
                for q in range(8):
                    pe.wait_ge(s["a_pt_ready"], 2 * i + q // 4 + 1)
                    for kh in range(2):
                        mm = pe.matmul(ps[:, 7, AD * q:AD * q + AD], a_pt[:, q, kh, :], a_v[:, q // 2, kh, :],
                                       start=(kh == 0), stop=(kh == 1))
                mm.then_inc(s["a_pv"], 1)
            pe.wait_ge(s["a_o_ready"], 2 * AH)
            for b in range(B):
                for c in range(2):
                    mm = pe.matmul(ps[:, b // 2, N * (b % 2) + P * c:][:, 0:P],
                                   a_o[:, b // 2, c, b % 2, :, :].rearrange("p h d -> p (h d)"), a_wo,
                                   start=True, stop=True)
                if b % 2:
                    mm.then_inc(s["a_out_mm"], 1)

            def x1_chunk(pe, c):
                pe.wait_ge(s["x1_ready"], B)

            ln_tensor(pe, x1_c, x1_chunk, 1)

            def q_k(pair, m):
                n = 2 * pair + m
                pe.wait_ge(s["x_staged"], 2 * n + 2)
                for j, done in ((0, "q_proj"), (1, "k_proj")):
                    pe.wait_ge(s["q_copied" if j == 0 else "k_copied"], n if j == 0 else
                               (3 * pair if m == 0 else 3 * pair + 2))
                    for c in range(2):
                        mm = pe.matmul(ps[:, 2 * j + c, :], x_u[:, m, :],
                                       wqkv_sb[:, INNER * j + 512 * c:][:, 0:512], start=True, stop=True)
                    mm.then_inc(s[done], 1)

            def v(pair, m):
                n = 2 * pair + m
                pe.wait_ge(s["roped"], 4 * n + 2)
                pe.wait_ge(s["squared"], 2 * n + 1)
                for c in range(2):
                    mm = pe.matmul(ps[:, c, :], x_u[:, m, :], wqkv_sb[:, 2 * INNER + 512 * c:][:, 0:512],
                                   start=True, stop=True)
                mm.then_inc(s["v_proj"], 1)

            def turn_q_k(pair, m):
                n = 2 * pair + m
                for j, done in ((0, "q_turned"), (1, "k_turned")):
                    pe.wait_ge(s["rope_scaled"], 2 * n + j + 1)
                    if j == 0:
                        pe.wait_ge(s["v_copied"], n + 1)
                    else:
                        pe.wait_ge(s["roped"], 4 * n + 4)
                        pe.wait_ge(s["squared"], 2 * n + 2)
                        pe.wait_ge(s["pp_copied"], pair)
                    for c in range(H // 2):
                        mm = pe.transpose(ps[:, 2 * j + c // 4, P * (c % 4):][:, 0:P],
                                          t_cos[:, j, P * c:P * c + P], ident)
                    mm.then_inc(s[done], 1)

            def scores(pair, m):
                n = 2 * pair + m
                pe.wait_ge(s["q_copied"], n + 1)
                pe.wait_ge(s["k_copied"], 3 * pair + m + 2)
                for g in range(2):
                    if g == 0:
                        pe.wait_ge(s["o_copied"], n)
                    else:
                        pe.wait_ge(s["att_done"], n)
                    for c in range(2):
                        pe.matmul(ps[:, 4 + 2 * g + c, 0:4 * SPAN], ident_bf[:, :],
                                  mask_bf[:, m, :, :].rearrange("p a b -> p (a b)"),
                                  start=True, stop=False, skip_group_check=True)
                        for hh in range(4):
                            h = HC * g + 2 * hh + c
                            r = D * c
                            for j in range(2):
                                mm = pe.matmul(ps[64 * j:64 * j + 64, 4 + 2 * g + c, SPAN * hh:SPAN * hh + SPAN],
                                               q_t[r:r + D, h // 2, 64 * j:64 * j + 64],
                                               k_t[r:r + D, m, h // 2, 64 * j:64 * j + SPAN],
                                               start=False, stop=(hh == 3), skip_group_check=True,
                                               tile_position=(r, 64 * j))
                    mm.then_inc(s["scored"], 1)

            def turn_p(pair, m, ahead):
                n = 2 * pair + m
                for g in range(2):
                    if m == 1 and g == 1 and ahead:
                        pe.wait_ge(s["roped"], 4 * n + 8)
                        pe.wait_ge(s["squared"], 2 * n + 4)
                    elif m == 1 and g == 1:
                        pe.wait_ge(s["k_copied"], 3 * pair + 3)
                    pe.wait_ge(s["exped"], 4 * n + 2 * g + 2)
                    pe.wait_ge(s["centred"], 2 * n + g + 1)
                    for hh in range(HC):
                        h = HC * g + hh
                        mm = pe.transpose(ps[:, 4 + 2 * g + hh // 4, P * (hh % 4):][:, 0:P],
                                          pd[:, 96 + DENSE * h + W:][:, 0:P], ident)
                    mm.then_inc(s["p_turned"], 1)
                if m == 1:
                    for h in range(H):
                        mm = pe.transpose(ps[:, 2, W * h:W * h + W], pd[0:W, DENSE * h:][:, 0:P],
                                          ident[0:W, 0:W])
                    mm.then_inc(s["pp_turned"], 1)

            def attend(pair, m):
                n = 2 * pair + m
                pe.wait_ge(s["v_copied"], n + 1)
                if m == 1:
                    pe.wait_ge(s["v_prev_loaded"], 16 * pair + 16)
                    pe.wait_ge(s["pp_copied"], pair + 1)
                for g in range(2):
                    pe.wait_ge(s["p_copied"], 2 * n + g + 1)
                    for hh in range(HC):
                        h = HC * g + hh
                        o = ps[:, 4 + 2 * g + hh // 4, OW * (hh % 4):][:, 0:OW]
                        mm = pe.matmul(o, p_t[:, h, :], v_sb[:, m, VD * h:VD * h + OW], start=True,
                                       stop=(m == 0), skip_group_check=True)
                        if m == 1:
                            mm = pe.matmul(o[0:W], pp_t[96:128, h, :], v_prev[96:128, VD * h:VD * h + OW],
                                           start=False, stop=True, skip_group_check=True,
                                           tile_position=(96, 0))
                    mm.then_inc(s["attended"], 1)

            def project(pair, m):
                n = 2 * pair + m
                pe.wait_ge(s["o_normed"], 2 * n + 2)
                for c in range(H // 2):
                    mm = pe.transpose(ps[:, 4 + c // 4, P * (c % 4):][:, 0:P], o_n[:, P * c:P * c + P], ident)
                mm.then_inc(s["o_turned"], 1)

            def project_out(pair, m):
                n = 2 * pair + m
                pe.wait_ge(s["o_copied"], n + 1)
                for c in range(H // 2):
                    mm = pe.matmul(ps[:, 6, 0:P], wo_sb[:, c, :], o_t[:, c, :], start=(c == 0),
                                   stop=(c == H // 2 - 1))
                mm.then_inc(s["projected"], 1)

            def step(pair, m, after):
                if after:
                    q_k(*after)
                scores(pair, m)
                if after:
                    v(*after)
                turn_p(pair, m, bool(after))
                attend(pair, m)
                project(pair, m)
                if after:
                    turn_q_k(*after)
                project_out(pair, m)

            pe.wait_ge(s["zeroed"], 4)
            pe.wait_ge(s["bf_ready"], 2)
            pe.wait_ge(s["h0_ready"], B)
            with pe.Fori(0, DEPTH) as layer:
                first = pe.snap(layer * B)
                pe.wait_ge(s["w_q_loaded"], 32 * layer + 32)
                pe.wait_ge(s["w_a_loaded"], 16 * layer + 16)
                pe.wait_ge(s["f_done"], NC * layer)
                q_k(first, 0)
                v(first, 0)
                turn_q_k(first, 0)
                with pe.Fori(0, B - 1) as b:
                    pair = pe.snap(first + b)
                    step(pair, 0, (pair, 1))
                    step(pair, 1, (pair + 1, 0))
                last = pe.snap(first + (B - 1))
                step(last, 0, (last, 1))
                step(last, 1, None)

                pe.wait_ge(s["w_f_loaded"], 64 * layer + 64)
                pe.wait_ge(s["att_done"], 16 * layer + 16)

                def shifted(pe, c):
                    pe.wait_ge(s["f_shifted"], 2 * NC * layer + 2 * NC)

                ln_tensor(pe, f_x, shifted, layer + 2)
                for c in range(NC):
                    n = NC * layer + c
                    pe.wait_ge(s["ln_scaled"], n + 1 + B + B)
                    if c == 0:
                        pe.wait_ge(s["ln_rstd"], NC * layer + 3 * NC)
                    if c:
                        pe.wait_ge(s["f_gated"], 3 * n)
                        pe.wait_ge(s["f_prod"], 3 * n)
                    for k in range(2):
                        for i, (at, size) in enumerate(HT):
                            col = HID * (1 - k) + at
                            pe.matmul(ps[0:size, 3 * (1 - k) + i, :], w1_sb[:, col:col + size], f_xn[:, c, :],
                                      start=True, stop=True).then_inc(s["f_up"], 1)
                    if c >= 2:
                        pe.wait_ge(s["f_done"], n - 1)
                    for i, (at, size) in enumerate(HT):
                        pe.wait_ge(s["f_prod"], 3 * n + i + 1)
                        mm = pe.matmul(ps[:, 6 + c % 2, :], w2_sb[0:size, i, :], f_a[0:size, i, :],
                                       start=(i == 0), stop=(i == 2))
                    mm.then_inc(s["f_down"], 1)

        @block.scalar
        def _(act):
            act.preload_act_table_set("natural_log_exp_and_others")
            act.wait_ge(s["mod_loaded"], 32)
            act.activation(a_sil, a_cT, ACT.Exp, scale=-1.0).then_inc(s["silu_e"], 1)
            act.wait_ge(s["mod_mm"], 1)
            act.activation(mod[:, :, :].rearrange("p k b -> p (k b)"), ps[:, 7, 0:6 * B], ACT.Copy)\
               .then_inc(s["mod_ready"], 1)
            ln_scalar(act, 0)
            for g in range(AG):
                act.wait_ge(s["a_summed"], g + 1)
                act.activation(a_k[:, g, :], ps[:, 4 + g % 2, :], ACT.Copy).then_inc(s["a_k_ready"], 1)

            with act.Fori(0, 2 * AH) as i:
                act.wait_ge(s["a_v_mm"], i + 1)
                act.wait_ge(s["a_pv"], i)
                for r in range(4):
                    act.activation(a_v[32 * r:32 * r + 32, :, :, :],
                                   ps[32 * r:32 * r + 32, 6, :]
                                   .rearrange("p (j k r d) -> p j k r d", j=4, k=2, r=4)[:, :, :, r, :],
                                   ACT.Copy).then_inc(s["a_v_ready"], 1)
                for half in range(2):
                    act.wait_ge(s["a_negated"], 2 * i + half + 1)
                    act.wait_ge(s["a_turned"], 2 * i)
                    for q in range(4):
                        k = 4 * half + q
                        act.activation(a_p[:, k, :], ps[:, 2 * half + q // 2, N * (q % 2):][:, 0:N], ACT.Exp,
                                       bias=a_nmax[:, k:k + 1], scale=AH ** -0.5,
                                       accum_out=a_den[:, k:k + 1]).then_inc(s["a_exped"], 1)
                for half in range(2):
                    act.wait_ge(s["a_turned"], 2 * i + half + 1)
                    act.wait_ge(s["a_pv"], i)
                    act.activation(a_pt[:, 4 * half:4 * half + 4, :, :].rearrange("p a b c -> p (a b c)"),
                                   ps[:, 4:6, :].rearrange("p a b -> p (a b)"), ACT.Copy)\
                       .then_inc(s["a_pt_ready"], 1)
            ln_scalar(act, 1)

            def squares(pair, m):
                n = 2 * pair + m
                for j, ready in ((0, "q_proj"), (1, "k_proj")):
                    act.wait_ge(s[ready], n + 1)
                    if j == 0:
                        act.wait_ge(s["normed"], n)
                    act.activation(sq[:, j, :], ps[:, 2 * j:2 * j + 2, :].rearrange("p a b -> p (a b)"),
                                   ACT.Square).then_inc(s["squared"], 1)

            def inverse_norms(pair, m):
                n = 2 * pair + m
                act.wait_ge(s["guarded"], n + 1)
                act.activation(norml[:, :], norm2[:, :], ACT.Ln, scale=2.0 ** 24).then_inc(s["logged"], 1)
                act.wait_ge(s["logged"], n + 1)
                act.wait_ge(s["rope_scaled"], 2 * n)
                act.activation(rnorm[:, :], norml[:, :], ACT.Exp, scale=-0.5, bias=8.317766166719343)\
                   .then_inc(s["inverted"], 1)

            def copy_q_k(pair, m):
                n = 2 * pair + m
                act.wait_ge(s["q_turned"], n + 1)
                act.wait_ge(s["scored"], 2 * n)
                act.activation(q_t.rearrange("p a b -> p (a b)"),
                               pair_of_banks(0).rearrange("p a b -> p (a b)"), ACT.Copy)\
                   .then_inc(s["q_copied"], 1)
                act.wait_ge(s["k_turned"], n + 1)
                src = pair_of_banks(1).rearrange("p a (b c) -> p (a b) c", b=4)
                act.activation(k_t[:, m, :, W:DENSE], src, ACT.Copy).then_inc(s["k_copied"], 1)
                if m == 0:
                    act.activation(k_t[:, 1, :, 0:W], src[:, :, P - W:P], ACT.Copy).then_inc(s["k_copied"], 1)

            def copy_v(pair, m):
                n = 2 * pair + m
                act.wait_ge(s["v_proj"], n + 1)
                act.wait_ge(s["attended"], 4 * pair)
                if m == 0:
                    act.wait_ge(s["v_prev_loaded"], 16 * pair)
                act.activation(v_sb[:, m, 0:H * VD].rearrange("p (h d) -> p h d", h=H)[:, :, 0:D],
                               pair_of_banks(0).rearrange("p a (b c) -> p (a b) c", b=8), ACT.Copy)\
                   .then_inc(s["v_copied"], 1)

            def exps(pair, m):
                n = 2 * pair + m
                for g in range(2):
                    act.wait_ge(s["centred"], 2 * n + g + 1)
                    act.wait_ge(s["p_turned"], 2 * n)
                    act.wait_ge(s["pp_turned"], pair)
                    for j in range(2):
                        o = pd[64 * j:64 * j + 64, 96:].rearrange("p (h k) -> p h k", h=H)
                        act.activation(o[:, HC * g:HC * g + HC, 64 * j:64 * j + SPAN],
                                       s_sb[64 * j:64 * j + 64, g, :, :], ACT.Exp).then_inc(s["exped"], 1)

            def copy_p(pair, m):
                n = 2 * pair + m
                for g in range(2):
                    act.wait_ge(s["p_turned"], 2 * n + g + 1)
                    act.wait_ge(s["attended"], 2 * n)
                    act.activation(p_t[:, HC * g:HC * g + HC, :].rearrange("p a b -> p (a b)"),
                                   pair_of_banks(2 + g).rearrange("p a b -> p (a b)"), ACT.Copy)\
                       .then_inc(s["p_copied"], 1)
                if m == 1:
                    act.wait_ge(s["pp_turned"], pair + 1)
                    act.activation(pp_t[96:128, :, :].rearrange("p a b -> p (a b)"), ps[96:128, 2, :],
                                   ACT.Copy).then_inc(s["pp_copied"], 1)

            def copy_o(pair, m):
                n = 2 * pair + m
                act.wait_ge(s["o_turned"], n + 1)
                act.wait_ge(s["projected"], n)
                act.activation(o_t.rearrange("p a b -> p (a b)"),
                               pair_of_banks(2).rearrange("p a b -> p (a b)"), ACT.Copy)\
                   .then_inc(s["o_copied"], 1)

            def step(pair, m, after):
                if after:
                    squares(*after)
                exps(pair, m)
                if after:
                    inverse_norms(*after)
                copy_p(pair, m)
                if after and m == 0:
                    copy_v(*after)
                if after and m == 1:
                    copy_v(*after)
                copy_o(pair, m)
                if after:
                    copy_q_k(*after)

            act.wait_ge(s["zeroed"], 4)
            with act.Fori(0, DEPTH) as layer:
                act.preload_act_table_set("natural_log_exp_and_others")
                first = act.snap(layer * B)
                act.wait_ge(s["f_done"], NC * layer)
                squares(first, 0)
                inverse_norms(first, 0)
                copy_v(first, 0)
                copy_q_k(first, 0)
                with act.Fori(0, B - 1) as b:
                    pair = act.snap(first + b)
                    step(pair, 0, (pair, 1))
                    step(pair, 1, (pair + 1, 0))
                last = act.snap(first + (B - 1))
                step(last, 0, (last, 1))
                step(last, 1, None)
                act.wait_ge(s["att_done"], 16 * layer + 16)
                act.wait_ge(s["projected"], 16 * layer + 16)
                for c in range(NC):
                    act.activation(f_x[64:128, c, :].rearrange("p (b t) -> p b t", b=2),
                                   h1_b[64:128, 2 * c:2 * c + 2, 0:N], ACT.Copy).then_inc(s["f_shifted"], 1)
                ln_scalar(act, layer + 2)
                for c in range(NC):
                    n = NC * layer + c
                    for i, (at, size) in enumerate(HT):
                        act.wait_ge(s["f_up"], 6 * n + i + 1)
                        act.wait_ge(s["f_prod"], 3 * n)
                        act.activation(f_g[0:size, i, :], ps[0:size, 3 + i, :], ACT.Gelu,
                                       bias=par[0:size, L_BG + i:L_BG + i + 1]).then_inc(s["f_gated"], 1)

        @block.vector
        def _(dve):
            dve.wait_ge(s["silu_e"], 1)
            dve.tensor_scalar(a_sil, a_sil, 1.0, None, ALU.add).then_inc(s["silu_1"], 1)
            dve.wait_ge(s["silu_1"], 1)
            dve.reciprocal(a_sil, a_sil).then_inc(s["silu_r"], 1)
            dve.wait_ge(s["silu_r"], 1)
            dve.tensor_tensor(a_sil, a_sil, a_cT, ALU.mult).then_inc(s["silu_ready"], 1)
            dve.wait_ge(s["const_loaded"], 16)
            dve.tensor_copy(ident_bf[:, :], ident).then_inc(s["bf_ready"], 1)
            dve.tensor_copy(mask_bf[:, :, :, :],
                            cst[:, C_MASK:C_MASK + U * SPAN].rearrange("p (m k) -> p m k", m=U)
                            .unsqueeze(2).to_broadcast([P, U, 4, SPAN])).then_inc(s["bf_ready"], 1)
            dve.wait_ge(s["mod_ready"], 1)
            for n, k in enumerate((2, 5)):
                dve.tensor_scalar(gate[:, n, :], mod[:, k, :], 0.25, None, ALU.max).then_inc(s["gate_abs"], 1)
                dve.wait_ge(s["gate_abs"], 2 * n + 1)
                dve.scalar_tensor_tensor(gate[:, n, :], mod[:, k, :], -1.0, gate[:, n, :], ALU.mult, ALU.max)\
                   .then_inc(s["gate_abs"], 1)
                dve.tensor_scalar(mod[:, k, :], mod[:, k, :], 0.0, 2.0, ALU.is_ge, ALU.mult)\
                   .then_inc(s["gate_sign"], 1)
            dve.wait_ge(s["gate_sign"], 2)
            dve.wait_ge(s["gate_abs"], 4)
            for n, k in enumerate((2, 5)):
                dve.scalar_tensor_tensor(gate[:, n, :], mod[:, k, :], -1.0, gate[:, n, :], ALU.add, ALU.mult)\
                   .then_inc(s["gate_sign"], 1)
            for k in (1, 4):
                dve.tensor_scalar(mod[:, k, :], mod[:, k, :], 1.0, None, ALU.add).then_inc(s["gate_sign"], 1)
            dve.wait_ge(s["gate_sign"], 6)
            dve.wait_ge(s["x_loaded"], 16)
            ln_vector(dve, x1_c, 0)
            xc = f_xc.rearrange("p c t -> p (c t)")
            for b in range(B):
                dve.wait_ge(s["ln_normed"], b // 2 + 1)
                dve.tensor_scalar(a_h[:, N * b:N * b + N], xc[:, N * b:N * b + N], mod[:, 1, b:b + 1],
                                  mod[:, 0, b:b + 1], ALU.mult, ALU.add).then_inc(s["ln_scaled"], 1)
            dve.wait_ge(s["ln_scaled"], B)
            tab = cst[:, C_ROPE1:C_ROPE1 + AG * AT].rearrange("p (g t) -> p g t", g=AG)
            for n, dst in enumerate((a_q, a_k)):
                for g in range(AG):
                    i = n * AG + g
                    dve.wait_ge(s["a_proj"], i + 1)
                    dve.tensor_tensor(dst[:, g, :].rearrange("p (i t) -> p i t", t=AT),
                                      ps[:, i % 4, :].rearrange("p (i t) -> p i t", t=AT),
                                      tab[:, g, :].unsqueeze(1).to_broadcast([P, CH // AT, AT]), ALU.mult)\
                       .then_inc(s["a_roped"], 1)
            with dve.Fori(0, 2) as bb:
                with dve.Fori(0, AH) as head:
                    i = dve.snap(bb * AH + head)
                    for half in range(2):
                        dve.wait_ge(s["a_scored"], 2 * i + half + 1)
                        dve.tensor_reduce(a_max[:, 4 * half:4 * half + 4],
                                          ps[:, 2 * half:2 * half + 2, :].rearrange("p a (b c) -> p (a b) c", b=2),
                                          AX.X, ALU.max).then_inc(s["a_maxed"], 1)
                        dve.wait_ge(s["a_maxed"], 2 * i + half + 1)
                        dve.tensor_scalar(a_nmax[:, 4 * half:4 * half + 4], a_max[:, 4 * half:4 * half + 4],
                                          -AH ** -0.5, None, ALU.mult).then_inc(s["a_negated"], 1)
                    dve.wait_ge(s["a_exped"], 8 * i + 8)
                    dve.reciprocal(a_rden[:, :], a_den[:, :]).then_inc(s["a_recip"], 1)
                    dve.wait_ge(s["a_recip"], i + 1)
                    dve.wait_ge(s["a_pv"], i + 1)
                    dve.tensor_tensor(a_o[:, :, :, bass.ds(bb, 1), bass.ds(head, 1), :]
                                      .rearrange("p j c b h d -> p (j c) (b h d)"),
                                      ps[:, 7, 0:P].rearrange("p (q d) -> p q d", q=8),
                                      a_rden[:, :].unsqueeze(2).to_broadcast([P, 8, AD]), ALU.mult)\
                       .then_inc(s["a_o_ready"], 1)
            for b in range(B):
                dve.wait_ge(s["a_out_mm"], b // 2 + 1)
                dve.scalar_tensor_tensor(x1[:, N * b:N * b + N], ps[:, b // 2, N * (b % 2):][:, 0:N],
                                         gate[:, 0, b:b + 1], x1[:, N * b:N * b + N], ALU.mult, ALU.add)\
                   .then_inc(s["x1_ready"], 1)
            dve.wait_ge(s["x1_ready"], B)
            ln_vector(dve, x1_c, 1)
            dve.wait_ge(s["zeroed"], 4)
            for b in range(B):
                dve.wait_ge(s["ln_normed"], NC + b // 2 + 1)
                dve.tensor_scalar(h0[:, HP * b + 1:HP * b + HP], xc[:, N * b:N * b + N], mod[:, 4, b:b + 1],
                                  mod[:, 3, b:b + 1], ALU.mult, ALU.add).then_inc(s["h0_ready"], 1)
                dve.sem_inc(s["ln_scaled"], 1)
            dve.wait_ge(s["a_pt_ready"], 4 * AH)
            dve.wait_ge(s["a_pv"], 2 * AH)
            dve.memset(h1[:, :], 0.0)
            dve.wait_ge(s["h0_ready"], B)

            def rope_products(pair, m):
                n = 2 * pair + m
                for j in range(2):
                    dve.wait_ge(s["squared"], 2 * n + j + 1)
                    src = pair_of_banks(j).rearrange("p a (h d) -> p (a h) d", h=8)
                    tc, ts = rope[:, m, 2 * j, :], rope[:, m, 2 * j + 1, :]
                    dve.tensor_tensor(t_cos[:, j, :].rearrange("p (h d) -> p h d", h=H), src,
                                      tc.unsqueeze(1).to_broadcast([P, H, D]), ALU.mult).then_inc(s["roped"], 1)
                    dve.tensor_tensor(t_sin[:, j, :].rearrange("p (h s d) -> p h s d", h=H, s=2),
                                      pair_of_banks(j).rearrange("p a (h s d) -> p (a h) s d", h=8, s=2)[:, :, ::-1, :],
                                      ts.rearrange("p (s d) -> p s d", s=2).unsqueeze(1)
                                      .to_broadcast([P, H, 2, D // 2]), ALU.mult).then_inc(s["roped"], 1)

            def norms(pair, m):
                n = 2 * pair + m
                dve.wait_ge(s["squared"], 2 * n + 2)
                dve.wait_ge(s["logged"], n)
                dve.tensor_reduce(norm2[:, :], sq.rearrange("p a (h d) -> p (a h) d", h=H), AX.X, ALU.add)\
                   .then_inc(s["normed"], 1)
                dve.wait_ge(s["normed"], n + 1)
                dve.tensor_scalar(norm2[:, :], norm2[:, :], 1e-24, None, ALU.max).then_inc(s["guarded"], 1)

            def centre(pair, m, g):
                n = 2 * pair + m
                dve.wait_ge(s["scored"], 2 * n + g + 1)
                src = pair_of_banks(2 + g)[:, :, 0:4 * SPAN].rearrange("p a (h k) -> p a h k", h=4)
                mx = rmax[:, HC * g:HC * g + HC].rearrange("p (h a) -> p a h", a=2)
                dve.tensor_reduce(mx, src, AX.X, ALU.max)\
                   .then_inc(s["maxed"], 1)
                dve.wait_ge(s["maxed"], 2 * n + g + 1)
                dve.wait_ge(s["exped"], 4 * n)
                dve.tensor_tensor(s_sb[:, g, :, :].rearrange("p (h a) k -> p a h k", a=2), src,
                                  mx.unsqueeze(3).to_broadcast([P, 2, 4, SPAN]), ALU.subtract).then_inc(s["centred"], 1)

            def normalise(pair, m):
                n = 2 * pair + m
                for g in range(2):
                    dve.wait_ge(s["attended"], 2 * n + g + 1)
                    o = pair_of_banks(2 + g)[:, :, 0:4 * OW].rearrange("p a (h k) -> p a h k", h=4)
                    rd = rden[:, HC * g:HC * g + HC].rearrange("p (a h) -> p a h", a=2)
                    dve.reciprocal(rd, o[:, :, :, D]).then_inc(s["recip"], 1)
                    dve.wait_ge(s["recip"], 2 * n + g + 1)
                    dve.wait_ge(s["o_turned"], n)
                    dve.tensor_tensor(o_n[:, HC * D * g:HC * D * (g + 1)]
                                      .rearrange("p (a h d) -> p a h d", a=2, h=4), o[:, :, :, 0:D],
                                      rd.unsqueeze(3).to_broadcast([P, 2, 4, D]), ALU.mult)\
                       .then_inc(s["o_normed"], 1)

            def residual(pair, b, m):
                n = 2 * pair + m
                col = b * HP + (1 + P * m)
                dve.wait_ge(s["projected"], n + 1)
                dve.tensor_tensor(h1[:, bass.ds(col, P)], ps[:, 6, 0:P], h0[:, bass.ds(col, P)], ALU.add)\
                   .then_inc(s["att_done"], 1)

            def stage(b, m):
                col = b * HP + P * m
                dve.tensor_scalar(x_u[0:64, m, :], h0[0:64, bass.ds(col + 1, P)], 1.0, None, ALU.mult)\
                   .then_inc(s["x_staged"], 1)
                dve.tensor_scalar(x_u[64:128, m, :], h0[64:128, bass.ds(col, P)], 1.0, None, ALU.mult)\
                   .then_inc(s["x_staged"], 1)

            def step(pair, b, m, after, ahead=None):
                if after:
                    rope_products(*after)
                centre(pair, m, 0)
                if after:
                    norms(*after)
                if ahead:
                    dve.wait_ge(s["v_proj"], 2 * pair + m + 1)
                    stage(b + 1, m)
                centre(pair, m, 1)
                normalise(pair, m)
                residual(pair, b, m)

            with dve.Fori(0, DEPTH) as layer:
                first = dve.snap(layer * B)
                dve.wait_ge(s["v_proj"], 2 * first)
                dve.wait_ge(s["f_done"], NC * layer)
                stage(0, 0)
                stage(0, 1)
                dve.wait_ge(s["rope_ready"], layer + 1)
                rope_products(first, 0)
                norms(first, 0)
                with dve.Fori(0, B - 1) as b:
                    pair = dve.snap(first + b)
                    step(pair, b, 0, (pair, 1), ahead=True)
                    step(pair, b, 1, (pair + 1, 0), ahead=True)
                last = dve.snap(first + (B - 1))
                step(last, B - 1, 0, (last, 1))
                step(last, B - 1, 1, None)

                dve.wait_ge(s["att_done"], 16 * layer + 16)
                for c in range(NC):
                    dve.tensor_copy(f_x[0:64, c, :].rearrange("p (b t) -> p b t", b=2),
                                    h1_b[0:64, 2 * c:2 * c + 2, 1:HP]).then_inc(s["f_shifted"], 1)
                dve.wait_ge(s["f_shifted"], 2 * NC * layer + 2 * NC)
                dve.wait_ge(s["w_f_loaded"], 64 * layer + 64)
                ln_vector(dve, f_x, layer + 2)
                for c in range(NC):
                    dve.wait_ge(s["ln_normed"], NC * layer + 2 * NC + c + 1)
                    dve.tensor_scalar(f_xn[:, c, :], f_xc[:, c, :], par[:, L_G:L_G + 1], par[:, L_B:L_B + 1],
                                      ALU.mult, ALU.add).then_inc(s["ln_scaled"], 1)
                for c in range(NC):
                    n = NC * layer + c
                    for i, (at, size) in enumerate(HT):
                        dve.wait_ge(s["f_gated"], 3 * n + i + 1)
                        dve.wait_ge(s["f_up"], 6 * n + 3 + i + 1)
                        dve.wait_ge(s["f_down"], n)
                        dve.scalar_tensor_tensor(f_a[0:size, i, :], ps[0:size, i, :],
                                                 par[0:size, L_BA + i:L_BA + i + 1], f_g[0:size, i, :],
                                                 ALU.add, ALU.mult).then_inc(s["f_prod"], 1)
                    dve.wait_ge(s["f_down"], n + 1)
                    v = h1_b[:, 2 * c:2 * c + 2, 1:HP]
                    dve.scalar_tensor_tensor(h0_b[:, 2 * c:2 * c + 2, 1:HP], ps[:, 6 + c % 2, :].rearrange("p (b t) -> p b t", b=2),
                                             par[:, L_B2:L_B2 + 1], v, ALU.add, ALU.add)\
                       .then_inc(s["f_done"], 1)
            dve.wait_ge(s["f_done"], NC * DEPTH)
            for b in range(B):
                dve.scalar_tensor_tensor(x1[:, N * b:N * b + N], h0[:, HP * b + 1:HP * b + HP],
                                         gate[:, 1, b:b + 1], x1[:, N * b:N * b + N], ALU.mult, ALU.add)\
                   .then_inc(s["final_done"], 1)


def constants():
    import numpy as np

    f = np.float32
    c = np.zeros((P, C_END), f)
    c[:, C_ID:C_ID + P] = np.eye(P, dtype=f)
    c[:, C_MEAN:C_MEAN + P] = f(1 / 128)
    i = np.arange(P)
    c[:, C_SUM2:C_SUM2 + P] = (i[:, None] // 32 == i[None] // 32) & (i[:, None] % 16 == i[None] % 16)
    key = 64 * (i // 64)[:, None] - W + np.arange(SPAN)[None]
    for m in range(U):
        seen = (key <= i[:, None]) & (key >= i[:, None] - W) & (key + P * m >= 0)
        c[:, C_MASK + SPAN * m:C_MASK + SPAN * (m + 1)] = np.where(seen, f(0), f(NEG))
    half = np.arange(0, D, 2, dtype=f)
    inv = f(1) / f(10000.0) ** (half / f(D))
    t = np.arange(N, dtype=f)
    freqs = (t[:, None] * inv[None]).astype(f)
    base = (half + f(0.4 * D)) / f(1.4 * D)
    power = (t - f(N // 2)) / f(W // 2)
    scale = (base[None] ** power[:, None]).astype(f)
    cos, sin = np.cos(freqs), np.sin(freqs)
    for m in range(U):
        r = slice(P * m, P * m + P)
        for k, (a, x) in enumerate(((8 * cos * scale, 1), (8 * sin * scale, -1), (cos / scale, 1), (sin / scale, -1))):
            at = C_ROPE + D * (4 * m + k)
            c[:, at:at + D] = np.concatenate([x * a[r], a[r]], -1)
    inv1 = f(1) / f(10000.0) ** (np.arange(0, AD, 2, dtype=f) / f(AD))
    fr = np.repeat((np.arange(N, dtype=f)[:, None] * inv1[None]).astype(f), 2, -1)
    sign = np.where(np.arange(AD) % 2 == 0, f(-1), f(1))
    both = np.concatenate([np.cos(fr), np.sin(fr) * sign], -1).reshape(AT, AG, 2 * AD)
    c[:, C_ROPE1:] = np.tile(both.transpose(2, 1, 0).reshape(2 * AD, AG * AT), (4, 1))
    return c


def kernel(**inputs):
    import numpy as np
    import concourse.bacc as bacc
    from concourse.bass_utils import run_bass_kernel_spmd

    x = {k: np.asarray(v) for k, v in inputs.items()}
    f = "L0_ffn_"

    def stacked(w):
        w = w.reshape(AG, AD // 2, 2, E)
        return np.stack([w, w[:, :, ::-1]], 1).reshape(AG * 2 * AD, E).T

    def tiles(b):
        return np.pad(b, ((0, 0), (0, 3 * P - HID))).reshape(DEPTH, 3, P).transpose(0, 2, 1)

    q, k = x[f + "q_scale"], x[f + "k_scale"]
    b1 = x[f + "b1"]
    arrays = {
        "xT": x["L0_attn_emb"].reshape(T, E).T,
        "w1s": stacked(x["L0_attn_W1"]).reshape(E, AG, 2 * AD),
        "w2s": stacked(x["L0_attn_W2"]).reshape(E, AG, 2 * AD),
        "w3T": x["L0_attn_W3"].T,
        "woT": x["L0_attn_Wo"].T.reshape(16, AG, E).transpose(1, 0, 2).reshape(P, E),
        "cT": x["L0_c"].T,
        "wmod": x["L0_wmod"],
        "wqkv": x[f + "Wqkv"],
        "scales": np.stack([q, np.roll(q, D // 2, 1), k, np.roll(k, D // 2, 1)], 1),
        "wo": x[f + "Wo"],
        "params": np.concatenate([x[f + "ln_g"][:, :, None], x[f + "ln_b"][:, :, None], x[f + "b2"][:, :, None],
                                  tiles(b1[:, :HID]), tiles(b1[:, HID:])], 2),
        "w1": x[f + "W1"],
        "w2": x[f + "W2"],
        "consts": constants(),
    }
    arrays = {n: np.ascontiguousarray(a) for n, a in arrays.items()}
    nc = bacc.Bacc("TRN2", target_bir_lowering=False, num_devices=1)
    args = [nc.dram_tensor(n, a.shape, mybir.dt.from_np(a.dtype), kind="ExternalInput").ap()
            for n, a in arrays.items()]
    out = nc.dram_tensor("out", (E, T), F32, kind="ExternalOutput").ap()
    build(nc, *args, out)
    r = run_bass_kernel_spmd(nc, [arrays], core_ids=[0])
    return np.ascontiguousarray(r.results[0]["out"].T.reshape(B, N, E))
```

```python
from contextlib import ExitStack

import concourse.bass as bass
from concourse import mybir

ACT = mybir.ActivationFunctionType
ALU = mybir.AluOpType
AX = mybir.AxisListType
F32 = mybir.dt.float32
BF16 = mybir.dt.bfloat16

P = 128
B, N, E = 8, 256, 128
T = B * N
DEPTH = 6
AH, AD = 8, 16
AG = E // AD
AW = 32
AT = N // AH
H, D = 16, 64
INNER = H * D
W = 32
SPAN = 96
U = N // P
HC = H // 2
VD = D + 1
ON = 66
OW = 96
HID = 341
HT = [(0, 128), (128, 128), (256, HID - 256)]
CH = 512
NC = T // CH
HP = N + 1
NEG = -1e30
CREDIT = 4

C_ID, C_MEAN, C_SUM2, C_MASK, C_ROPE, C_ROPE1 = 0, 128, 256, 384, 384 + 2 * SPAN, 384 + 2 * SPAN + 2 * 4 * D
C_END = C_ROPE1 + AG * AT
L_G, L_B, L_B2, L_BA, L_BG, L_END = 0, 1, 2, 3, 6, 9


def build(nc, xT, w1s, w2s, w3T, woT, cT, wmod, wqkv, scales, wo, params, w1, w2, consts, out):
    with ExitStack() as ctx:
        def sb(name, shape, dt=F32):
            return ctx.enter_context(nc.sbuf_tensor(name, shape, dt))

        def sem(name):
            return ctx.enter_context(nc.semaphore(name))

        cst = sb("cst", [P, C_END])
        ident = cst[:, C_ID:C_ID + P]
        mean_w = cst[:, C_MEAN:C_MEAN + P]
        sum2_w = cst[:, C_SUM2:C_SUM2 + P]
        ident_bf = sb("ident_bf", [P, P], BF16)
        mask_bf = sb("mask_bf", [P, U, 4, SPAN], BF16)
        x1 = sb("x1", [P, T])
        h0 = sb("h0", [P, B * HP])
        h1 = sb("h1", [P, B * HP])
        mod = sb("mod", [P, 6, B])
        gate = sb("gate", [P, 2, B])
        wqkv_sb = sb("wqkv_sb", [P, 3 * INNER])
        wo_sb = sb("wo_sb", [P, INNER // P, E])
        w1_sb = sb("w1_sb", [P, 2 * HID])
        w2_sb = sb("w2_sb", [P, 3, E])
        par = sb("par", [P, L_END])
        scl = sb("scl", [P, 4, D])
        rope = sb("rope", [P, U, 4, D])
        k_t = sb("k_t", [P, U, H // 2, 2, SPAN])
        v_sb = sb("v_sb", [P, U, 2, H * VD + OW - VD])
        x_u = sb("x_u", [P, U, P])
        norm2 = sb("norm2", [P, 2 * H])
        norml = sb("norml", [P, 2 * H])
        rnorm = sb("rnorm", [P, 2 * H])
        rmax = sb("rmax", [P, H])
        rden = sb("rden", [P, H])
        f_x = sb("f_x", [P, 2, CH])
        f_sq = sb("f_sq", [P, 2, CH])
        f_xn = sb("f_xn", [P, NC, CH])
        arena = sb("arena", [P, 15 * 1024])

        def take(at, *shape):
            n = 1
            for s in shape:
                n *= s
            assert at + n <= 15 * 1024
            v = arena[:, at:at + n]
            if len(shape) == 2:
                v = v.rearrange("p (a b) -> p a b", a=shape[0])
            elif len(shape) == 3:
                v = v.rearrange("p (a b c) -> p a b c", a=shape[0], b=shape[1])
            return v

        t_cos = take(0, 2, INNER)
        t_sin = take(2048, 2, INNER)
        sq = take(4096, 2, INNER)
        q_t = take(6144, H // 2, P)
        s_sb = take(7168, 2, HC, SPAN)
        p_t = take(8704, H, P)
        o_n = take(11264, INNER)
        o_t = take(12288, H // 2, P)
        f_g = take(7168, 3, CH)
        f_a = take(8704, 3, CH)
        ln_xc = take(2048, NC, CH)
        ln_sq = take(4096, NC, CH)
        ln_r = take(6144, NC, CH)
        a_h = take(0, T)
        a_q = take(2048, AG, T // 4)
        a_k = take(6144, AG, T // 4)
        a_w1 = take(11264, AG, 2 * AD)
        a_w2 = take(11520, AG, 2 * AD)
        a_w3 = take(11776, E)
        a_wo = take(11904, E)
        a_cT = take(12032, B)
        a_sil = take(12040, B)
        a_wm = take(12288, 6 * E)
        a_v = sb("a_v", [P, 4, 2 * AH, 2, AW])
        a_qs = sb("a_qs", [P, 2, 2, P])
        a_ks = sb("a_ks", [P, 2, N])
        a_vs = sb("a_vs", [P, 2, 4, 2, AW])
        a_p = wqkv_sb[:, 0:2048].rearrange("p (a b) -> p a b", a=8)
        a_pt = h1[:, 0:2048].rearrange("p (a b c) -> p a b c", a=8, b=2)
        a_of = sb("a_of", [P, 2, P])
        a_o = sb("a_o", [P, 4, 2, 2, AH, AD])
        a_o_i = a_o[:, :, :, :, :, :].rearrange("p j c b h d -> p j c (b h) d")
        a_max = sb("a_max", [P, 8])
        a_nmax = sb("a_nmax", [P, 8])
        a_rden = sb("a_rden", [P, 2, 4])

        ps = ctx.enter_context(nc.psum_tensor("ps", [P, 8, 512], F32))

        def pair_of_banks(g):
            return ps[:, 2 * g:2 * g + 2, :]

        names = """
        const_loaded x_loaded a_loaded mod_loaded w_a_loaded w_f_loaded w_q_loaded zeroed bf_ready
        silu_e silu_1 silu_r silu_ready mod_mm mod_ready gate_abs gate_sign
        ln_mean ln_centred ln_squared ln_var ln_log ln_rstd ln_normed ln_scaled
        a_zeroed a_v_mm a_v_ready a_proj a_roped a_summed a_k_ready a_staged a_v_staged a_scored a_maxed a_negated a_exped
        a_turned a_pt_ready a_pv a_o_copied a_o_turned a_recip a_o_ready a_out_mm x1_ready h0_ready
        f_lower f_upper f_mean f_centred f_squared f_var f_log f_rstd f_normed f_scaled
        f_gate_up f_value_up f_gated f_prod f_down f_done
        rope_ready x_staged q_proj k_proj v_proj squared roped normed guarded logged inverted
        rope_added q_scaled k_scaled q_turned k_turned q_copied k_copied v_copied
        scored maxed centred exped p_turned p_copied attended recip o_normed
        o_turned o_copied projected att_done final_done stored
        """.split()
        s = {n: sem(n) for n in names}

        def ln_tensor(pe, src, ready, k):
            for c in range(NC):
                ready(pe, c)
                pe.matmul(ps[:, c, :], mean_w, src[:, c, :], start=True, stop=True).then_inc(s["ln_mean"], 1)
            for c in range(NC):
                pe.wait_ge(s["ln_squared"], NC * k + c + 1)
                pe.matmul(ps[:, 4 + c, :], mean_w, ln_sq[:, c, :], start=True, stop=True).then_inc(s["ln_var"], 1)

        def ln_vector(dve, src, k):
            for c in range(NC):
                dve.wait_ge(s["ln_mean"], NC * k + c + 1)
                dve.tensor_tensor(ln_xc[:, c, :], src[:, c, :], ps[:, c, :], ALU.subtract)\
                   .then_inc(s["ln_centred"], 1)
            for c in range(NC):
                dve.wait_ge(s["ln_rstd"], NC * k + c + 1)
                dve.wait_ge(s["ln_centred"], NC * k + c + 1)
                dve.tensor_tensor(ln_xc[:, c, :], ln_xc[:, c, :], ln_r[:, c, :], ALU.mult)\
                   .then_inc(s["ln_normed"], 1)

        def ln_scalar(act, k):
            for c in range(NC):
                act.wait_ge(s["ln_centred"], NC * k + c + 1)
                act.activation(ln_sq[:, c, :], ln_xc[:, c, :], ACT.Square).then_inc(s["ln_squared"], 1)
            for c in range(NC):
                act.wait_ge(s["ln_var"], NC * k + c + 1)
                act.activation(ln_r[:, c, :], ps[:, 4 + c, :], ACT.Ln, bias=1e-5).then_inc(s["ln_log"], 1)
                act.wait_ge(s["ln_log"], NC * k + c + 1)
                act.activation(ln_r[:, c, :], ln_r[:, c, :], ACT.Exp, scale=-0.5).then_inc(s["ln_rstd"], 1)

        x1_c = x1[:, :].rearrange("p (c t) -> p c t", c=NC)

        credited = """
        f_lower f_upper f_mean f_centred f_squared f_var f_log f_rstd f_normed f_scaled
        f_gate_up f_value_up f_gated f_prod f_down f_done
        rope_ready x_staged q_proj k_proj v_proj squared roped normed guarded logged inverted
        rope_added q_scaled k_scaled q_turned k_turned q_copied k_copied v_copied
        scored maxed centred exped p_turned p_copied attended recip o_normed
        o_turned o_copied projected att_done
        a_scored a_exped a_pt_ready a_o_ready a_pv a_turned
        """.split()

        h0_b = h0[:, :].rearrange("p (b t) -> p b t", b=B)
        h1_b = h1[:, :].rearrange("p (b t) -> p b t", b=B)

        def snap(engine, value):
            return value if isinstance(value, int) else engine.snap(value)

        block = ctx.enter_context(nc.Block())

        @block.sync
        def _(sp):
            sp.dma_start(cst[:, :], consts).then_inc(s["const_loaded"], 16)
            sp.dma_start(x1[:, :], xT).then_inc(s["x_loaded"], 16)
            sp.dma_start(a_cT, cT).then_inc(s["mod_loaded"], 16)
            sp.dma_start(a_wm, wmod).then_inc(s["mod_loaded"], 16)
            sp.dma_start(a_w1, w1s).then_inc(s["a_loaded"], 16)
            sp.dma_start(a_w2, w2s).then_inc(s["a_loaded"], 16)
            sp.dma_start(a_w3, w3T).then_inc(s["a_loaded"], 16)
            sp.dma_start(a_wo, woT).then_inc(s["a_loaded"], 16)
            sp.wait_ge(s["a_turned"], CREDIT + 32)
            with sp.Fori(0, DEPTH) as layer:
                sp.wait_ge(s["v_proj"], CREDIT + 16 * layer)
                sp.dma_start(wqkv_sb[:, :], wqkv[layer, :, :]).then_inc(s["w_q_loaded"], 16)
                sp.wait_ge(s["rope_ready"], CREDIT + layer)
                sp.dma_start(scl[:, :, :], scales[layer, :, :].unsqueeze(0).to_broadcast([P, 4, D]))\
                  .then_inc(s["w_q_loaded"], 16)
                sp.wait_ge(s["projected"], CREDIT + 16 * layer)
                sp.dma_start(wo_sb[:, :, :], wo[layer, :, :].rearrange("(c p) e -> p c e", p=P))\
                  .then_inc(s["w_a_loaded"], 16)
                sp.wait_ge(s["f_done"], CREDIT + NC * layer)
                sp.dma_start(w1_sb[:, :], w1[layer, :, :]).then_inc(s["w_f_loaded"], 16)
                sp.dma_start(w2_sb[:, 0:2, :], w2[layer, 0:256, :].rearrange("(c p) e -> p c e", p=P))\
                  .then_inc(s["w_f_loaded"], 16)
                sp.dma_start(w2_sb[0:HT[2][1], 2, :], w2[layer, 256:HID, :]).then_inc(s["w_f_loaded"], 16)
                sp.dma_start(par[:, :], params[layer, :, :]).then_inc(s["w_f_loaded"], 16)
            for c in range(NC):
                sp.wait_ge(s["final_done"], 2 * c + 2)
                sp.dma_start(out[:, CH * c:CH * c + CH], x1[:, CH * c:CH * c + CH]).then_inc(s["stored"], 16)
            sp.wait_ge(s["stored"], 16 * NC)

        @block.gpsimd
        def _(pool):
            pool.memset(a_v[:, :, :, :, :], 1.0).then_inc(s["a_zeroed"], 1)
            pool.memset(h0[:, :], 0.0).then_inc(s["zeroed"], 1)
            pool.memset(v_sb[:, :, :, :], 1.0).then_inc(s["zeroed"], 1)
            pool.memset(k_t[:, :, :, :, :], 0.0).then_inc(s["zeroed"], 1)

            def rotate(pair, m):
                n = 2 * pair + m
                for j in range(2):
                    pool.wait_ge(s["roped"], CREDIT + 4 * n + 2 * j + 2)
                    pool.tensor_tensor(t_cos[:, j, :], t_cos[:, j, :], t_sin[:, j, :], ALU.add)\
                        .then_inc(s["rope_added"], 1)
                pool.wait_ge(s["inverted"], CREDIT + n + 1)
                pool.wait_ge(s["rope_added"], CREDIT + 2 * n + 2)
                k = t_cos[:, 1, :].rearrange("p (h d) -> p h d", h=H)
                pool.tensor_tensor(k, k, rnorm[:, H:2 * H].unsqueeze(2).to_broadcast([P, H, D]), ALU.mult)\
                    .then_inc(s["k_scaled"], 1)

            def tables(layer):
                pool.wait_ge(s["w_q_loaded"], 32 * layer + 32)
                pool.wait_ge(s["rope_added"], CREDIT + 32 * layer)
                for m in range(U):
                    pool.tensor_tensor(rope[:, m, :, :],
                                       cst[:, C_ROPE + 4 * D * m:C_ROPE + 4 * D * (m + 1)]
                                       .rearrange("p (k d) -> p k d", k=4), scl[:, :, :], ALU.mult)
                pool.drain().then_inc(s["rope_ready"], 1)

            def layer_body(layer, more):
                first = snap(pool, layer * B)
                with pool.Fori(0, B - 1) as b:
                    pair = pool.snap(first + b)
                    rotate(pair, 1)
                    rotate(pair + 1, 0)
                rotate(first + (B - 1), 1)
                if more:
                    tables(layer + 1)
                    rotate(first + B, 0)

            tables(0)
            rotate(0, 0)
            with pool.Fori(0, DEPTH - 1) as layer:
                layer_body(layer, True)
            layer_body(DEPTH - 1, False)

        @block.tensor
        def _(pe):
            pe.wait_ge(s["mod_loaded"], 32)
            pe.wait_ge(s["silu_ready"], 1)
            for k in range(6):
                mm = pe.matmul(ps[:, 7, B * k:B * k + B], a_wm[:, E * k:E * k + E], a_sil, start=True, stop=True)
            mm.then_inc(s["mod_mm"], 1)
            pe.wait_ge(s["mod_ready"], 1)
            pe.wait_ge(s["const_loaded"], 16)

            def x_ready(pe, c):
                pe.wait_ge(s["x_loaded"], 16)

            ln_tensor(pe, x1_c, x_ready, 0)
            pe.wait_ge(s["ln_scaled"], B)
            pe.wait_ge(s["a_loaded"], 64)
            for u in range(T // P):
                mm = pe.matmul(ps[:, 4 + u // 4, P * (u % 4):][:, 0:P], a_h[:, P * u:P * u + P], a_w3,
                               start=True, stop=True)
            mm.then_inc(s["a_v_mm"], 1)
            for n, w in enumerate((a_w1, a_w2)):
                for g in range(AG):
                    i = n * AG + g
                    if i >= 4:
                        pe.wait_ge(s["a_roped"], i - 3)
                    for j in range(4):
                        mm = pe.matmul(ps[32 * j:32 * j + 32, i % 4, :], w[:, g, :],
                                       a_h[:, CH * j:CH * j + CH], start=True, stop=True)
                    mm.then_inc(s["a_proj"], 1)
            for g in range(AG):
                pe.wait_ge(s["a_roped"], AG + g + 1)
                if g >= 2:
                    pe.wait_ge(s["a_k_ready"], g - 1)
                if g == 0:
                    pe.wait_ge(s["a_v_ready"], 16)
                pe.matmul(ps[:, 4 + g % 2, :], sum2_w, a_k[:, g, :], start=True, stop=True)\
                    .then_inc(s["a_summed"], 1)
            pe.wait_ge(s["a_k_ready"], AG)
            pe.wait_ge(s["a_roped"], 2 * AG)

            def a_scores(i, k, half):
                pe.wait_ge(s["a_staged"], 2 * i + 2)
                pe.wait_ge(s["a_exped"], CREDIT + 8 * i - 4 + 4 * half)
                for q in range(4):
                    j, c = 2 * half + q % 2, q // 2
                    mm = pe.matmul(ps[:, j, N * c:N * c + N], a_qs[32 * j:32 * j + 32, k, c, :],
                                   a_ks[32 * j:32 * j + 32, k, :], start=True, stop=True,
                                   tile_position=(32 * j, 0))
                mm.then_inc(s["a_scored"], 1)

            def a_turn(i, half):
                pe.wait_ge(s["a_exped"], CREDIT + 8 * i + 4 * half + 4)
                pe.wait_ge(s["a_pt_ready"], CREDIT + 2 * i + half)
                for q in range(4):
                    for kh in range(2):
                        mm = pe.transpose(ps[:, 4 + q // 2, P * (2 * (q % 2) + kh):][:, 0:P],
                                          a_p[:, 4 * half + q, P * kh:P * kh + P], ident)
                mm.then_inc(s["a_turned"], 1)

            def a_attend(i, k):
                pe.wait_ge(s["a_pt_ready"], CREDIT + 2 * i + 2)
                pe.wait_ge(s["a_v_staged"], i + 1)
                if not (isinstance(i, int) and i == 0):
                    pe.wait_ge(s["a_o_copied"], i)
                for c in range(2):
                    for kh in range(2):
                        for j in range(4):
                            mm = pe.matmul(ps[32 * j:32 * j + 32, 6, P * c:P * c + P], a_vs[:, k, j, kh, :],
                                           a_pt[:, 2 * j + c, kh, :], start=(kh == 0), stop=(kh == 1),
                                           tile_position=(0, 32 * j), skip_group_check=True)
                mm.then_inc(s["a_pv"], 1)

            def a_turn_o(i):
                pe.wait_ge(s["a_o_copied"], i + 1)
                pe.wait_ge(s["a_o_ready"], CREDIT + i)
                for c in range(2):
                    mm = pe.transpose(ps[:, 7, P * c:P * c + P], a_of[:, c, :], ident)
                mm.then_inc(s["a_o_turned"], 1)

            def a_step(i, k, before=True, more=True):
                a_turn(i, 0)
                if more:
                    a_scores(i + 1, 1 - k, 0)
                a_turn(i, 1)
                if more:
                    a_scores(i + 1, 1 - k, 1)
                if before:
                    a_turn_o(i - 1)
                a_attend(i, k)

            a_scores(0, 0, 0)
            a_scores(0, 0, 1)
            a_step(0, 0, before=False)
            a_step(1, 1)
            with pe.Fori(1, AH - 1) as two:
                a_step(pe.snap(2 * two), 0)
                a_step(pe.snap(2 * two + 1), 1)
            a_step(2 * AH - 2, 0)
            a_step(2 * AH - 1, 1, more=False)
            a_turn_o(2 * AH - 1)
            pe.wait_ge(s["a_o_ready"], CREDIT + 2 * AH)
            for b in range(B):
                for c in range(2):
                    mm = pe.matmul(ps[:, b // 2, N * (b % 2) + P * c:][:, 0:P],
                                   a_o[:, b // 2, c, b % 2, :, :].rearrange("p h d -> p (h d)"), a_wo,
                                   start=True, stop=True)
                if b % 2:
                    mm.then_inc(s["a_out_mm"], 1)

            def x1_chunk(pe, c):
                pe.wait_ge(s["x1_ready"], B)

            ln_tensor(pe, x1_c, x1_chunk, 1)

            def q_k(pair, m):
                n = 2 * pair + m
                pe.wait_ge(s["x_staged"], CREDIT + 2 * n + 2)
                for j, done in ((0, "q_proj"), (1, "k_proj")):
                    if j == 0:
                        pe.wait_ge(s["q_copied"], CREDIT + n)
                    else:
                        pe.wait_ge(s["k_copied"], CREDIT + 5 * pair + 3 * m)
                    for c in range(2):
                        mm = pe.matmul(ps[:, 2 * j + c, :], x_u[:, m, :],
                                       wqkv_sb[:, INNER * j + 512 * c:][:, 0:512], start=True, stop=True)
                    mm.then_inc(s[done], 1)

            def v(pair, m):
                n = 2 * pair + m
                pe.wait_ge(s["roped"], CREDIT + 4 * n + 2)
                pe.wait_ge(s["squared"], CREDIT + 2 * n + 2)
                for c in range(2):
                    mm = pe.matmul(ps[:, c, :], x_u[:, m, :], wqkv_sb[:, 2 * INNER + 512 * c:][:, 0:512],
                                   start=True, stop=True)
                mm.then_inc(s["v_proj"], 1)

            def turn_q_k(pair, m):
                n = 2 * pair + m
                for j, ready, done in ((0, "q_scaled", "q_turned"), (1, "k_scaled", "k_turned")):
                    pe.wait_ge(s[ready], CREDIT + n + 1)
                    if j == 0:
                        pe.wait_ge(s["v_copied"], CREDIT + 7 * pair + 4 + 3 * m)
                    else:
                        pe.wait_ge(s["roped"], CREDIT + 4 * n + 4)
                        pe.wait_ge(s["squared"], CREDIT + 2 * n + 2)
                    for c in range(H // 2):
                        mm = pe.transpose(ps[:, 2 * j + c // 4, P * (c % 4):][:, 0:P],
                                          t_cos[:, j, P * c:P * c + P], ident)
                    mm.then_inc(s[done], 1)

            def scores(pair, m):
                n = 2 * pair + m
                pe.wait_ge(s["q_copied"], CREDIT + n + 1)
                pe.wait_ge(s["k_copied"], CREDIT + 5 * pair + 3 + 2 * m)
                for g in range(2):
                    if g == 0:
                        pe.wait_ge(s["o_copied"], CREDIT + n)
                    else:
                        pe.wait_ge(s["att_done"], CREDIT + n)
                    for c in range(2):
                        pe.matmul(ps[:, 4 + 2 * g + c, 0:4 * SPAN], ident_bf[:, :],
                                  mask_bf[:, m, :, :].rearrange("p a b -> p (a b)"),
                                  start=True, stop=False, skip_group_check=True)
                        for hh in range(4):
                            h = HC * g + 2 * hh + c
                            r = D * c
                            for j in range(2):
                                mm = pe.matmul(ps[64 * j:64 * j + 64, 4 + 2 * g + c, SPAN * hh:SPAN * hh + SPAN],
                                               q_t[r:r + D, h // 2, 64 * j:64 * j + 64],
                                               k_t[r:r + D, m, h // 2, j, :],
                                               start=False, stop=(hh == 3), skip_group_check=True,
                                               tile_position=(r, 64 * j))
                    mm.then_inc(s["scored"], 1)

            def turn_p(pair, m):
                n = 2 * pair + m
                for g in range(2):
                    pe.wait_ge(s["exped"], CREDIT + 2 * n + g + 1)
                    pe.wait_ge(s["centred"], CREDIT + 2 * n + g + 1)
                    for hh in range(HC):
                        mm = pe.transpose(ps[0:SPAN, 4 + 2 * g + hh // 4, P * (hh % 4):][:, 0:P],
                                          s_sb[:, g, hh, :], ident)
                    mm.then_inc(s["p_turned"], 1)

            def attend(pair, m):
                n = 2 * pair + m
                pe.wait_ge(s["v_copied"], CREDIT + 7 * pair + 3 + 4 * m)
                for g in range(2):
                    pe.wait_ge(s["p_copied"], CREDIT + 2 * n + g + 1)
                    for hh in range(HC):
                        h = HC * g + hh
                        for j in range(2):
                            mm = pe.matmul(ps[64 * j:64 * j + 64, 4 + 2 * g + hh // 4, OW * (hh % 4):][:, 0:ON],
                                           p_t[0:SPAN, h, 64 * j:64 * j + 64],
                                           v_sb[0:SPAN, m, j, VD * h:VD * h + ON], start=True,
                                           stop=True, skip_group_check=True, tile_position=(0, 64 * j))
                    mm.then_inc(s["attended"], 1)

            def project(pair, m):
                n = 2 * pair + m
                pe.wait_ge(s["o_normed"], CREDIT + 2 * n + 2)
                for c in range(H // 2):
                    mm = pe.transpose(ps[:, 4 + c // 4, P * (c % 4):][:, 0:P], o_n[:, P * c:P * c + P], ident)
                mm.then_inc(s["o_turned"], 1)

            def project_out(pair, m):
                n = 2 * pair + m
                pe.wait_ge(s["o_copied"], CREDIT + n + 1)
                for c in range(H // 2):
                    mm = pe.matmul(ps[:, 6, 0:P], wo_sb[:, c, :], o_t[:, c, :], start=(c == 0),
                                   stop=(c == H // 2 - 1))
                mm.then_inc(s["projected"], 1)

            def step(pair, m, after):
                scores(pair, m)
                if after:
                    q_k(*after)
                turn_p(pair, m)
                if after:
                    v(*after)
                attend(pair, m)
                project(pair, m)
                if after:
                    turn_q_k(*after)
                project_out(pair, m)

            def mean(layer, c):
                q = NC * layer + c
                pe.wait_ge(s["f_lower"], CREDIT + q + 1)
                pe.wait_ge(s["f_upper"], CREDIT + q + 1)
                pe.wait_ge(s["f_centred"], CREDIT + q - 1)
                pe.matmul(ps[:, c % 2, :], mean_w, f_x[:, c % 2, :], start=True, stop=True)\
                  .then_inc(s["f_mean"], 1)

            def variance(layer, c):
                q = NC * layer + c
                pe.wait_ge(s["f_squared"], CREDIT + q + 1)
                pe.wait_ge(s["f_log"], CREDIT + q - 1)
                pe.matmul(ps[:, 2 + c % 2, :], mean_w, f_sq[:, c % 2, :], start=True, stop=True)\
                  .then_inc(s["f_var"], 1)

            def last_step(layer, pair):
                scores(pair, 1)
                mean(layer, 0)
                mean(layer, 1)
                turn_p(pair, 1)
                variance(layer, 0)
                variance(layer, 1)
                attend(pair, 1)
                mean(layer, 2)
                project(pair, 1)
                variance(layer, 2)
                project_out(pair, 1)

            def feed_forward(layer, more):
                first = NC * layer

                def gate_up(c, i):
                    at, size = HT[i]
                    k = 3 * c + i
                    pe.wait_ge(s["f_gated"], CREDIT + 3 * first + k - 1)
                    pe.matmul(ps[0:size, 4 + k % 2, :], w1_sb[:, HID + at:HID + at + size], f_xn[:, c, :],
                              start=True, stop=True).then_inc(s["f_gate_up"], 1)

                def value_up(c, i):
                    at, size = HT[i]
                    pe.wait_ge(s["f_prod"], CREDIT + 3 * first + 3 * c + i)
                    pe.matmul(ps[0:size, 6, :], w1_sb[:, at:at + size], f_xn[:, c, :],
                              start=True, stop=True).then_inc(s["f_value_up"], 1)

                def down(c, i):
                    at, size = HT[i]
                    pe.wait_ge(s["f_prod"], CREDIT + 3 * first + 3 * c + i + 1)
                    if i == 0:
                        pe.wait_ge(s["f_done"], CREDIT + first + c)
                    mm = pe.matmul(ps[:, 7, :], w2_sb[0:size, i, :], f_a[0:size, i, :],
                                   start=(i == 0), stop=(i == 2))
                    if i == 2:
                        mm.then_inc(s["f_down"], 1)

                pe.wait_ge(s["w_f_loaded"], 64 * layer + 64)
                for c in range(NC):
                    if c == 3 and more:
                        pe.wait_ge(s["w_q_loaded"], 32 * layer + 64)
                        pe.wait_ge(s["w_a_loaded"], 16 * layer + 32)
                        pe.wait_ge(s["f_centred"], CREDIT + first + NC)
                        pe.wait_ge(s["f_log"], CREDIT + first + NC)
                        q_k(layer * B + B, 0)
                    pe.wait_ge(s["f_scaled"], CREDIT + first + c + 1)
                    gate_up(c, 0)
                    if c:
                        down(c - 1, 2)
                    else:
                        pe.wait_ge(s["att_done"], CREDIT + 16 * layer + 16)
                    value_up(c, 0)
                    gate_up(c, 1)
                    value_up(c, 1)
                    down(c, 0)
                    gate_up(c, 2)
                    value_up(c, 2)
                    down(c, 1)
                    if c == 0:
                        mean(layer, 3)
                    if c == 1:
                        variance(layer, 3)
                down(NC - 1, 2)
                if more:
                    v(layer * B + B, 0)
                    turn_q_k(layer * B + B, 0)

            def layer_body(layer, more):
                first = snap(pe, layer * B)
                with pe.Fori(0, B - 1) as b:
                    pair = pe.snap(first + b)
                    step(pair, 0, (pair, 1))
                    step(pair, 1, (pair + 1, 0))
                last = snap(pe, first + (B - 1))
                step(last, 0, (last, 1))
                last_step(layer, last)
                feed_forward(layer, more)

            pe.wait_ge(s["zeroed"], 3)
            pe.wait_ge(s["bf_ready"], 2)
            pe.wait_ge(s["h0_ready"], B)
            pe.wait_ge(s["w_q_loaded"], 32)
            pe.wait_ge(s["w_a_loaded"], 16)
            q_k(0, 0)
            v(0, 0)
            turn_q_k(0, 0)
            with pe.Fori(0, DEPTH - 1) as layer:
                layer_body(layer, True)
            layer_body(DEPTH - 1, False)

        @block.scalar
        def _(act):
            act.preload_act_table_set("natural_log_exp_and_others")
            act.wait_ge(s["mod_loaded"], 32)
            act.activation(a_sil, a_cT, ACT.Exp, scale=-1.0).then_inc(s["silu_e"], 1)
            act.wait_ge(s["mod_mm"], 1)
            act.activation(mod[:, :, :].rearrange("p k b -> p (k b)"), ps[:, 7, 0:6 * B], ACT.Copy)\
               .then_inc(s["mod_ready"], 1)
            ln_scalar(act, 0)
            act.wait_ge(s["a_v_mm"], 1)
            act.wait_ge(s["a_zeroed"], 1)
            for a in range(4):
                for r in range(4):
                    act.activation(a_v[32 * r:32 * r + 32, :, :, :, 0:AD]
                                   .rearrange("p j (u a) k d -> p (j u) a k d", a=4)[:, :, a, :, :],
                                   ps[32 * a:32 * a + 32, 4:8, :]
                                   .rearrange("p b (u k r d) -> p (b u) k r d", u=4, k=2, r=4)[:, :, :, r, :],
                                   ACT.Copy).then_inc(s["a_v_ready"], 1)
            for g in range(AG):
                act.wait_ge(s["a_summed"], g + 1)
                act.activation(a_k[:, g, :], ps[:, 4 + g % 2, :], ACT.Copy).then_inc(s["a_k_ready"], 1)

            def a_exps(i, half):
                act.wait_ge(s["a_negated"], 2 * i + half + 1)
                act.wait_ge(s["a_turned"], CREDIT + 2 * i - 1 + half)
                for q in range(4):
                    k = 4 * half + q
                    act.activation(a_p[:, k, :], ps[:, 2 * half + q // 2, N * (q % 2):][:, 0:N], ACT.Exp,
                                   bias=a_nmax[:, k:k + 1], scale=AH ** -0.5).then_inc(s["a_exped"], 1)

            def a_copy_p(i, half):
                act.wait_ge(s["a_turned"], CREDIT + 2 * i + half + 1)
                act.wait_ge(s["a_pv"], CREDIT + i)
                act.activation(a_pt[:, 4 * half:4 * half + 4, :, :].rearrange("p a b c -> p (a b c)"),
                               ps[:, 4:6, :].rearrange("p a b -> p (a b)"), ACT.Copy)\
                   .then_inc(s["a_pt_ready"], 1)

            def a_stage_v(i, k):
                act.wait_ge(s["a_pv"], CREDIT + i - 1)
                act.activation(a_vs[:, k, :, :, :].rearrange("p j k d -> p j (k d)"),
                               a_v[:, :, bass.ds(i, 1), :, :].rearrange("p j i k d -> p j (i k d)"), ACT.Copy)\
                   .then_inc(s["a_v_staged"], 1)

            def a_step(i, k, more=True):
                a_exps(i, 0)
                a_exps(i, 1)
                a_copy_p(i, 0)
                if more:
                    a_stage_v(i + 1, 1 - k)
                a_copy_p(i, 1)

            act.wait_ge(s["a_v_ready"], 16)
            a_stage_v(0, 0)
            a_step(0, 0)
            a_step(1, 1)
            with act.Fori(1, AH - 1) as two:
                a_step(act.snap(2 * two), 0)
                a_step(act.snap(2 * two + 1), 1)
            a_step(2 * AH - 2, 0)
            a_step(2 * AH - 1, 1, more=False)
            ln_scalar(act, 1)

            def squares(pair, m):
                n = 2 * pair + m
                act.wait_ge(s["k_proj"], CREDIT + n + 1)
                act.wait_ge(s["normed"], CREDIT + n)
                act.activation(sq[:, 1, :], pair_of_banks(1).rearrange("p a b -> p (a b)"),
                               ACT.Square).then_inc(s["squared"], 1)
                act.wait_ge(s["roped"], CREDIT + 4 * n + 2)
                act.activation(sq[:, 0, :], pair_of_banks(0).rearrange("p a b -> p (a b)"),
                               ACT.Square).then_inc(s["squared"], 1)

            def inverse_norms(pair, m):
                n = 2 * pair + m
                act.wait_ge(s["guarded"], CREDIT + n + 1)
                act.activation(norml[:, :], norm2[:, :], ACT.Ln, scale=2.0 ** 24).then_inc(s["logged"], 1)
                act.wait_ge(s["logged"], CREDIT + n + 1)
                act.wait_ge(s["q_scaled"], CREDIT + n)
                act.wait_ge(s["k_scaled"], CREDIT + n)
                act.activation(rnorm[:, :], norml[:, :], ACT.Exp, scale=-0.5, bias=8.317766166719343)\
                   .then_inc(s["inverted"], 1)

            def copy_q_k(pair, m):
                n = 2 * pair + m
                act.wait_ge(s["q_turned"], CREDIT + n + 1)
                act.wait_ge(s["scored"], CREDIT + 2 * n)
                act.activation(q_t.rearrange("p a b -> p (a b)"),
                               pair_of_banks(0).rearrange("p a b -> p (a b)"), ACT.Copy)\
                   .then_inc(s["q_copied"], 1)
                act.wait_ge(s["k_turned"], CREDIT + n + 1)
                src = pair_of_banks(1).rearrange("p a (b c) -> p (a b) c", b=4)
                act.activation(k_t[:, m, :, :, 0:64], src.rearrange("p b (j k) -> p b j k", j=2), ACT.Copy)\
                   .then_inc(s["k_copied"], 1)
                act.activation(k_t[:, m, :, 1, 64:SPAN], src[:, :, 32:64], ACT.Copy).then_inc(s["k_copied"], 1)
                if m == 0:
                    act.activation(k_t[:, 1, :, 0, 64:SPAN], src[:, :, P - W:P], ACT.Copy)\
                       .then_inc(s["k_copied"], 1)

            def copy_v(pair, m):
                n = 2 * pair + m
                act.wait_ge(s["v_proj"], CREDIT + n + 1)
                act.wait_ge(s["attended"], CREDIT + 4 * pair - 2 * (1 - m))

                def part(unit, half, rows, src):
                    dst = v_sb[rows[0]:rows[1], unit, half, 0:H * VD].rearrange("p (h d) -> p h d", h=H)[:, :, 0:D]
                    act.activation(dst, pair_of_banks(0)[src:src + rows[1] - rows[0]]
                                   .rearrange("p a (b c) -> p (a b) c", b=8), ACT.Copy).then_inc(s["v_copied"], 1)

                part(m, 0, (0, 64), 0)
                part(m, 1, (0, 64), 64)
                inverse_norms(pair, m)
                part(m, 1, (64, 96), 32)
                if m == 0:
                    act.wait_ge(s["attended"], CREDIT + 4 * pair)
                    part(1, 0, (64, 96), 96)

            def exps(pair, m):
                n = 2 * pair + m
                for g in range(2):
                    act.wait_ge(s["centred"], CREDIT + 2 * n + g + 1)
                    v = s_sb[:, g, :, :].rearrange("p h k -> p (h k)")
                    act.activation(v, v, ACT.Exp).then_inc(s["exped"], 1)

            def copy_p(pair, m):
                n = 2 * pair + m
                for g in range(2):
                    act.wait_ge(s["p_turned"], CREDIT + 2 * n + g + 1)
                    act.wait_ge(s["attended"], CREDIT + 2 * n)
                    act.activation(p_t[0:SPAN, HC * g:HC * g + HC, :].rearrange("p a b -> p (a b)"),
                                   pair_of_banks(2 + g)[0:SPAN].rearrange("p a b -> p (a b)"), ACT.Copy)\
                       .then_inc(s["p_copied"], 1)

            def copy_o(pair, m):
                n = 2 * pair + m
                act.wait_ge(s["o_turned"], CREDIT + n + 1)
                act.wait_ge(s["projected"], CREDIT + n)
                act.activation(o_t.rearrange("p a b -> p (a b)"),
                               pair_of_banks(2).rearrange("p a b -> p (a b)"), ACT.Copy)\
                   .then_inc(s["o_copied"], 1)

            def step(pair, m, after):
                exps(pair, m)
                if after:
                    squares(*after)
                copy_p(pair, m)
                if after:
                    copy_v(*after)
                copy_o(pair, m)
                if after:
                    copy_q_k(*after)

            def shift(layer, c):
                act.wait_ge(s["att_done"], CREDIT + 16 * layer + 4 * c + 4)
                act.wait_ge(s["f_centred"], CREDIT + NC * layer + c - 1)
                act.activation(f_x[64:128, c % 2, :].rearrange("p (b t) -> p b t", b=2),
                               h1_b[64:128, 2 * c:2 * c + 2, 0:N], ACT.Copy).then_inc(s["f_upper"], 1)

            def square(layer, c):
                q = NC * layer + c
                act.wait_ge(s["f_centred"], CREDIT + q + 1)
                act.wait_ge(s["f_normed"], CREDIT + q - 1)
                act.activation(f_sq[:, c % 2, :], f_xn[:, c, :], ACT.Square).then_inc(s["f_squared"], 1)

            def inverse_deviation(layer, c):
                q = NC * layer + c
                act.wait_ge(s["f_var"], CREDIT + q + 1)
                act.activation(f_sq[:, c % 2, :], ps[:, 2 + c % 2, :], ACT.Ln, bias=1e-5).then_inc(s["f_log"], 1)
                act.wait_ge(s["f_log"], CREDIT + q + 1)
                act.activation(f_sq[:, c % 2, :], f_sq[:, c % 2, :], ACT.Exp, scale=-0.5)\
                   .then_inc(s["f_rstd"], 1)

            def last_step(layer, pair):
                shift(layer, 0)
                shift(layer, 1)
                exps(pair, 1)
                square(layer, 0)
                square(layer, 1)
                copy_p(pair, 1)
                shift(layer, 2)
                inverse_deviation(layer, 0)
                inverse_deviation(layer, 1)
                copy_o(pair, 1)
                square(layer, 2)
                inverse_deviation(layer, 2)
                shift(layer, 3)

            def gates(layer, c):
                for i, (at, size) in enumerate(HT):
                    k = 3 * c + i
                    act.wait_ge(s["f_gate_up"], CREDIT + 3 * NC * layer + k + 1)
                    act.wait_ge(s["f_prod"], CREDIT + 3 * NC * layer + k - 2)
                    act.activation(f_g[0:size, i, :], ps[0:size, 4 + k % 2, :], ACT.Gelu,
                                   bias=par[0:size, L_BG + i:L_BG + i + 1]).then_inc(s["f_gated"], 1)

            def feed_forward(layer, more):
                act.wait_ge(s["attended"], CREDIT + 32 * layer + 32)
                gates(layer, 0)
                square(layer, 3)
                gates(layer, 1)
                act.preload_act_table_set("natural_log_exp_and_others")
                inverse_deviation(layer, 3)
                gates(layer, 2)
                if more:
                    squares(layer * B + B, 0)
                gates(layer, 3)
                if more:
                    act.preload_act_table_set("natural_log_exp_and_others")
                    copy_v(layer * B + B, 0)
                    copy_q_k(layer * B + B, 0)

            def layer_body(layer, more):
                first = snap(act, layer * B)
                with act.Fori(0, B - 1) as b:
                    pair = act.snap(first + b)
                    step(pair, 0, (pair, 1))
                    step(pair, 1, (pair + 1, 0))
                last = snap(act, first + (B - 1))
                step(last, 0, (last, 1))
                last_step(layer, last)
                feed_forward(layer, more)

            act.wait_ge(s["zeroed"], 3)
            act.preload_act_table_set("natural_log_exp_and_others")
            squares(0, 0)
            copy_v(0, 0)
            copy_q_k(0, 0)
            with act.Fori(0, DEPTH - 1) as layer:
                act.preload_act_table_set("natural_log_exp_and_others")
                layer_body(layer, True)
            act.preload_act_table_set("natural_log_exp_and_others")
            layer_body(DEPTH - 1, False)

        @block.vector
        def _(dve):
            for name in credited:
                dve.sem_inc(s[name], CREDIT)
            dve.wait_ge(s["silu_e"], 1)
            dve.tensor_scalar(a_sil, a_sil, 1.0, None, ALU.add).then_inc(s["silu_1"], 1)
            dve.wait_ge(s["silu_1"], 1)
            dve.reciprocal(a_sil, a_sil).then_inc(s["silu_r"], 1)
            dve.wait_ge(s["silu_r"], 1)
            dve.tensor_tensor(a_sil, a_sil, a_cT, ALU.mult).then_inc(s["silu_ready"], 1)
            dve.wait_ge(s["const_loaded"], 16)
            dve.tensor_copy(ident_bf[:, :], ident).then_inc(s["bf_ready"], 1)
            dve.tensor_copy(mask_bf[:, :, :, :],
                            cst[:, C_MASK:C_MASK + U * SPAN].rearrange("p (m k) -> p m k", m=U)
                            .unsqueeze(2).to_broadcast([P, U, 4, SPAN])).then_inc(s["bf_ready"], 1)
            dve.wait_ge(s["mod_ready"], 1)
            for n, k in enumerate((2, 5)):
                dve.tensor_scalar(gate[:, n, :], mod[:, k, :], 0.25, None, ALU.max).then_inc(s["gate_abs"], 1)
                dve.wait_ge(s["gate_abs"], 2 * n + 1)
                dve.scalar_tensor_tensor(gate[:, n, :], mod[:, k, :], -1.0, gate[:, n, :], ALU.mult, ALU.max)\
                   .then_inc(s["gate_abs"], 1)
                dve.tensor_scalar(mod[:, k, :], mod[:, k, :], 0.0, 2.0, ALU.is_ge, ALU.mult)\
                   .then_inc(s["gate_sign"], 1)
            dve.wait_ge(s["gate_sign"], 2)
            dve.wait_ge(s["gate_abs"], 4)
            for n, k in enumerate((2, 5)):
                dve.scalar_tensor_tensor(gate[:, n, :], mod[:, k, :], -1.0, gate[:, n, :], ALU.add, ALU.mult)\
                   .then_inc(s["gate_sign"], 1)
            for k in (1, 4):
                dve.tensor_scalar(mod[:, k, :], mod[:, k, :], 1.0, None, ALU.add).then_inc(s["gate_sign"], 1)
            dve.wait_ge(s["gate_sign"], 6)
            dve.wait_ge(s["x_loaded"], 16)
            ln_vector(dve, x1_c, 0)
            xc = ln_xc.rearrange("p c t -> p (c t)")
            for b in range(B):
                dve.wait_ge(s["ln_normed"], b // 2 + 1)
                dve.tensor_scalar(a_h[:, N * b:N * b + N], xc[:, N * b:N * b + N], mod[:, 1, b:b + 1],
                                  mod[:, 0, b:b + 1], ALU.mult, ALU.add).then_inc(s["ln_scaled"], 1)
            dve.wait_ge(s["ln_scaled"], B)
            tab = cst[:, C_ROPE1:C_ROPE1 + AG * AT].rearrange("p (g t) -> p g t", g=AG)
            for n, dst in enumerate((a_q, a_k)):
                for g in range(AG):
                    i = n * AG + g
                    dve.wait_ge(s["a_proj"], i + 1)
                    dve.tensor_tensor(dst[:, g, :].rearrange("p (i t) -> p i t", t=AT),
                                      ps[:, i % 4, :].rearrange("p (i t) -> p i t", t=AT),
                                      tab[:, g, :].unsqueeze(1).to_broadcast([P, CH // AT, AT]), ALU.mult)\
                       .then_inc(s["a_roped"], 1)
            def a_stage(i, k):
                if not isinstance(i, int) or i >= 2:
                    dve.wait_ge(s["a_scored"], CREDIT + 2 * i - 2)
                dve.tensor_copy(a_qs[:, k, :, :].rearrange("p c (g t) -> p c g t", g=AG),
                                a_q[:, :, bass.ds(AT * i, AT)].rearrange("p g (c t) -> p c g t", c=2))\
                   .then_inc(s["a_staged"], 1)
                dve.tensor_copy(a_ks[:, k, :].rearrange("p (g t) -> p g t", g=AG),
                                a_k[:, :, bass.ds(AT * i, AT)]).then_inc(s["a_staged"], 1)

            def a_maximum(i, half):
                dve.wait_ge(s["a_scored"], CREDIT + 2 * i + half + 1)
                mx = a_max[:, 4 * half:4 * half + 4]
                dve.tensor_reduce(mx, ps[:, 2 * half:2 * half + 2, :].rearrange("p a (b c) -> p (a b) c", b=2),
                                  AX.X, ALU.max).then_inc(s["a_maxed"], 1)
                dve.wait_ge(s["a_maxed"], 2 * i + half + 1)
                dve.wait_ge(s["a_exped"], CREDIT + 8 * i - 4 + 4 * half)
                dve.tensor_scalar(a_nmax[:, 4 * half:4 * half + 4], mx, -AH ** -0.5, None, ALU.mult)\
                   .then_inc(s["a_negated"], 1)

            def a_copy_o(i):
                dve.wait_ge(s["a_pv"], CREDIT + i + 1)
                dve.tensor_copy(a_of[:, :, :], ps[:, 6, 0:2 * P].rearrange("p (c q) -> p c q", c=2))\
                   .then_inc(s["a_o_copied"], 1)

            def a_normalise(i):
                dve.wait_ge(s["a_o_turned"], i + 1)
                o = ps[:, 7, 0:2 * P].rearrange("p (c j d) -> p c j d", c=2, j=4)
                dve.reciprocal(a_rden[:, :, :], o[:, :, :, AD]).then_inc(s["a_recip"], 1)
                dve.wait_ge(s["a_recip"], i + 1)
                dve.tensor_tensor(a_o_i[:, :, :, bass.ds(i, 1), :].rearrange("p j c i d -> p c j (i d)"),
                                  o[:, :, :, 0:AD], a_rden[:, :, :].unsqueeze(3).to_broadcast([P, 2, 4, AD]),
                                  ALU.mult).then_inc(s["a_o_ready"], 1)

            def a_step(i, k, before=True, more=True, stage=True):
                if more:
                    a_maximum(i + 1, 0)
                    a_maximum(i + 1, 1)
                if before:
                    a_normalise(i - 1)
                if stage:
                    a_stage(i + 2, k)
                a_copy_o(i)

            dve.wait_ge(s["a_roped"], 2 * AG)
            dve.wait_ge(s["a_k_ready"], AG)
            a_stage(0, 0)
            a_stage(1, 1)
            a_maximum(0, 0)
            a_maximum(0, 1)
            a_step(0, 0, before=False)
            a_step(1, 1)
            with dve.Fori(1, AH - 1) as two:
                a_step(dve.snap(2 * two), 0)
                a_step(dve.snap(2 * two + 1), 1)
            a_step(2 * AH - 2, 0, stage=False)
            a_step(2 * AH - 1, 1, more=False, stage=False)
            a_normalise(2 * AH - 1)
            for b in range(B):
                dve.wait_ge(s["a_out_mm"], b // 2 + 1)
                dve.scalar_tensor_tensor(x1[:, N * b:N * b + N], ps[:, b // 2, N * (b % 2):][:, 0:N],
                                         gate[:, 0, b:b + 1], x1[:, N * b:N * b + N], ALU.mult, ALU.add)\
                   .then_inc(s["x1_ready"], 1)
            dve.wait_ge(s["x1_ready"], B)
            ln_vector(dve, x1_c, 1)
            dve.wait_ge(s["zeroed"], 3)
            for b in range(B):
                dve.wait_ge(s["ln_normed"], NC + b // 2 + 1)
                dve.tensor_scalar(h0[:, HP * b + 1:HP * b + HP], xc[:, N * b:N * b + N], mod[:, 4, b:b + 1],
                                  mod[:, 3, b:b + 1], ALU.mult, ALU.add).then_inc(s["h0_ready"], 1)
                dve.sem_inc(s["ln_scaled"], 1)
            dve.wait_ge(s["a_pt_ready"], CREDIT + 4 * AH)
            dve.wait_ge(s["a_pv"], CREDIT + 2 * AH)
            dve.memset(h1[:, :], 0.0)
            dve.wait_ge(s["h0_ready"], B)

            def rope_products(pair, m):
                n = 2 * pair + m
                for j in range(2):
                    if j == 0:
                        dve.wait_ge(s["q_proj"], CREDIT + n + 1)
                    else:
                        dve.wait_ge(s["squared"], CREDIT + 2 * n + 1)
                    dve.wait_ge(s["q_turned" if j == 0 else "k_turned"], CREDIT + n)
                    src = pair_of_banks(j).rearrange("p a (h d) -> p (a h) d", h=8)
                    tc, ts = rope[:, m, 2 * j, :], rope[:, m, 2 * j + 1, :]
                    dve.tensor_tensor(t_cos[:, j, :].rearrange("p (h d) -> p h d", h=H), src,
                                      tc.unsqueeze(1).to_broadcast([P, H, D]), ALU.mult).then_inc(s["roped"], 1)
                    dve.tensor_tensor(t_sin[:, j, :].rearrange("p (h s d) -> p h s d", h=H, s=2),
                                      pair_of_banks(j).rearrange("p a (h s d) -> p (a h) s d", h=8, s=2)[:, :, ::-1, :],
                                      ts.rearrange("p (s d) -> p s d", s=2).unsqueeze(1)
                                      .to_broadcast([P, H, 2, D // 2]), ALU.mult).then_inc(s["roped"], 1)

            def norms(pair, m):
                n = 2 * pair + m
                dve.wait_ge(s["squared"], CREDIT + 2 * n + 2)
                dve.wait_ge(s["logged"], CREDIT + n)
                dve.tensor_reduce(norm2[:, :], sq.rearrange("p a (h d) -> p (a h) d", h=H), AX.X, ALU.add)\
                   .then_inc(s["normed"], 1)
                dve.wait_ge(s["normed"], CREDIT + n + 1)
                dve.tensor_scalar(norm2[:, :], norm2[:, :], 1e-24, None, ALU.max).then_inc(s["guarded"], 1)

            def centre(pair, m, g):
                n = 2 * pair + m
                dve.wait_ge(s["scored"], CREDIT + 2 * n + g + 1)
                src = pair_of_banks(2 + g)[:, :, 0:4 * SPAN].rearrange("p a (h k) -> p a h k", h=4)
                mx = rmax[:, HC * g:HC * g + HC].rearrange("p (h a) -> p a h", a=2)
                dve.tensor_reduce(mx, src, AX.X, ALU.max)\
                   .then_inc(s["maxed"], 1)
                dve.wait_ge(s["maxed"], CREDIT + 2 * n + g + 1)
                dve.wait_ge(s["p_turned"], CREDIT + 2 * n)
                dve.tensor_tensor(s_sb[:, g, :, :].rearrange("p (h a) k -> p a h k", a=2), src,
                                  mx.unsqueeze(3).to_broadcast([P, 2, 4, SPAN]), ALU.subtract).then_inc(s["centred"], 1)

            def normalise(pair, m, g):
                n = 2 * pair + m
                dve.wait_ge(s["attended"], CREDIT + 2 * n + g + 1)
                o = pair_of_banks(2 + g)[:, :, 0:4 * OW].rearrange("p a (h k) -> p a h k", h=4)
                rd = rden[:, HC * g:HC * g + HC].rearrange("p (a h) -> p a h", a=2)
                dve.reciprocal(rd, o[:, :, :, D]).then_inc(s["recip"], 1)
                dve.wait_ge(s["recip"], CREDIT + 2 * n + g + 1)
                dve.wait_ge(s["o_turned"], CREDIT + n)
                dve.tensor_tensor(o_n[:, HC * D * g:HC * D * (g + 1)]
                                  .rearrange("p (a h d) -> p a h d", a=2, h=4), o[:, :, :, 0:D],
                                  rd.unsqueeze(3).to_broadcast([P, 2, 4, D]), ALU.mult)\
                   .then_inc(s["o_normed"], 1)

            def residual(pair, b, m):
                n = 2 * pair + m
                col = b * HP + (1 + P * m)
                dve.wait_ge(s["projected"], CREDIT + n + 1)
                dve.tensor_tensor(h1[:, bass.ds(col, P)], ps[:, 6, 0:P], h0[:, bass.ds(col, P)], ALU.add)\
                   .then_inc(s["att_done"], 1)

            def stage(b, m):
                col = b * HP + P * m
                dve.tensor_scalar(x_u[0:64, m, :], h0[0:64, bass.ds(col + 1, P)], 1.0, None, ALU.mult)\
                   .then_inc(s["x_staged"], 1)
                dve.tensor_scalar(x_u[64:128, m, :], h0[64:128, bass.ds(col, P)], 1.0, None, ALU.mult)\
                   .then_inc(s["x_staged"], 1)

            def scale_q(pair, m):
                n = 2 * pair + m
                dve.wait_ge(s["inverted"], CREDIT + n + 1)
                dve.wait_ge(s["rope_added"], CREDIT + 2 * n + 1)
                q = t_cos[:, 0, :].rearrange("p (h d) -> p h d", h=H)
                dve.tensor_tensor(q, q, rnorm[:, 0:H].unsqueeze(2).to_broadcast([P, H, D]), ALU.mult)\
                   .then_inc(s["q_scaled"], 1)

            def step(pair, b, m, after, ahead=None):
                centre(pair, m, 0)
                centre(pair, m, 1)
                if after:
                    rope_products(*after)
                    norms(*after)
                if ahead:
                    dve.wait_ge(s["v_proj"], CREDIT + 2 * pair + m + 1)
                    stage(b + 1, m)
                normalise(pair, m, 0)
                normalise(pair, m, 1)
                if after:
                    scale_q(*after)
                residual(pair, b, m)

            def shift(layer, c):
                q = NC * layer + c
                dve.wait_ge(s["att_done"], CREDIT + 16 * layer + 4 * c + 4)
                dve.wait_ge(s["f_centred"], CREDIT + q - 1)
                dve.tensor_copy(f_x[0:64, c % 2, :].rearrange("p (b t) -> p b t", b=2),
                                h1_b[0:64, 2 * c:2 * c + 2, 1:HP]).then_inc(s["f_lower"], 1)

            def subtract_mean(layer, c):
                dve.wait_ge(s["f_mean"], CREDIT + NC * layer + c + 1)
                dve.tensor_tensor(f_xn[:, c, :], f_x[:, c % 2, :], ps[:, c % 2, :], ALU.subtract)\
                   .then_inc(s["f_centred"], 1)

            def divide(layer, c):
                q = NC * layer + c
                dve.wait_ge(s["f_rstd"], CREDIT + q + 1)
                dve.wait_ge(s["f_centred"], CREDIT + q + 1)
                dve.tensor_tensor(f_xn[:, c, :], f_xn[:, c, :], f_sq[:, c % 2, :], ALU.mult)\
                   .then_inc(s["f_normed"], 1)
                dve.wait_ge(s["f_normed"], CREDIT + q + 1)
                dve.tensor_scalar(f_xn[:, c, :], f_xn[:, c, :], par[:, L_G:L_G + 1], par[:, L_B:L_B + 1],
                                  ALU.mult, ALU.add).then_inc(s["f_scaled"], 1)

            def last_step(layer, pair):
                shift(layer, 0)
                shift(layer, 1)
                centre(pair, 1, 0)
                centre(pair, 1, 1)
                subtract_mean(layer, 0)
                subtract_mean(layer, 1)
                shift(layer, 2)
                dve.wait_ge(s["w_f_loaded"], 64 * layer + 64)
                divide(layer, 0)
                normalise(pair, 1, 0)
                normalise(pair, 1, 1)
                subtract_mean(layer, 2)
                divide(layer, 1)
                residual(pair, B - 1, 1)
                shift(layer, 3)
                divide(layer, 2)

            def feed_forward(layer, more):
                first = NC * layer

                def product(c, i):
                    size = HT[i][1]
                    k = 3 * first + 3 * c + i
                    dve.wait_ge(s["f_gated"], CREDIT + k + 1)
                    dve.wait_ge(s["f_value_up"], CREDIT + k + 1)
                    dve.wait_ge(s["f_down"], CREDIT + first + c)
                    dve.scalar_tensor_tensor(f_a[0:size, i, :], ps[0:size, 6, :],
                                             par[0:size, L_BA + i:L_BA + i + 1], f_g[0:size, i, :],
                                             ALU.add, ALU.mult).then_inc(s["f_prod"], 1)

                def add(c):
                    dve.wait_ge(s["f_down"], CREDIT + first + c + 1)
                    dve.scalar_tensor_tensor(h0_b[:, 2 * c:2 * c + 2, 1:HP],
                                             ps[:, 7, :].rearrange("p (b t) -> p b t", b=2), par[:, L_B2:L_B2 + 1],
                                             h1_b[:, 2 * c:2 * c + 2, 1:HP], ALU.add, ALU.add)\
                       .then_inc(s["f_done"], 1)

                dve.wait_ge(s["attended"], CREDIT + 32 * layer + 32)
                for c in range(NC):
                    for i in range(3):
                        product(c, i)
                        if c == 3 and i == 1 and more:
                            norms(layer * B + B, 0)
                    if c == 0:
                        subtract_mean(layer, 3)
                    if c == 2 and more:
                        dve.wait_ge(s["rope_ready"], CREDIT + layer + 2)
                        rope_products(layer * B + B, 0)
                    add(c)
                    if c == 0 and more:
                        dve.wait_ge(s["f_done"], CREDIT + first + 1)
                        dve.wait_ge(s["v_proj"], CREDIT + 16 * layer + 16)
                        stage(0, 0)
                        stage(0, 1)
                    if c == 1:
                        divide(layer, 3)
                    if not more:
                        dve.wait_ge(s["f_done"], CREDIT + first + c + 1)
                        for b in (2 * c, 2 * c + 1):
                            dve.scalar_tensor_tensor(x1[:, N * b:N * b + N], h0[:, HP * b + 1:HP * b + HP],
                                                     gate[:, 1, b:b + 1], x1[:, N * b:N * b + N],
                                                     ALU.mult, ALU.add).then_inc(s["final_done"], 1)
                if more:
                    scale_q(layer * B + B, 0)

            def layer_body(layer, more):
                first = snap(dve, layer * B)
                with dve.Fori(0, B - 1) as b:
                    pair = dve.snap(first + b)
                    step(pair, b, 0, (pair, 1), ahead=True)
                    step(pair, b, 1, (pair + 1, 0), ahead=True)
                last = snap(dve, first + (B - 1))
                step(last, B - 1, 0, (last, 1))
                last_step(layer, last)
                feed_forward(layer, more)

            stage(0, 0)
            stage(0, 1)
            dve.wait_ge(s["rope_ready"], CREDIT + 1)
            rope_products(0, 0)
            norms(0, 0)
            scale_q(0, 0)
            with dve.Fori(0, DEPTH - 1) as layer:
                layer_body(layer, True)
            layer_body(DEPTH - 1, False)


def constants():
    import numpy as np

    f = np.float32
    c = np.zeros((P, C_END), f)
    c[:, C_ID:C_ID + P] = np.eye(P, dtype=f)
    c[:, C_MEAN:C_MEAN + P] = f(1 / 128)
    i = np.arange(P)
    c[:, C_SUM2:C_SUM2 + P] = (i[:, None] // 32 == i[None] // 32) & (i[:, None] % 16 == i[None] % 16)
    own = np.arange(SPAN)
    key = 64 * (i // 64)[:, None] + np.where(own < 64, own, own - SPAN)[None]
    for m in range(U):
        seen = (key <= i[:, None]) & (key >= i[:, None] - W) & (key + P * m >= 0)
        c[:, C_MASK + SPAN * m:C_MASK + SPAN * (m + 1)] = np.where(seen, f(0), f(NEG))
    half = np.arange(0, D, 2, dtype=f)
    inv = f(1) / f(10000.0) ** (half / f(D))
    t = np.arange(N, dtype=f)
    freqs = (t[:, None] * inv[None]).astype(f)
    base = (half + f(0.4 * D)) / f(1.4 * D)
    power = (t - f(N // 2)) / f(W // 2)
    scale = (base[None] ** power[:, None]).astype(f)
    cos, sin = np.cos(freqs), np.sin(freqs)
    for m in range(U):
        r = slice(P * m, P * m + P)
        for k, (a, x) in enumerate(((8 * cos * scale, 1), (8 * sin * scale, -1), (cos / scale, 1), (sin / scale, -1))):
            at = C_ROPE + D * (4 * m + k)
            c[:, at:at + D] = np.concatenate([x * a[r], a[r]], -1)
    inv1 = f(1) / f(10000.0) ** (np.arange(0, AD, 2, dtype=f) / f(AD))
    fr = np.repeat((np.arange(N, dtype=f)[:, None] * inv1[None]).astype(f), 2, -1)
    sign = np.where(np.arange(AD) % 2 == 0, f(-1), f(1))
    both = np.concatenate([np.cos(fr), np.sin(fr) * sign], -1).reshape(AT, AG, 2 * AD)
    c[:, C_ROPE1:] = np.tile(both.transpose(2, 1, 0).reshape(2 * AD, AG * AT), (4, 1))
    return c


def kernel(**inputs):
    import numpy as np
    import concourse.bacc as bacc
    from concourse.bass_utils import run_bass_kernel_spmd

    x = {k: np.asarray(v) for k, v in inputs.items()}
    f = "L0_ffn_"

    def stacked(w):
        w = w.reshape(AG, AD // 2, 2, E)
        return np.stack([w, w[:, :, ::-1]], 1).reshape(AG * 2 * AD, E).T

    def tiles(b):
        return np.pad(b, ((0, 0), (0, 3 * P - HID))).reshape(DEPTH, 3, P).transpose(0, 2, 1)

    q, k = x[f + "q_scale"], x[f + "k_scale"]
    b1 = x[f + "b1"]
    arrays = {
        "xT": x["L0_attn_emb"].reshape(T, E).T,
        "w1s": stacked(x["L0_attn_W1"]).reshape(E, AG, 2 * AD),
        "w2s": stacked(x["L0_attn_W2"]).reshape(E, AG, 2 * AD),
        "w3T": x["L0_attn_W3"].T,
        "woT": x["L0_attn_Wo"].T.reshape(16, AG, E).transpose(1, 0, 2).reshape(P, E),
        "cT": x["L0_c"].T,
        "wmod": x["L0_wmod"],
        "wqkv": x[f + "Wqkv"],
        "scales": np.stack([q, np.roll(q, D // 2, 1), k, np.roll(k, D // 2, 1)], 1),
        "wo": x[f + "Wo"],
        "params": np.concatenate([x[f + "ln_g"][:, :, None], x[f + "ln_b"][:, :, None], x[f + "b2"][:, :, None],
                                  tiles(b1[:, :HID]), tiles(b1[:, HID:])], 2),
        "w1": x[f + "W1"],
        "w2": x[f + "W2"],
        "consts": constants(),
    }
    arrays = {n: np.ascontiguousarray(a) for n, a in arrays.items()}
    nc = bacc.Bacc("TRN2", target_bir_lowering=False, num_devices=1)
    args = [nc.dram_tensor(n, a.shape, mybir.dt.from_np(a.dtype), kind="ExternalInput").ap()
            for n, a in arrays.items()]
    out = nc.dram_tensor("out", (E, T), F32, kind="ExternalOutput").ap()
    build(nc, *args, out)
    r = run_bass_kernel_spmd(nc, [arrays], core_ids=[0])
    return np.ascontiguousarray(r.results[0]["out"].T.reshape(B, N, E))
```

```python
from contextlib import ExitStack

import concourse.bass as bass
from concourse import mybir

ACT = mybir.ActivationFunctionType
ALU = mybir.AluOpType
AX = mybir.AxisListType
F32 = mybir.dt.float32
BF16 = mybir.dt.bfloat16
F32R = mybir.dt.float32r

P = 128
B, N, E = 8, 256, 128
T = B * N
DEPTH = 6
AH, AD = 8, 16
AG = E // AD
AW = 32
AT = N // AH
H, D = 16, 64
INNER = H * D
W = 32
SPAN = 96
U = N // P
HC = H // 2
VD = D + 1
ON = 66
OW = 96
HID = 341
HT = [(0, 128), (128, 128), (256, HID - 256)]
CH = 512
NC = T // CH
HP = N + 1
NEG = -1e30
CREDIT = 4

C_ID, C_MEAN, C_SUM2, C_MASK, C_ROPE, C_ROPE1 = 0, 128, 256, 384, 384 + 2 * SPAN, 384 + 2 * SPAN + 2 * 4 * D
C_END = C_ROPE1 + AG * AT
L_G, L_B, L_B2, L_BA, L_BG, L_END = 0, 1, 2, 3, 6, 9


def build(nc, xT, w1s, w2s, w3T, woT, cT, wmod, wqkv, scales, wo, params, w1, w2, consts, out):
    with ExitStack() as ctx:
        def sb(name, shape, dt=F32):
            return ctx.enter_context(nc.sbuf_tensor(name, shape, dt))

        def sem(name):
            return ctx.enter_context(nc.semaphore(name))

        cst = sb("cst", [P, C_END])
        ident = cst[:, C_ID:C_ID + P]
        mean_w = cst[:, C_MEAN:C_MEAN + P]
        sum2_w = cst[:, C_SUM2:C_SUM2 + P]
        ident_bf = sb("ident_bf", [P, P], BF16)
        mask_bf = sb("mask_bf", [P, U, 4, SPAN], BF16)
        x1 = sb("x1", [P, T])
        h0 = sb("h0", [P, B * HP])
        h1 = sb("h1", [P, B * HP])
        mod = sb("mod", [P, 6, B])
        gate = sb("gate", [P, 2, B])
        wqkv_sb = sb("wqkv_sb", [P, 3 * INNER])
        wqkv_hi = sb("wqkv_hi", [P, 3 * INNER], F32R)
        wqkv_lo = sb("wqkv_lo", [P, 3 * INNER], F32R)
        wo_sb = sb("wo_sb", [P, INNER // P, E])
        w1_sb = sb("w1_sb", [P, 2 * HID])
        w1_hi = sb("w1_hi", [P, 2, 3 * P], F32R)
        w1_lo = sb("w1_lo", [P, 2, 3 * P], F32R)
        w2_sb = sb("w2_sb", [P, 3, E])
        par = sb("par", [P, L_END])
        scl = sb("scl", [P, 4, D])
        rope = sb("rope", [P, U, 4, D])
        k_t = sb("k_t", [P, U, H // 2, 2, SPAN])
        v_sb = sb("v_sb", [P, U, 2, H * VD + OW - VD])
        x_u = sb("x_u", [P, U, P])
        x_hi = sb("x_hi", [P, U, P], F32R)
        x_lo = sb("x_lo", [P, U, P], F32R)
        norm2 = sb("norm2", [P, 2 * H])
        norml = sb("norml", [P, 2 * H])
        rnorm = sb("rnorm", [P, 2 * H])
        rmax = sb("rmax", [P, H])
        rden = sb("rden", [P, H])
        f_x = sb("f_x", [P, 2, CH])
        f_hi = sb("f_hi", [P, 2, CH], F32R)
        f_lo = sb("f_lo", [P, 2, CH], F32R)
        f_sq = sb("f_sq", [P, 3, CH])
        f_xn = sb("f_xn", [P, NC, CH])
        arena = sb("arena", [P, 15 * 1024])

        def take(at, *shape):
            n = 1
            for s in shape:
                n *= s
            assert at + n <= 15 * 1024
            v = arena[:, at:at + n]
            if len(shape) == 2:
                v = v.rearrange("p (a b) -> p a b", a=shape[0])
            elif len(shape) == 3:
                v = v.rearrange("p (a b c) -> p a b c", a=shape[0], b=shape[1])
            return v

        t_cos = take(0, 2, INNER)
        t_sin = take(2048, 2, INNER)
        sq = take(4096, 2, INNER)
        q_t = take(6144, H // 2, P)
        s_sb = take(7168, 2, HC, SPAN)
        p_t = take(8704, H, P)
        o_n = take(11264, INNER)
        o_t = take(12288, H // 2, P)
        f_g = take(7168, 3, CH)
        f_a = take(8704, 3, CH)
        ln_xc = take(2048, NC, CH)
        ln_sq = take(4096, NC, CH)
        ln_r = take(6144, NC, CH)
        a_h = take(0, T)
        a_q = take(2048, AG, T // 4)
        a_k = take(6144, AG, T // 4)
        a_w1 = take(11264, AG, 2 * AD)
        a_w2 = take(11520, AG, 2 * AD)
        a_w3 = take(11776, E)
        a_wo = take(11904, E)
        a_cT = take(12032, B)
        a_sil = take(12040, B)
        a_wm = take(12288, 6 * E)
        a_v = (v_sb[:, :, :, :].rearrange("p u h c -> p (u h c)")[:, 0:4 * 2 * AH * 2 * AW]
               .rearrange("p (j i k d) -> p j i k d", j=4, i=2 * AH, k=2))
        a_qs = f_x[:, 0, :].rearrange("p (k c t) -> p k c t", k=2, c=2)
        a_ks = f_x[:, 1, :].rearrange("p (k t) -> p k t", k=2)
        a_vs = f_sq[:, 0, :].rearrange("p (k j h d) -> p k j h d", k=2, j=4, h=2)
        a_p = take(0, 8, N)
        a_pt = h1[:, 0:2048].rearrange("p (a b c) -> p a b c", a=8, b=2)
        a_of = sb("a_of", [P, 2, P])
        a_o = f_xn[:, :, :].rearrange("p j (c b h d) -> p j c b h d", c=2, b=2, h=AH)
        a_o_i = f_xn[:, :, :].rearrange("p j (c i d) -> p j c i d", c=2, d=AD)
        a_max = sb("a_max", [P, 8])
        a_nmax = sb("a_nmax", [P, 8])
        a_rden = sb("a_rden", [P, 2, 4])

        ps = ctx.enter_context(nc.psum_tensor("ps", [P, 8, 512], F32))

        def pair_of_banks(g):
            return ps[:, 2 * g:2 * g + 2, :]

        names = """
        const_loaded x_loaded a_loaded mod_loaded w_a_loaded w_f_loaded w_q_loaded w_s_loaded zeroed bf_ready
        silu_e silu_1 silu_r silu_ready mod_mm mod_ready gate_abs gate_sign
        ln_mean ln_centred ln_squared ln_var ln_log ln_rstd ln_normed ln_scaled
        a_zeroed a_v_mm a_v_ready a_proj a_roped a_summed a_k_ready a_staged a_v_staged a_scored a_maxed
        a_negated a_exped
        a_turned a_pt_ready a_pv a_o_copied a_o_turned a_recip a_o_ready a_out_mm x1_ready h0_ready
        f_lower f_upper f_mean f_centred f_squared f_var f_log f_rstd f_normed f_scaled
        f_high f_split w1_high w1_split
        f_gate_up f_value_up f_gated f_prod f_down f_done
        w_high w_split rope_ready x_staged x_high x_split q_proj k_proj v_proj squared roped
        normed guarded logged inverted rope_added q_scaled k_scaled q_turned k_turned q_copied k_copied v_copied
        scored maxed centred exped p_turned p_copied attended recip o_normed
        o_turned o_copied projected att_done final_done stored
        """.split()
        s = {n: sem(n) for n in names}

        def ln_tensor(pe, src, ready, k):
            for c in range(NC):
                ready(pe, c)
                pe.matmul(ps[:, c, :], mean_w, src[:, c, :], start=True, stop=True).then_inc(s["ln_mean"], 1)
            for c in range(NC):
                pe.wait_ge(s["ln_squared"], NC * k + c + 1)
                pe.matmul(ps[:, 4 + c, :], mean_w, ln_sq[:, c, :], start=True, stop=True).then_inc(s["ln_var"], 1)

        def ln_vector(dve, src, k):
            for c in range(NC):
                dve.wait_ge(s["ln_mean"], NC * k + c + 1)
                dve.tensor_tensor(ln_xc[:, c, :], src[:, c, :], ps[:, c, :], ALU.subtract)\
                   .then_inc(s["ln_centred"], 1)
            for c in range(NC):
                dve.wait_ge(s["ln_rstd"], NC * k + c + 1)
                dve.wait_ge(s["ln_centred"], NC * k + c + 1)
                dve.tensor_tensor(ln_xc[:, c, :], ln_xc[:, c, :], ln_r[:, c, :], ALU.mult)\
                   .then_inc(s["ln_normed"], 1)

        def ln_scalar(act, k):
            for c in range(NC):
                act.wait_ge(s["ln_centred"], NC * k + c + 1)
                act.activation(ln_sq[:, c, :], ln_xc[:, c, :], ACT.Square).then_inc(s["ln_squared"], 1)
            for c in range(NC):
                act.wait_ge(s["ln_var"], NC * k + c + 1)
                act.activation(ln_r[:, c, :], ps[:, 4 + c, :], ACT.Ln, bias=1e-5).then_inc(s["ln_log"], 1)
                act.wait_ge(s["ln_log"], NC * k + c + 1)
                act.activation(ln_r[:, c, :], ln_r[:, c, :], ACT.Exp, scale=-0.5).then_inc(s["ln_rstd"], 1)

        x1_c = x1[:, :].rearrange("p (c t) -> p c t", c=NC)

        credited = """
        f_lower f_upper f_mean f_centred f_squared f_var f_log f_rstd f_normed f_scaled
        f_high f_split w1_high w1_split
        f_gate_up f_value_up f_gated f_prod f_down f_done
        w_high w_split rope_ready x_staged x_high x_split q_proj k_proj v_proj squared roped
        normed guarded logged inverted rope_added q_scaled k_scaled q_turned k_turned q_copied k_copied v_copied
        scored maxed centred exped p_turned p_copied attended recip o_normed
        o_turned o_copied projected att_done
        a_scored a_exped a_pt_ready a_o_ready a_pv a_turned
        """.split()

        h0_b = h0[:, :].rearrange("p (b t) -> p b t", b=B)
        h1_b = h1[:, :].rearrange("p (b t) -> p b t", b=B)

        def snap(engine, value):
            return value if isinstance(value, int) else engine.snap(value)

        block = ctx.enter_context(nc.Block())

        @block.sync
        def _(sp):
            sp.dma_start(cst[:, :], consts).then_inc(s["const_loaded"], 16)
            sp.dma_start(x1[:, :], xT).then_inc(s["x_loaded"], 16)
            sp.dma_start(a_cT, cT).then_inc(s["mod_loaded"], 16)
            sp.dma_start(a_wm, wmod).then_inc(s["mod_loaded"], 16)
            sp.dma_start(a_w1, w1s).then_inc(s["a_loaded"], 16)
            sp.dma_start(a_w2, w2s).then_inc(s["a_loaded"], 16)
            sp.dma_start(a_w3, w3T).then_inc(s["a_loaded"], 16)
            sp.dma_start(a_wo, woT).then_inc(s["a_loaded"], 16)
            with sp.Fori(0, DEPTH) as layer:
                sp.wait_ge(s["w_split"], CREDIT + layer)
                sp.dma_start(wqkv_sb[:, :], wqkv[layer, :, :]).then_inc(s["w_q_loaded"], 16)
                sp.wait_ge(s["rope_ready"], CREDIT + layer)
                sp.dma_start(scl[:, :, :], scales[layer, :, :].unsqueeze(0).to_broadcast([P, 4, D]))\
                  .then_inc(s["w_s_loaded"], 16)
                sp.wait_ge(s["projected"], CREDIT + 16 * layer)
                sp.dma_start(wo_sb[:, :, :], wo[layer, :, :].rearrange("(c p) e -> p c e", p=P))\
                  .then_inc(s["w_a_loaded"], 16)
                sp.wait_ge(s["f_done"], CREDIT + NC * layer)
                sp.dma_start(w1_sb[:, :], w1[layer, :, :]).then_inc(s["w_f_loaded"], 16)
                sp.dma_start(w2_sb[:, 0:2, :], w2[layer, 0:256, :].rearrange("(c p) e -> p c e", p=P))\
                  .then_inc(s["w_f_loaded"], 16)
                sp.dma_start(w2_sb[0:HT[2][1], 2, :], w2[layer, 256:HID, :]).then_inc(s["w_f_loaded"], 16)
                sp.dma_start(par[:, :], params[layer, :, :]).then_inc(s["w_f_loaded"], 16)
            for c in range(NC):
                sp.wait_ge(s["final_done"], 2 * c + 2)
                sp.dma_start(out[:, CH * c:CH * c + CH], x1[:, CH * c:CH * c + CH]).then_inc(s["stored"], 16)
            sp.wait_ge(s["stored"], 16 * NC)

        @block.gpsimd
        def _(pool):
            pool.memset(v_sb[:, :, :, :], 1.0).then_inc(s["a_zeroed"], 1)
            pool.memset(h0[:, :], 0.0).then_inc(s["zeroed"], 1)
            pool.memset(w1_hi[:, :, :].bitcast(F32), 0.0).then_inc(s["zeroed"], 1)
            pool.memset(w1_lo[:, :, :].bitcast(F32), 0.0).then_inc(s["zeroed"], 1)
            pool.memset(k_t[:, :, :, :, :], 0.0).then_inc(s["zeroed"], 1)

            def rotate(pair, m):
                n = 2 * pair + m
                for j in range(2):
                    pool.wait_ge(s["roped"], CREDIT + 4 * n + 2 * j + 2)
                    pool.tensor_tensor(t_cos[:, j, :], t_cos[:, j, :], t_sin[:, j, :], ALU.add)\
                        .then_inc(s["rope_added"], 1)
                pool.wait_ge(s["inverted"], CREDIT + n + 1)
                pool.wait_ge(s["rope_added"], CREDIT + 2 * n + 2)
                k = t_cos[:, 1, :].rearrange("p (h d) -> p h d", h=H)
                pool.tensor_tensor(k, k, rnorm[:, H:2 * H].unsqueeze(2).to_broadcast([P, H, D]), ALU.mult)\
                    .then_inc(s["k_scaled"], 1)

            def tables(layer):
                pool.wait_ge(s["w_s_loaded"], 16 * layer + 16)
                pool.wait_ge(s["rope_added"], CREDIT + 32 * layer)
                for m in range(U):
                    pool.tensor_tensor(rope[:, m, :, :],
                                       cst[:, C_ROPE + 4 * D * m:C_ROPE + 4 * D * (m + 1)]
                                       .rearrange("p (k d) -> p k d", k=4), scl[:, :, :], ALU.mult)
                pool.drain().then_inc(s["rope_ready"], 1)

            def split_weights(layer):
                pool.wait_ge(s["w_high"], CREDIT + layer + 1)
                pool.tensor_tensor(wqkv_lo[:, :], wqkv_sb[:, :], wqkv_hi[:, :].bitcast(F32), ALU.subtract)\
                    .then_inc(s["w_split"], 1)

            def layer_body(layer, more):
                first = snap(pool, layer * B)
                with pool.Fori(0, B - 1) as b:
                    pair = pool.snap(first + b)
                    rotate(pair, 1)
                    rotate(pair + 1, 0)
                rotate(first + (B - 1), 1)
                pool.wait_ge(s["w1_high"], CREDIT + layer + 1)
                pool.tensor_tensor(w1_lo[:, :, 0:HID], w1_sb[:, :].rearrange("p (k c) -> p k c", k=2),
                                   w1_hi[:, :, 0:HID].bitcast(F32), ALU.subtract).then_inc(s["w1_split"], 1)
                if more:
                    split_weights(layer + 1)
                    tables(layer + 1)
                    rotate(first + B, 0)

            split_weights(0)
            tables(0)
            pool.wait_ge(s["a_v_staged"], 2 * AH)
            pool.memset(v_sb[:, :, :, :], 1.0).then_inc(s["zeroed"], 1)
            rotate(0, 0)
            with pool.Fori(0, DEPTH - 1) as layer:
                layer_body(layer, True)
            layer_body(DEPTH - 1, False)

        @block.tensor
        def _(pe):
            pe.wait_ge(s["mod_loaded"], 32)
            pe.wait_ge(s["silu_ready"], 1)
            for k in range(6):
                mm = pe.matmul(ps[:, 7, B * k:B * k + B], a_wm[:, E * k:E * k + E], a_sil, start=True, stop=True)
            mm.then_inc(s["mod_mm"], 1)
            pe.wait_ge(s["mod_ready"], 1)
            pe.wait_ge(s["const_loaded"], 16)

            def x_ready(pe, c):
                pe.wait_ge(s["x_loaded"], 16)

            ln_tensor(pe, x1_c, x_ready, 0)
            pe.wait_ge(s["ln_scaled"], B)
            pe.wait_ge(s["a_loaded"], 64)
            for u in range(T // P):
                mm = pe.matmul(ps[:, 4 + u // 4, P * (u % 4):][:, 0:P], a_h[:, P * u:P * u + P], a_w3,
                               start=True, stop=True)
            mm.then_inc(s["a_v_mm"], 1)
            for n, w in enumerate((a_w1, a_w2)):
                for g in range(AG):
                    i = n * AG + g
                    if i >= 4:
                        pe.wait_ge(s["a_roped"], i - 3)
                    for j in range(4):
                        mm = pe.matmul(ps[32 * j:32 * j + 32, i % 4, :], w[:, g, :],
                                       a_h[:, CH * j:CH * j + CH], start=True, stop=True)
                    mm.then_inc(s["a_proj"], 1)
            for g in range(AG):
                pe.wait_ge(s["a_roped"], AG + g + 1)
                if g >= 2:
                    pe.wait_ge(s["a_k_ready"], g - 1)
                if g == 0:
                    pe.wait_ge(s["a_v_ready"], 16)
                pe.matmul(ps[:, 4 + g % 2, :], sum2_w, a_k[:, g, :], start=True, stop=True)\
                    .then_inc(s["a_summed"], 1)
            pe.wait_ge(s["a_k_ready"], AG)
            pe.wait_ge(s["a_roped"], 2 * AG)

            def a_scores(i, k, half):
                pe.wait_ge(s["a_staged"], 2 * i + 2)
                pe.wait_ge(s["a_exped"], CREDIT + 8 * i - 4 + 4 * half)
                for q in range(4):
                    j, c = 2 * half + q % 2, q // 2
                    mm = pe.matmul(ps[:, j, N * c:N * c + N], a_qs[32 * j:32 * j + 32, k, c, :],
                                   a_ks[32 * j:32 * j + 32, k, :], start=True, stop=True,
                                   tile_position=(32 * j, 0))
                mm.then_inc(s["a_scored"], 1)

            def a_turn(i, half):
                pe.wait_ge(s["a_exped"], CREDIT + 8 * i + 4 * half + 4)
                pe.wait_ge(s["a_pt_ready"], CREDIT + 2 * i + half)
                for q in range(4):
                    for kh in range(2):
                        mm = pe.transpose(ps[:, 4 + q // 2, P * (2 * (q % 2) + kh):][:, 0:P],
                                          a_p[:, 4 * half + q, P * kh:P * kh + P], ident)
                mm.then_inc(s["a_turned"], 1)

            def a_attend(i, k):
                pe.wait_ge(s["a_pt_ready"], CREDIT + 2 * i + 2)
                pe.wait_ge(s["a_v_staged"], i + 1)
                if not (isinstance(i, int) and i == 0):
                    pe.wait_ge(s["a_o_copied"], i)
                for c in range(2):
                    for kh in range(2):
                        for j in range(4):
                            mm = pe.matmul(ps[32 * j:32 * j + 32, 6, P * c:P * c + P], a_vs[:, k, j, kh, :],
                                           a_pt[:, 2 * j + c, kh, :], start=(kh == 0), stop=(kh == 1),
                                           tile_position=(0, 32 * j), skip_group_check=True)
                mm.then_inc(s["a_pv"], 1)

            def a_turn_o(i):
                pe.wait_ge(s["a_o_copied"], i + 1)
                pe.wait_ge(s["a_o_ready"], CREDIT + i)
                for c in range(2):
                    mm = pe.transpose(ps[:, 7, P * c:P * c + P], a_of[:, c, :], ident)
                mm.then_inc(s["a_o_turned"], 1)

            def a_step(i, k, before=True, more=True):
                a_turn(i, 0)
                if more:
                    a_scores(i + 1, 1 - k, 0)
                a_turn(i, 1)
                if more:
                    a_scores(i + 1, 1 - k, 1)
                if before:
                    a_turn_o(i - 1)
                a_attend(i, k)

            a_scores(0, 0, 0)
            a_scores(0, 0, 1)
            a_step(0, 0, before=False)
            a_step(1, 1)
            with pe.Fori(1, AH - 1) as two:
                a_step(pe.snap(2 * two), 0)
                a_step(pe.snap(2 * two + 1), 1)
            a_step(2 * AH - 2, 0)
            a_step(2 * AH - 1, 1, more=False)
            a_turn_o(2 * AH - 1)
            pe.wait_ge(s["a_o_ready"], CREDIT + 2 * AH)
            for b in range(B):
                for c in range(2):
                    mm = pe.matmul(ps[:, b // 2, N * (b % 2) + P * c:][:, 0:P],
                                   a_o[:, b // 2, c, b % 2, :, :].rearrange("p h d -> p (h d)"), a_wo,
                                   start=True, stop=True)
                if b % 2:
                    mm.then_inc(s["a_out_mm"], 1)

            def x1_chunk(pe, c):
                pe.wait_ge(s["x1_ready"], 2 * c + 2)

            ln_tensor(pe, x1_c, x1_chunk, 1)

            def q_k(pair, m):
                n = 2 * pair + m
                pe.wait_ge(s["x_split"], CREDIT + n + 1)
                for j, done in ((0, "q_proj"), (1, "k_proj")):
                    if j == 0:
                        pe.wait_ge(s["q_copied"], CREDIT + n)
                    else:
                        pe.wait_ge(s["k_copied"], CREDIT + 5 * pair + 3 * m)
                    project_in(m, j, 2 * j).then_inc(s[done], 1)

            def project_in(m, j, bank):
                for c in range(2):
                    w = slice(INNER * j + 512 * c, INNER * j + 512 * c + 512)
                    pe.matmul(ps[:, bank + c, :], x_lo[:, m, :], wqkv_hi[:, w], start=True, stop=False)
                for c in range(2):
                    w = slice(INNER * j + 512 * c, INNER * j + 512 * c + 512)
                    pe.matmul(ps[:, bank + c, :], x_hi[:, m, :], wqkv_lo[:, w], start=False, stop=False)
                    mm = pe.matmul(ps[:, bank + c, :], x_hi[:, m, :], wqkv_hi[:, w], start=False, stop=True)
                return mm

            def v(pair, m):
                n = 2 * pair + m
                pe.wait_ge(s["roped"], CREDIT + 4 * n + 2)
                pe.wait_ge(s["squared"], CREDIT + 2 * n + 2)
                project_in(m, 2, 0).then_inc(s["v_proj"], 1)

            def turn_q_k(pair, m, before=False):
                n = 2 * pair + m
                for j, ready, done in ((0, "q_scaled", "q_turned"), (1, "k_scaled", "k_turned")):
                    pe.wait_ge(s[ready], CREDIT + n + 1)
                    if j == 0:
                        pe.wait_ge(s["v_copied"], CREDIT + 7 * pair + 3 + 4 * m)
                    else:
                        pe.wait_ge(s["roped"], CREDIT + 4 * n + 4)
                        pe.wait_ge(s["squared"], CREDIT + 2 * n + 1)
                        if before:
                            pe.wait_ge(s["att_done"], CREDIT + n - 1)
                    for c in range(H // 2):
                        mm = pe.transpose(ps[:, 2 * j + c // 4, P * (c % 4):][:, 0:P],
                                          t_cos[:, j, P * c:P * c + P], ident)
                    mm.then_inc(s[done], 1)

            def scores(pair, m, banks=(0, 1, 2, 3)):
                n = 2 * pair + m
                pe.wait_ge(s["q_copied"], CREDIT + n + 1)
                pe.wait_ge(s["k_copied"], CREDIT + 5 * pair + 3 + 2 * m)
                for bank in banks:
                    g, c = bank // 2, bank % 2
                    pe.wait_ge(s["o_copied" if g == 0 else "o_normed"], CREDIT + n * (1 + g))
                    pe.matmul(ps[:, 4 + bank, 0:4 * SPAN], ident_bf[:, :],
                              mask_bf[:, m, :, :].rearrange("p a b -> p (a b)"),
                              start=True, stop=False, skip_group_check=True)
                    for hh in range(4):
                        h = HC * g + 2 * hh + c
                        r = D * c
                        for j in range(2):
                            mm = pe.matmul(ps[64 * j:64 * j + 64, 4 + bank, SPAN * hh:SPAN * hh + SPAN],
                                           q_t[r:r + D, h // 2, 64 * j:64 * j + 64],
                                           k_t[r:r + D, m, h // 2, j, :],
                                           start=False, stop=(hh == 3), skip_group_check=True,
                                           tile_position=(r, 64 * j))
                    if c == 1:
                        mm.then_inc(s["scored"], 1)

            def turn_p(pair, m):
                n = 2 * pair + m
                for g in range(2):
                    pe.wait_ge(s["exped"], CREDIT + 2 * n + g + 1)
                    pe.wait_ge(s["centred"], CREDIT + 2 * n + g + 1)
                    for hh in range(HC):
                        mm = pe.transpose(ps[0:SPAN, 4 + 2 * g + hh // 4, P * (hh % 4):][:, 0:P],
                                          s_sb[:, g, hh, :], ident)
                    mm.then_inc(s["p_turned"], 1)

            def attend(pair, m):
                n = 2 * pair + m
                pe.wait_ge(s["v_copied"], CREDIT + 7 * pair + 3 + 4 * m)
                for g in range(2):
                    pe.wait_ge(s["p_copied"], CREDIT + 2 * n + g + 1)
                    for hh in range(HC):
                        h = HC * g + hh
                        for j in range(2):
                            mm = pe.matmul(ps[64 * j:64 * j + 64, 4 + 2 * g + hh // 4, OW * (hh % 4):][:, 0:ON],
                                           p_t[0:SPAN, h, 64 * j:64 * j + 64],
                                           v_sb[0:SPAN, m, j, VD * h:VD * h + ON], start=True,
                                           stop=True, skip_group_check=True, tile_position=(0, 64 * j))
                    mm.then_inc(s["attended"], 1)

            def project(pair, m):
                n = 2 * pair + m
                pe.wait_ge(s["o_normed"], CREDIT + 2 * n + 2)
                for c in range(H // 2):
                    mm = pe.transpose(ps[:, 4 + c // 4, P * (c % 4):][:, 0:P], o_n[:, P * c:P * c + P], ident)
                mm.then_inc(s["o_turned"], 1)

            def project_out(n, bank, under=None):
                pe.wait_ge(s["o_copied"], CREDIT + n + 1)
                if bank == 2 and under:
                    pe.wait_ge(s["roped"], CREDIT + 4 * n + 12)
                    pe.wait_ge(s["squared"], CREDIT + 2 * n + 6)
                for c in range(H // 2):
                    mm = pe.matmul(ps[:, bank, 0:P], wo_sb[:, c, :], o_t[:, c, :], start=(c == 0),
                                   stop=(c == H // 2 - 1))
                mm.then_inc(s["projected"], 1)

            def step(pair, m, after, before=True):
                q_k(*after)
                scores(pair, m, (0, 1, 2))
                v(*after)
                scores(pair, m, (3,))
                if before:
                    project_out(2 * pair + m - 1, 2, True)
                turn_p(pair, m)
                attend(pair, m)
                turn_q_k(*after, before=before)
                project(pair, m)

            def mean(layer, c):
                q = NC * layer + c
                pe.wait_ge(s["f_lower"], CREDIT + q + 1)
                pe.wait_ge(s["f_upper"], CREDIT + q + 1)
                pe.wait_ge(s["f_centred"], CREDIT + q - 1)
                pe.matmul(ps[:, c % 2, :], mean_w, f_x[:, c % 2, :], start=True, stop=True)\
                  .then_inc(s["f_mean"], 1)

            def variance(layer, c):
                q = NC * layer + c
                pe.wait_ge(s["f_squared"], CREDIT + q + 1)
                pe.wait_ge(s["f_log"], CREDIT + q - 1)
                pe.matmul(ps[:, 2 + c % 2, :], mean_w, f_sq[:, c % 3, :], start=True, stop=True)\
                  .then_inc(s["f_var"], 1)

            def last_step(layer, pair):
                pe.wait_ge(s["q_copied"], CREDIT + 2 * pair + 2)
                mean(layer, 0)
                mean(layer, 1)
                scores(pair, 1)
                project_out(2 * pair, 2)
                mean(layer, 2)
                turn_p(pair, 1)
                attend(pair, 1)
                pe.wait_ge(s["att_done"], CREDIT + 2 * pair + 1)
                variance(layer, 0)
                project(pair, 1)
                variance(layer, 1)
                variance(layer, 2)
                project_out(2 * pair + 1, 6)

            def feed_forward(layer, more):
                first = NC * layer

                def up(out, k, c, i):
                    w = slice(P * i, P * i + P)
                    pe.matmul(out, w1_lo[:, k, w], f_hi[:, c % 2, :], start=True, stop=False)
                    pe.matmul(out, w1_hi[:, k, w], f_lo[:, c % 2, :], start=False, stop=False)
                    return pe.matmul(out, w1_hi[:, k, w], f_hi[:, c % 2, :], start=False, stop=True)

                def gate_up(c, i):
                    k = 3 * c + i
                    pe.wait_ge(s["f_gated"], CREDIT + 3 * first + k - 1)
                    up(ps[:, 4 + k % 2, :], 1, c, i).then_inc(s["f_gate_up"], 1)

                def value_up(c, i):
                    pe.wait_ge(s["f_prod"], CREDIT + 3 * first + 3 * c + i)
                    up(ps[:, 6, :], 0, c, i).then_inc(s["f_value_up"], 1)

                def down(c, i):
                    at, size = HT[i]
                    pe.wait_ge(s["f_prod"], CREDIT + 3 * first + 3 * c + i + 1)
                    if i == 0:
                        pe.wait_ge(s["f_done"], CREDIT + first + c)
                    mm = pe.matmul(ps[:, 7, :], w2_sb[0:size, i, :], f_a[0:size, i, :],
                                   start=(i == 0), stop=(i == 2))
                    if i == 2:
                        mm.then_inc(s["f_down"], 1)

                pe.wait_ge(s["w_f_loaded"], 64 * layer + 64)
                pe.wait_ge(s["w1_split"], CREDIT + layer + 1)
                for c in range(NC):
                    if c == 3 and more:
                        pe.wait_ge(s["w_split"], CREDIT + layer + 2)
                        pe.wait_ge(s["w_a_loaded"], 16 * layer + 32)
                        pe.wait_ge(s["f_centred"], CREDIT + first + NC)
                        pe.wait_ge(s["f_log"], CREDIT + first + NC)
                        q_k(layer * B + B, 0)
                    pe.wait_ge(s["f_split"], CREDIT + first + c + 1)
                    gate_up(c, 0)
                    gate_up(c, 1)
                    if c:
                        down(c - 1, 2)
                    else:
                        pe.wait_ge(s["att_done"], CREDIT + 16 * layer + 16)
                    value_up(c, 0)
                    if c == 3 and more:
                        v(layer * B + B, 0)
                    gate_up(c, 2)
                    value_up(c, 1)
                    down(c, 0)
                    value_up(c, 2)
                    down(c, 1)
                    if c == 0:
                        mean(layer, 3)
                    if c == 1:
                        variance(layer, 3)
                down(NC - 1, 2)
                if more:
                    turn_q_k(layer * B + B, 0)

            def layer_body(layer, more):
                first = snap(pe, layer * B)
                pe.wait_ge(s["f_done"], CREDIT + NC * layer)
                step(first, 0, (first, 1), before=False)
                step(first, 1, (first + 1, 0))
                with pe.Fori(1, B - 1) as b:
                    pair = pe.snap(first + b)
                    step(pair, 0, (pair, 1))
                    step(pair, 1, (pair + 1, 0))
                last = snap(pe, first + (B - 1))
                step(last, 0, (last, 1))
                last_step(layer, last)
                feed_forward(layer, more)

            pe.wait_ge(s["zeroed"], 5)
            pe.wait_ge(s["bf_ready"], 2)
            pe.wait_ge(s["w_split"], CREDIT + 1)
            pe.wait_ge(s["w_a_loaded"], 16)
            q_k(0, 0)
            v(0, 0)
            turn_q_k(0, 0)
            with pe.Fori(0, DEPTH - 1) as layer:
                layer_body(layer, True)
            layer_body(DEPTH - 1, False)

        @block.scalar
        def _(act):
            act.preload_act_table_set("natural_log_exp_and_others")
            act.wait_ge(s["mod_loaded"], 32)
            act.activation(a_sil, a_cT, ACT.Exp, scale=-1.0).then_inc(s["silu_e"], 1)
            act.wait_ge(s["mod_mm"], 1)
            act.activation(mod[:, :, :].rearrange("p k b -> p (k b)"), ps[:, 7, 0:6 * B], ACT.Copy)\
               .then_inc(s["mod_ready"], 1)
            ln_scalar(act, 0)
            def round_weights(layer):
                act.wait_ge(s["w_q_loaded"], 16 * layer + 16)
                act.wait_ge(s["v_proj"], CREDIT + 16 * layer)
                act.activation(wqkv_hi[:, :], wqkv_sb[:, :], ACT.Copy).then_inc(s["w_high"], 1)

            round_weights(0)
            act.wait_ge(s["a_v_mm"], 1)
            act.wait_ge(s["a_zeroed"], 1)
            for a in range(4):
                for r in range(4):
                    act.activation(a_v[32 * r:32 * r + 32, :, :, :, 0:AD]
                                   .rearrange("p j (u a) k d -> p (j u) a k d", a=4)[:, :, a, :, :],
                                   ps[32 * a:32 * a + 32, 4:8, :]
                                   .rearrange("p b (u k r d) -> p (b u) k r d", u=4, k=2, r=4)[:, :, :, r, :],
                                   ACT.Copy).then_inc(s["a_v_ready"], 1)
            for g in range(AG):
                act.wait_ge(s["a_summed"], g + 1)
                act.activation(a_k[:, g, :], ps[:, 4 + g % 2, :], ACT.Copy).then_inc(s["a_k_ready"], 1)

            def a_exps(i, half):
                act.wait_ge(s["a_negated"], 2 * i + half + 1)
                act.wait_ge(s["a_turned"], CREDIT + 2 * i - 1 + half)
                for q in range(4):
                    k = 4 * half + q
                    act.activation(a_p[:, k, :], ps[:, 2 * half + q // 2, N * (q % 2):][:, 0:N], ACT.Exp,
                                   bias=a_nmax[:, k:k + 1], scale=AH ** -0.5).then_inc(s["a_exped"], 1)

            def a_copy_p(i, half):
                act.wait_ge(s["a_turned"], CREDIT + 2 * i + half + 1)
                act.wait_ge(s["a_pv"], CREDIT + i)
                act.activation(a_pt[:, 4 * half:4 * half + 4, :, :].rearrange("p a b c -> p (a b c)"),
                               ps[:, 4:6, :].rearrange("p a b -> p (a b)"), ACT.Copy)\
                   .then_inc(s["a_pt_ready"], 1)

            def a_stage_v(i, k):
                act.wait_ge(s["a_pv"], CREDIT + i - 1)
                act.activation(a_vs[:, k, :, :, :].rearrange("p j k d -> p j (k d)"),
                               a_v[:, :, bass.ds(i, 1), :, :].rearrange("p j i k d -> p j (i k d)"), ACT.Copy)\
                   .then_inc(s["a_v_staged"], 1)

            def a_step(i, k, more=True):
                a_exps(i, 0)
                a_exps(i, 1)
                a_copy_p(i, 0)
                if more:
                    a_stage_v(i + 1, 1 - k)
                a_copy_p(i, 1)

            act.wait_ge(s["a_v_ready"], 16)
            a_stage_v(0, 0)
            a_step(0, 0)
            a_step(1, 1)
            with act.Fori(1, AH - 1) as two:
                a_step(act.snap(2 * two), 0)
                a_step(act.snap(2 * two + 1), 1)
            a_step(2 * AH - 2, 0)
            a_step(2 * AH - 1, 1, more=False)
            ln_scalar(act, 1)

            def squares(pair, m):
                n = 2 * pair + m
                act.wait_ge(s["k_proj"], CREDIT + n + 1)
                act.wait_ge(s["normed"], CREDIT + 2 * n)
                act.activation(sq[:, 1, :], pair_of_banks(1).rearrange("p a b -> p (a b)"),
                               ACT.Square).then_inc(s["squared"], 1)
                act.wait_ge(s["roped"], CREDIT + 4 * n + 2)
                act.activation(sq[:, 0, :], pair_of_banks(0).rearrange("p a b -> p (a b)"),
                               ACT.Square).then_inc(s["squared"], 1)

            def inverse_norms(pair, m):
                n = 2 * pair + m
                act.wait_ge(s["guarded"], CREDIT + n + 1)
                act.activation(norml[:, :], norm2[:, :], ACT.Ln, scale=2.0 ** 24).then_inc(s["logged"], 1)
                act.wait_ge(s["logged"], CREDIT + n + 1)
                act.wait_ge(s["q_scaled"], CREDIT + n)
                act.wait_ge(s["k_scaled"], CREDIT + n)
                act.activation(rnorm[:, :], norml[:, :], ACT.Exp, scale=-0.5, bias=8.317766166719343)\
                   .then_inc(s["inverted"], 1)

            def copy_q_k(pair, m):
                n = 2 * pair + m
                act.wait_ge(s["q_turned"], CREDIT + n + 1)
                act.wait_ge(s["scored"], CREDIT + 2 * n)
                act.activation(q_t.rearrange("p a b -> p (a b)"),
                               pair_of_banks(0).rearrange("p a b -> p (a b)"), ACT.Copy)\
                   .then_inc(s["q_copied"], 1)
                act.wait_ge(s["k_turned"], CREDIT + n + 1)
                src = pair_of_banks(1).rearrange("p a (b c) -> p (a b) c", b=4)
                act.activation(k_t[:, m, :, :, 0:64], src.rearrange("p b (j k) -> p b j k", j=2), ACT.Copy)\
                   .then_inc(s["k_copied"], 1)
                act.activation(k_t[:, m, :, 1, 64:SPAN], src[:, :, 32:64], ACT.Copy).then_inc(s["k_copied"], 1)
                if m == 0:
                    act.activation(k_t[:, 1, :, 0, 64:SPAN], src[:, :, P - W:P], ACT.Copy)\
                       .then_inc(s["k_copied"], 1)

            def copy_v(pair, m, parts):
                if 0 in parts:
                    act.wait_ge(s["v_proj"], CREDIT + 2 * pair + m + 1)
                    act.wait_ge(s["attended"], CREDIT + 4 * pair - 2 * (1 - m))
                for k in parts:
                    half, there, here, rows = ((0, 0, 0, 64), (1, 0, 64, 64), (1, 64, 32, 32))[k]
                    act.activation(v_sb[there:there + rows, m, half, 0:H * VD]
                                   .rearrange("p (h d) -> p h d", h=H)[:, :, 0:D],
                                   pair_of_banks(0)[here:here + rows].rearrange("p a (b c) -> p (a b) c", b=8),
                                   ACT.Copy).then_inc(s["v_copied"], 1)

            def copy_v_before(pair):
                act.wait_ge(s["attended"], CREDIT + 4 * pair)
                act.wait_ge(s["v_copied"], CREDIT + 7 * pair + 3)
                act.activation(v_sb[64:96, 1, 0, 0:H * VD].rearrange("p (h d) -> p h d", h=H)[:, :, 0:D],
                               v_sb[32:64, 0, 1, 0:H * VD].rearrange("p (h d) -> p h d", h=H)[:, :, 0:D],
                               ACT.Copy).then_inc(s["v_copied"], 1)

            def exps(pair, m, g):
                n = 2 * pair + m
                act.wait_ge(s["centred"], CREDIT + 2 * n + g + 1)
                v = s_sb[:, g, :, :].rearrange("p h k -> p (h k)")
                act.activation(v, v, ACT.Exp).then_inc(s["exped"], 1)

            def copy_p(pair, m, g):
                n = 2 * pair + m
                act.wait_ge(s["p_turned"], CREDIT + 2 * n + g + 1)
                act.wait_ge(s["attended"], CREDIT + 2 * n)
                act.activation(p_t[0:SPAN, HC * g:HC * g + HC, :].rearrange("p a b -> p (a b)"),
                               pair_of_banks(2 + g)[0:SPAN].rearrange("p a b -> p (a b)"), ACT.Copy)\
                   .then_inc(s["p_copied"], 1)

            def copy_o(pair, m):
                n = 2 * pair + m
                act.wait_ge(s["o_turned"], CREDIT + n + 1)
                act.wait_ge(s["projected"], CREDIT + n)
                act.activation(o_t.rearrange("p a b -> p (a b)"),
                               pair_of_banks(2).rearrange("p a b -> p (a b)"), ACT.Copy)\
                   .then_inc(s["o_copied"], 1)

            def step(pair, m, after, layer=None):
                squares(*after)
                copy_v(*after, (0, 1))
                exps(pair, m, 0)
                exps(pair, m, 1)
                copy_p(pair, m, 0)
                copy_p(pair, m, 1)
                inverse_norms(*after)
                copy_v(*after, (2,))
                if layer is not None:
                    shift(layer, 0)
                    shift(layer, 1)
                copy_q_k(*after)
                copy_o(pair, m)
                if m == 1:
                    copy_v_before(pair + 1)

            def shift(layer, c):
                act.wait_ge(s["att_done"], CREDIT + 16 * layer + 4 * c + 4)
                act.wait_ge(s["f_centred"], CREDIT + NC * layer + c - 1)
                act.activation(f_x[64:128, c % 2, :].rearrange("p (b t) -> p b t", b=2),
                               h1_b[64:128, 2 * c:2 * c + 2, 0:N], ACT.Copy).then_inc(s["f_upper"], 1)

            def square(layer, c):
                q = NC * layer + c
                act.wait_ge(s["f_centred"], CREDIT + q + 1)
                act.wait_ge(s["f_normed"], CREDIT + q - min(c, 2))
                act.activation(f_sq[:, c % 3, :], f_xn[:, c, :], ACT.Square).then_inc(s["f_squared"], 1)

            def inverse_deviation(layer, c):
                q = NC * layer + c
                act.wait_ge(s["f_var"], CREDIT + q + 1)
                act.activation(f_sq[:, c % 3, :], ps[:, 2 + c % 2, :], ACT.Ln, bias=1e-5).then_inc(s["f_log"], 1)
                act.wait_ge(s["f_log"], CREDIT + q + 1)
                act.activation(f_sq[:, c % 3, :], f_sq[:, c % 3, :], ACT.Exp, scale=-0.5)\
                   .then_inc(s["f_rstd"], 1)

            def last_step(layer, pair):
                act.wait_ge(s["w_f_loaded"], 64 * layer + 64)
                act.activation(w1_hi[:, :, 0:HID], w1_sb[:, :].rearrange("p (k c) -> p k c", k=2), ACT.Copy)\
                   .then_inc(s["w1_high"], 1)
                square(layer, 0)
                square(layer, 1)
                shift(layer, 2)
                exps(pair, 1, 0)
                exps(pair, 1, 1)
                copy_p(pair, 1, 0)
                copy_p(pair, 1, 1)
                square(layer, 2)
                inverse_deviation(layer, 0)
                copy_o(pair, 1)
                inverse_deviation(layer, 1)
                inverse_deviation(layer, 2)

            def gates(layer, c, tiles=(0, 1, 2)):
                for i in tiles:
                    size = HT[i][1]
                    k = 3 * c + i
                    act.wait_ge(s["f_gate_up"], CREDIT + 3 * NC * layer + k + 1)
                    act.wait_ge(s["f_prod"], CREDIT + 3 * NC * layer + k - 2)
                    act.activation(f_g[0:size, i, :], ps[0:size, 4 + k % 2, :], ACT.Gelu,
                                   bias=par[0:size, L_BG + i:L_BG + i + 1]).then_inc(s["f_gated"], 1)

            def feed_forward(layer, more):
                act.wait_ge(s["attended"], CREDIT + 32 * layer + 32)
                gates(layer, 0, (0,))
                shift(layer, 3)
                gates(layer, 0, (1, 2))
                if more:
                    round_weights(layer + 1)
                square(layer, 3)
                gates(layer, 1)
                act.preload_act_table_set("natural_log_exp_and_others")
                inverse_deviation(layer, 3)
                gates(layer, 2)
                if more:
                    squares(layer * B + B, 0)
                gates(layer, 3, (0, 1))
                if more:
                    copy_v(layer * B + B, 0, (0, 1))
                gates(layer, 3, (2,))
                if more:
                    copy_v(layer * B + B, 0, (2,))
                    act.preload_act_table_set("natural_log_exp_and_others")
                    inverse_norms(layer * B + B, 0)
                    copy_q_k(layer * B + B, 0)
                    copy_v_before(layer * B + B)

            def layer_body(layer, more):
                first = snap(act, layer * B)
                with act.Fori(0, B - 1) as b:
                    pair = act.snap(first + b)
                    step(pair, 0, (pair, 1))
                    step(pair, 1, (pair + 1, 0))
                last = snap(act, first + (B - 1))
                step(last, 0, (last, 1), layer)
                last_step(layer, last)
                feed_forward(layer, more)

            act.wait_ge(s["zeroed"], 5)
            act.preload_act_table_set("natural_log_exp_and_others")
            squares(0, 0)
            copy_v(0, 0, (0, 1))
            inverse_norms(0, 0)
            copy_v(0, 0, (2,))
            copy_q_k(0, 0)
            copy_v_before(0)
            with act.Fori(0, DEPTH - 1) as layer:
                act.preload_act_table_set("natural_log_exp_and_others")
                layer_body(layer, True)
            act.preload_act_table_set("natural_log_exp_and_others")
            layer_body(DEPTH - 1, False)

        @block.vector
        def _(dve):
            for name in credited:
                dve.sem_inc(s[name], CREDIT)
            dve.wait_ge(s["silu_e"], 1)
            dve.tensor_scalar(a_sil, a_sil, 1.0, None, ALU.add).then_inc(s["silu_1"], 1)
            dve.wait_ge(s["silu_1"], 1)
            dve.reciprocal(a_sil, a_sil).then_inc(s["silu_r"], 1)
            dve.wait_ge(s["silu_r"], 1)
            dve.tensor_tensor(a_sil, a_sil, a_cT, ALU.mult).then_inc(s["silu_ready"], 1)
            dve.wait_ge(s["const_loaded"], 16)
            dve.tensor_copy(ident_bf[:, :], ident).then_inc(s["bf_ready"], 1)
            dve.tensor_copy(mask_bf[:, :, :, :],
                            cst[:, C_MASK:C_MASK + U * SPAN].rearrange("p (m k) -> p m k", m=U)
                            .unsqueeze(2).to_broadcast([P, U, 4, SPAN])).then_inc(s["bf_ready"], 1)
            dve.wait_ge(s["mod_ready"], 1)
            for n, k in enumerate((2, 5)):
                dve.tensor_scalar(gate[:, n, :], mod[:, k, :], 0.25, None, ALU.max).then_inc(s["gate_abs"], 1)
                dve.wait_ge(s["gate_abs"], 2 * n + 1)
                dve.scalar_tensor_tensor(gate[:, n, :], mod[:, k, :], -1.0, gate[:, n, :], ALU.mult, ALU.max)\
                   .then_inc(s["gate_abs"], 1)
                dve.tensor_scalar(mod[:, k, :], mod[:, k, :], 0.0, 2.0, ALU.is_ge, ALU.mult)\
                   .then_inc(s["gate_sign"], 1)
            dve.wait_ge(s["gate_sign"], 2)
            dve.wait_ge(s["gate_abs"], 4)
            for n, k in enumerate((2, 5)):
                dve.scalar_tensor_tensor(gate[:, n, :], mod[:, k, :], -1.0, gate[:, n, :], ALU.add, ALU.mult)\
                   .then_inc(s["gate_sign"], 1)
            for k in (1, 4):
                dve.tensor_scalar(mod[:, k, :], mod[:, k, :], 1.0, None, ALU.add).then_inc(s["gate_sign"], 1)
            dve.wait_ge(s["gate_sign"], 6)
            dve.wait_ge(s["x_loaded"], 16)
            ln_vector(dve, x1_c, 0)
            xc = ln_xc.rearrange("p c t -> p (c t)")
            for b in range(B):
                dve.wait_ge(s["ln_normed"], b // 2 + 1)
                dve.tensor_scalar(a_h[:, N * b:N * b + N], xc[:, N * b:N * b + N], mod[:, 1, b:b + 1],
                                  mod[:, 0, b:b + 1], ALU.mult, ALU.add).then_inc(s["ln_scaled"], 1)
            dve.wait_ge(s["ln_scaled"], B)
            tab = cst[:, C_ROPE1:C_ROPE1 + AG * AT].rearrange("p (g t) -> p g t", g=AG)
            for n, dst in enumerate((a_q, a_k)):
                for g in range(AG):
                    i = n * AG + g
                    dve.wait_ge(s["a_proj"], i + 1)
                    dve.tensor_tensor(dst[:, g, :].rearrange("p (i t) -> p i t", t=AT),
                                      ps[:, i % 4, :].rearrange("p (i t) -> p i t", t=AT),
                                      tab[:, g, :].unsqueeze(1).to_broadcast([P, CH // AT, AT]), ALU.mult)\
                       .then_inc(s["a_roped"], 1)
            def a_stage(i, k):
                if not isinstance(i, int) or i >= 2:
                    dve.wait_ge(s["a_scored"], CREDIT + 2 * i - 2)
                dve.tensor_copy(a_qs[:, k, :, :].rearrange("p c (g t) -> p c g t", g=AG),
                                a_q[:, :, bass.ds(AT * i, AT)].rearrange("p g (c t) -> p c g t", c=2))\
                   .then_inc(s["a_staged"], 1)
                dve.tensor_copy(a_ks[:, k, :].rearrange("p (g t) -> p g t", g=AG),
                                a_k[:, :, bass.ds(AT * i, AT)]).then_inc(s["a_staged"], 1)

            def a_maximum(i, half):
                dve.wait_ge(s["a_scored"], CREDIT + 2 * i + half + 1)
                mx = a_max[:, 4 * half:4 * half + 4]
                dve.tensor_reduce(mx, ps[:, 2 * half:2 * half + 2, :].rearrange("p a (b c) -> p (a b) c", b=2),
                                  AX.X, ALU.max).then_inc(s["a_maxed"], 1)
                dve.wait_ge(s["a_maxed"], 2 * i + half + 1)
                dve.wait_ge(s["a_exped"], CREDIT + 8 * i - 4 + 4 * half)
                dve.tensor_scalar(a_nmax[:, 4 * half:4 * half + 4], mx, -AH ** -0.5, None, ALU.mult)\
                   .then_inc(s["a_negated"], 1)

            def a_copy_o(i):
                dve.wait_ge(s["a_pv"], CREDIT + i + 1)
                dve.tensor_copy(a_of[:, :, :], ps[:, 6, 0:2 * P].rearrange("p (c q) -> p c q", c=2))\
                   .then_inc(s["a_o_copied"], 1)

            def a_normalise(i):
                dve.wait_ge(s["a_o_turned"], i + 1)
                o = ps[:, 7, 0:2 * P].rearrange("p (c j d) -> p c j d", c=2, j=4)
                dve.reciprocal(a_rden[:, :, :], o[:, :, :, AD]).then_inc(s["a_recip"], 1)
                dve.wait_ge(s["a_recip"], i + 1)
                dve.tensor_tensor(a_o_i[:, :, :, bass.ds(i, 1), :].rearrange("p j c i d -> p c j (i d)"),
                                  o[:, :, :, 0:AD], a_rden[:, :, :].unsqueeze(3).to_broadcast([P, 2, 4, AD]),
                                  ALU.mult).then_inc(s["a_o_ready"], 1)

            def a_step(i, k, before=True, more=True, stage=True):
                if more:
                    a_maximum(i + 1, 0)
                    a_maximum(i + 1, 1)
                if before:
                    a_normalise(i - 1)
                if stage:
                    a_stage(i + 2, k)
                a_copy_o(i)

            dve.wait_ge(s["a_roped"], 2 * AG)
            dve.wait_ge(s["a_k_ready"], AG)
            a_stage(0, 0)
            a_stage(1, 1)
            a_maximum(0, 0)
            a_maximum(0, 1)
            a_step(0, 0, before=False)
            a_step(1, 1)
            with dve.Fori(1, AH - 1) as two:
                a_step(dve.snap(2 * two), 0)
                a_step(dve.snap(2 * two + 1), 1)
            a_step(2 * AH - 2, 0, stage=False)
            a_step(2 * AH - 1, 1, more=False, stage=False)
            a_normalise(2 * AH - 1)
            for b in range(B):
                dve.wait_ge(s["a_out_mm"], b // 2 + 1)
                dve.scalar_tensor_tensor(x1[:, N * b:N * b + N], ps[:, b // 2, N * (b % 2):][:, 0:N],
                                         gate[:, 0, b:b + 1], x1[:, N * b:N * b + N], ALU.mult, ALU.add)\
                   .then_inc(s["x1_ready"], 1)
            dve.wait_ge(s["x1_ready"], B)
            ln_vector(dve, x1_c, 1)
            dve.wait_ge(s["zeroed"], 5)

            def modulate(b):
                dve.wait_ge(s["ln_normed"], NC + b // 2 + 1)
                dve.tensor_scalar(h0[:, HP * b + 1:HP * b + HP], xc[:, N * b:N * b + N], mod[:, 4, b:b + 1],
                                  mod[:, 3, b:b + 1], ALU.mult, ALU.add).then_inc(s["h0_ready"], 1)

            def rope_products(pair, m):
                n = 2 * pair + m
                for j in range(2):
                    dve.wait_ge(s["q_proj" if j == 0 else "squared"], CREDIT + (n if j == 0 else 2 * n) + 1)
                    dve.wait_ge(s["q_turned" if j == 0 else "k_turned"], CREDIT + n)
                    src = pair_of_banks(j).rearrange("p a (h d) -> p (a h) d", h=8)
                    tc, ts = rope[:, m, 2 * j, :], rope[:, m, 2 * j + 1, :]
                    dve.tensor_tensor(t_cos[:, j, :].rearrange("p (h d) -> p h d", h=H), src,
                                      tc.unsqueeze(1).to_broadcast([P, H, D]), ALU.mult).then_inc(s["roped"], 1)
                    dve.tensor_tensor(t_sin[:, j, :].rearrange("p (h s d) -> p h s d", h=H, s=2),
                                      pair_of_banks(j).rearrange("p a (h s d) -> p (a h) s d", h=8, s=2)[:, :, ::-1, :],
                                      ts.rearrange("p (s d) -> p s d", s=2).unsqueeze(1)
                                      .to_broadcast([P, H, 2, D // 2]), ALU.mult).then_inc(s["roped"], 1)

            def norms(pair, m):
                n = 2 * pair + m
                for j in (1, 0):
                    dve.wait_ge(s["squared"], CREDIT + 2 * n + 2 - j)
                    dve.wait_ge(s["logged"], CREDIT + n)
                    dve.tensor_reduce(norm2[:, H * j:H * j + H], sq[:, j, :].rearrange("p (h d) -> p h d", h=H),
                                      AX.X, ALU.add).then_inc(s["normed"], 1)
                dve.wait_ge(s["normed"], CREDIT + 2 * n + 2)
                dve.tensor_scalar(norm2[:, :], norm2[:, :], 1e-24, None, ALU.max).then_inc(s["guarded"], 1)

            def centre(pair, m, g):
                n = 2 * pair + m
                dve.wait_ge(s["scored"], CREDIT + 2 * n + g + 1)
                src = pair_of_banks(2 + g)[:, :, 0:4 * SPAN].rearrange("p a (h k) -> p a h k", h=4)
                mx = rmax[:, HC * g:HC * g + HC].rearrange("p (h a) -> p a h", a=2)
                dve.tensor_reduce(mx, src, AX.X, ALU.max)\
                   .then_inc(s["maxed"], 1)
                dve.wait_ge(s["maxed"], CREDIT + 2 * n + g + 1)
                dve.wait_ge(s["p_turned"], CREDIT + 2 * n)
                dve.tensor_tensor(s_sb[:, g, :, :].rearrange("p (h a) k -> p a h k", a=2), src,
                                  mx.unsqueeze(3).to_broadcast([P, 2, 4, SPAN]), ALU.subtract).then_inc(s["centred"], 1)

            def normalise(pair, m, g):
                n = 2 * pair + m
                dve.wait_ge(s["attended"], CREDIT + 2 * n + g + 1)
                o = pair_of_banks(2 + g)[:, :, 0:4 * OW].rearrange("p a (h k) -> p a h k", h=4)
                rd = rden[:, HC * g:HC * g + HC].rearrange("p (a h) -> p a h", a=2)
                dve.reciprocal(rd, o[:, :, :, D]).then_inc(s["recip"], 1)
                dve.wait_ge(s["recip"], CREDIT + 2 * n + g + 1)
                dve.wait_ge(s["o_turned"], CREDIT + n)
                dve.tensor_tensor(o_n[:, HC * D * g:HC * D * (g + 1)]
                                  .rearrange("p (a h d) -> p a h d", a=2, h=4), o[:, :, :, 0:D],
                                  rd.unsqueeze(3).to_broadcast([P, 2, 4, D]), ALU.mult)\
                   .then_inc(s["o_normed"], 1)

            def residual(n, b, m, bank=2):
                col = b * HP + (1 + P * m)
                dve.wait_ge(s["projected"], CREDIT + n + 1)
                dve.tensor_tensor(h1[:, bass.ds(col, P)], ps[:, bank, 0:P], h0[:, bass.ds(col, P)], ALU.add)\
                   .then_inc(s["att_done"], 1)

            def stage(b, n, m):
                col = b * HP + P * m
                dve.tensor_scalar(x_u[0:64, m, :], h0[0:64, bass.ds(col + 1, P)], 1.0, None, ALU.mult)\
                   .then_inc(s["x_staged"], 1)
                dve.tensor_scalar(x_u[64:128, m, :], h0[64:128, bass.ds(col, P)], 1.0, None, ALU.mult)\
                   .then_inc(s["x_staged"], 1)
                dve.wait_ge(s["x_staged"], CREDIT + 2 * n + 2)
                dve.tensor_copy(x_hi[:, m, :], x_u[:, m, :]).then_inc(s["x_high"], 1)
                dve.wait_ge(s["x_high"], CREDIT + n + 1)
                dve.tensor_tensor(x_lo[:, m, :], x_u[:, m, :], x_hi[:, m, :].bitcast(F32), ALU.subtract)\
                   .then_inc(s["x_split"], 1)

            def scale_q(pair, m):
                n = 2 * pair + m
                dve.wait_ge(s["inverted"], CREDIT + n + 1)
                dve.wait_ge(s["rope_added"], CREDIT + 2 * n + 1)
                q = t_cos[:, 0, :].rearrange("p (h d) -> p h d", h=H)
                dve.tensor_tensor(q, q, rnorm[:, 0:H].unsqueeze(2).to_broadcast([P, H, D]), ALU.mult)\
                   .then_inc(s["q_scaled"], 1)

            def step(pair, b, m, after, before=True, ahead=True):
                rope_products(*after)
                centre(pair, m, 0)
                centre(pair, m, 1)
                if before:
                    residual(2 * pair + m - 1, b if m else b - 1, 1 - m)
                norms(*after)
                scale_q(*after)
                normalise(pair, m, 0)
                normalise(pair, m, 1)
                if ahead:
                    dve.wait_ge(s["v_proj"], CREDIT + 2 * pair + m + 1)
                    stage(b + 1, 2 * pair + m + 2, m)

            def shift(layer, c):
                q = NC * layer + c
                dve.wait_ge(s["att_done"], CREDIT + 16 * layer + 4 * c + 4)
                dve.wait_ge(s["f_centred"], CREDIT + q - 1)
                dve.tensor_copy(f_x[0:64, c % 2, :].rearrange("p (b t) -> p b t", b=2),
                                h1_b[0:64, 2 * c:2 * c + 2, 1:HP]).then_inc(s["f_lower"], 1)

            def subtract_mean(layer, c):
                dve.wait_ge(s["f_mean"], CREDIT + NC * layer + c + 1)
                dve.tensor_tensor(f_xn[:, c, :], f_x[:, c % 2, :], ps[:, c % 2, :], ALU.subtract)\
                   .then_inc(s["f_centred"], 1)

            def divide(layer, c):
                q = NC * layer + c
                dve.wait_ge(s["f_rstd"], CREDIT + q + 1)
                dve.wait_ge(s["f_centred"], CREDIT + q + 1)
                dve.tensor_tensor(f_xn[:, c, :], f_xn[:, c, :], f_sq[:, c % 3, :], ALU.mult)\
                   .then_inc(s["f_normed"], 1)
                dve.wait_ge(s["f_normed"], CREDIT + q + 1)
                dve.tensor_scalar(f_xn[:, c, :], f_xn[:, c, :], par[:, L_G:L_G + 1], par[:, L_B:L_B + 1],
                                  ALU.mult, ALU.add).then_inc(s["f_scaled"], 1)

            def split(layer, c):
                q = NC * layer + c
                dve.wait_ge(s["f_scaled"], CREDIT + q + 1)
                dve.wait_ge(s["f_value_up"], CREDIT + 3 * NC * layer + 3 * max(c - 1, 0))
                dve.tensor_copy(f_hi[:, c % 2, :], f_xn[:, c, :]).then_inc(s["f_high"], 1)
                dve.wait_ge(s["f_high"], CREDIT + q + 1)
                dve.tensor_tensor(f_lo[:, c % 2, :], f_xn[:, c, :], f_hi[:, c % 2, :].bitcast(F32), ALU.subtract)\
                   .then_inc(s["f_split"], 1)

            def last_step(layer, pair):
                shift(layer, 0)
                shift(layer, 1)
                subtract_mean(layer, 0)
                subtract_mean(layer, 1)
                shift(layer, 2)
                centre(pair, 1, 0)
                centre(pair, 1, 1)
                residual(2 * pair, B - 1, 0)
                subtract_mean(layer, 2)
                normalise(pair, 1, 0)
                normalise(pair, 1, 1)
                dve.wait_ge(s["w_f_loaded"], 64 * layer + 64)
                divide(layer, 0)
                split(layer, 0)
                divide(layer, 1)
                residual(2 * pair + 1, B - 1, 1, bank=6)
                split(layer, 1)
                divide(layer, 2)
                shift(layer, 3)

            def feed_forward(layer, more):
                first = NC * layer

                def product(c, i):
                    size = HT[i][1]
                    k = 3 * first + 3 * c + i
                    dve.wait_ge(s["f_gated"], CREDIT + k + 1)
                    dve.wait_ge(s["f_value_up"], CREDIT + k + 1)
                    dve.wait_ge(s["f_down"], CREDIT + first + c)
                    dve.scalar_tensor_tensor(f_a[0:size, i, :], ps[0:size, 6, :],
                                             par[0:size, L_BA + i:L_BA + i + 1], f_g[0:size, i, :],
                                             ALU.add, ALU.mult).then_inc(s["f_prod"], 1)

                def add(c):
                    dve.wait_ge(s["f_down"], CREDIT + first + c + 1)
                    dve.scalar_tensor_tensor(h0_b[:, 2 * c:2 * c + 2, 1:HP],
                                             ps[:, 7, :].rearrange("p (b t) -> p b t", b=2), par[:, L_B2:L_B2 + 1],
                                             h1_b[:, 2 * c:2 * c + 2, 1:HP], ALU.add, ALU.add)\
                       .then_inc(s["f_done"], 1)

                dve.wait_ge(s["attended"], CREDIT + 32 * layer + 32)
                for c in range(NC):
                    for i in range(3):
                        product(c, i)
                        if c == 1 and i < 2 and more:
                            if i == 0:
                                dve.wait_ge(s["f_done"], CREDIT + first + 1)
                                dve.wait_ge(s["v_proj"], CREDIT + 16 * layer + 16)
                            stage(0, 16 * layer + 16 + i, i)
                        if c == 2 and i == 0:
                            divide(layer, 3)
                        if c == 0 and i == 2:
                            split(layer, 2)
                        if c == 2 and i == 1:
                            split(layer, 3)
                        if c == 3 and i == 0 and more:
                            norms(layer * B + B, 0)
                    if c == 0:
                        subtract_mean(layer, 3)
                    if c == 2 and more:
                        dve.wait_ge(s["rope_ready"], CREDIT + layer + 2)
                        rope_products(layer * B + B, 0)
                    if c == 3 and more:
                        scale_q(layer * B + B, 0)
                    add(c)
                    if not more:
                        dve.wait_ge(s["f_done"], CREDIT + first + c + 1)
                        for b in (2 * c, 2 * c + 1):
                            dve.scalar_tensor_tensor(x1[:, N * b:N * b + N], h0[:, HP * b + 1:HP * b + HP],
                                                     gate[:, 1, b:b + 1], x1[:, N * b:N * b + N],
                                                     ALU.mult, ALU.add).then_inc(s["final_done"], 1)

            def layer_body(layer, more):
                first = snap(dve, layer * B)
                step(first, 0, 0, (first, 1), before=False)
                step(first, 0, 1, (first + 1, 0))
                with dve.Fori(1, B - 1) as b:
                    pair = dve.snap(first + b)
                    step(pair, b, 0, (pair, 1))
                    step(pair, b, 1, (pair + 1, 0))
                last = snap(dve, first + (B - 1))
                step(last, B - 1, 0, (last, 1), ahead=False)
                last_step(layer, last)
                feed_forward(layer, more)

            modulate(0)
            dve.wait_ge(s["h0_ready"], 1)
            stage(0, 0, 0)
            stage(0, 1, 1)
            for b in range(1, B):
                modulate(b)
            dve.wait_ge(s["h0_ready"], B)
            dve.wait_ge(s["a_pt_ready"], CREDIT + 4 * AH)
            dve.wait_ge(s["a_pv"], CREDIT + 2 * AH)
            dve.wait_ge(s["rope_ready"], CREDIT + 1)
            rope_products(0, 0)
            norms(0, 0)
            scale_q(0, 0)
            dve.memset(h1[:, :], 0.0)
            with dve.Fori(0, DEPTH - 1) as layer:
                layer_body(layer, True)
            layer_body(DEPTH - 1, False)


def constants():
    import numpy as np

    f = np.float32
    c = np.zeros((P, C_END), f)
    c[:, C_ID:C_ID + P] = np.eye(P, dtype=f)
    c[:, C_MEAN:C_MEAN + P] = f(1 / 128)
    i = np.arange(P)
    c[:, C_SUM2:C_SUM2 + P] = (i[:, None] // 32 == i[None] // 32) & (i[:, None] % 16 == i[None] % 16)
    own = np.arange(SPAN)
    key = 64 * (i // 64)[:, None] + np.where(own < 64, own, own - SPAN)[None]
    for m in range(U):
        seen = (key <= i[:, None]) & (key >= i[:, None] - W) & (key + P * m >= 0)
        c[:, C_MASK + SPAN * m:C_MASK + SPAN * (m + 1)] = np.where(seen, f(0), f(NEG))
    half = np.arange(0, D, 2, dtype=f)
    inv = f(1) / f(10000.0) ** (half / f(D))
    t = np.arange(N, dtype=f)
    freqs = (t[:, None] * inv[None]).astype(f)
    base = (half + f(0.4 * D)) / f(1.4 * D)
    power = (t - f(N // 2)) / f(W // 2)
    scale = (base[None] ** power[:, None]).astype(f)
    cos, sin = np.cos(freqs), np.sin(freqs)
    for m in range(U):
        r = slice(P * m, P * m + P)
        for k, (a, x) in enumerate(((8 * cos * scale, 1), (8 * sin * scale, -1), (cos / scale, 1), (sin / scale, -1))):
            at = C_ROPE + D * (4 * m + k)
            c[:, at:at + D] = np.concatenate([x * a[r], a[r]], -1)
    inv1 = f(1) / f(10000.0) ** (np.arange(0, AD, 2, dtype=f) / f(AD))
    fr = np.repeat((np.arange(N, dtype=f)[:, None] * inv1[None]).astype(f), 2, -1)
    sign = np.where(np.arange(AD) % 2 == 0, f(-1), f(1))
    both = np.concatenate([np.cos(fr), np.sin(fr) * sign], -1).reshape(AT, AG, 2 * AD)
    c[:, C_ROPE1:] = np.tile(both.transpose(2, 1, 0).reshape(2 * AD, AG * AT), (4, 1))
    return c


def kernel(**inputs):
    import numpy as np
    import concourse.bacc as bacc
    from concourse.bass_utils import run_bass_kernel_spmd

    x = {k: np.asarray(v) for k, v in inputs.items()}
    f = "L0_ffn_"

    def stacked(w):
        w = w.reshape(AG, AD // 2, 2, E)
        return np.stack([w, w[:, :, ::-1]], 1).reshape(AG * 2 * AD, E).T

    def tiles(b):
        return np.pad(b, ((0, 0), (0, 3 * P - HID))).reshape(DEPTH, 3, P).transpose(0, 2, 1)

    q, k = x[f + "q_scale"], x[f + "k_scale"]
    b1 = x[f + "b1"]
    arrays = {
        "xT": x["L0_attn_emb"].reshape(T, E).T,
        "w1s": stacked(x["L0_attn_W1"]).reshape(E, AG, 2 * AD),
        "w2s": stacked(x["L0_attn_W2"]).reshape(E, AG, 2 * AD),
        "w3T": x["L0_attn_W3"].T,
        "woT": x["L0_attn_Wo"].T.reshape(16, AG, E).transpose(1, 0, 2).reshape(P, E),
        "cT": x["L0_c"].T,
        "wmod": x["L0_wmod"],
        "wqkv": x[f + "Wqkv"],
        "scales": np.stack([q, np.roll(q, D // 2, 1), k, np.roll(k, D // 2, 1)], 1),
        "wo": x[f + "Wo"],
        "params": np.concatenate([x[f + "ln_g"][:, :, None], x[f + "ln_b"][:, :, None], x[f + "b2"][:, :, None],
                                  tiles(b1[:, :HID]), tiles(b1[:, HID:])], 2),
        "w1": x[f + "W1"],
        "w2": x[f + "W2"],
        "consts": constants(),
    }
    arrays = {n: np.ascontiguousarray(a) for n, a in arrays.items()}
    nc = bacc.Bacc("TRN2", target_bir_lowering=False, num_devices=1)
    args = [nc.dram_tensor(n, a.shape, mybir.dt.from_np(a.dtype), kind="ExternalInput").ap()
            for n, a in arrays.items()]
    out = nc.dram_tensor("out", (E, T), F32, kind="ExternalOutput").ap()
    build(nc, *args, out)
    r = run_bass_kernel_spmd(nc, [arrays], core_ids=[0])
    return np.ascontiguousarray(r.results[0]["out"].T.reshape(B, N, E))
```
